# Optimizing a Trainium2 kernel written in Bass

```python
import numpy as np
import jax
import jax.numpy as jnp

def _softmax(x, axis=-1):
    return jax.nn.softmax(x, axis=axis)
def _gelu(x):
    return jax.nn.gelu(x, approximate=True)
def _silu(x):
    return jax.nn.silu(x)
def _sigmoid(x):
    return jax.nn.sigmoid(x)
def _layernorm(x, axis=-1, eps=1e-5):
    m = jnp.mean(x, axis=axis, keepdims=True)
    v = jnp.var(x, axis=axis, keepdims=True)
    return (x - m) / jnp.sqrt(v + eps)
def _scatter_add(tgt, idx, src, axis=0):
    return tgt.at[idx].add(src)
def _segment_sum(src, seg, n):
    return jax.ops.segment_sum(src, seg, n)

kernel_name = 'mk_conv_seq_d2_conv_nchw256_a87b69'

def setup_inputs(seed: int = 0):
    np.random.seed(seed)
    _w = jnp.asarray
    def _rec_inputs():
        import jax
        import jax.numpy as jnp
        _gk = jax.random.key(seed)
        x = -0.0002928 + 1 * jax.random.normal(jax.random.fold_in(_gk, 1), (4, 256, 64, 64), jnp.float32)
        return x
    x = _rec_inputs()
    def _L0_conv_setup():
        import jax, jax.numpy as jnp
        import numpy as np
        CHANNELS = 256
        C8 = CHANNELS // 8
        key = jax.random.key(seed)
        ks = jax.random.split(key, 7)
        b, c, h, w = (4, CHANNELS, 64, 64)
        x = jax.random.normal(ks[0], (b, c, h, w), dtype=jnp.float32)
        s = 1.0 / np.sqrt(c)
        wq = jax.random.uniform(ks[1], (C8, c), jnp.float32, -s, s)
        bq = jax.random.uniform(ks[2], (C8,), jnp.float32, -s, s)
        wk = jax.random.uniform(ks[3], (C8, c), jnp.float32, -s, s)
        bk = jax.random.uniform(ks[4], (C8,), jnp.float32, -s, s)
        wv = jax.random.uniform(ks[5], (c, c), jnp.float32, -s, s)
        bv = jax.random.uniform(ks[6], (c,), jnp.float32, -s, s)
        return {'x': x, 'wq': wq, 'bq': bq, 'wk': wk, 'bk': bk, 'wv': wv, 'bv': bv}
    _L0_conv_all = _L0_conv_setup()
    _L0_conv_in = {k: v for k, v in _L0_conv_all.items() if k in ('wq', 'bq', 'wk', 'bk', 'wv', 'bv', )}
    del _L0_conv_all

    def _L1_conv_setup():
        import jax, jax.numpy as jnp
        import numpy as np
        NH = 8
        BNS = np.float32(1.0 / np.sqrt(1.0 + 1e-05))

        def conv2d(x, w, b=None, stride=1, pad=0):
            y = jax.lax.conv_general_dilated(x, w, (stride, stride), [(pad, pad), (pad, pad)], dimension_numbers=('NCHW', 'OIHW', 'NCHW'))
            return y if b is None else y + b[None, :, None, None]

        def l2n(x, axis=-1):
            return x / jnp.maximum(jnp.linalg.norm(x, axis=axis, keepdims=True), 1e-12)

        def spectral_transform(x, w1, wfu, w2):
            b, c, h, w = x.shape
            x = x.reshape(b, c, h // 2, 2, w // 2, 2).mean(axis=(3, 5))
            x = jax.nn.relu(conv2d(x, w1) * BNS)
            bb, cc, hh, ww = x.shape
            f = jnp.fft.rfft2(x, norm='ortho')
            f = jnp.stack((f.real, f.imag), axis=2).reshape(bb, 2 * cc, hh, ww // 2 + 1)
            f = jax.nn.relu(conv2d(f, wfu) * BNS)
            f = f.reshape(bb, cc, 2, hh, ww // 2 + 1)
            out = jnp.fft.irfft2(jax.lax.complex(f[:, :, 0], f[:, :, 1]), s=(hh, ww), norm='ortho')
            return conv2d(x + out, w2)

        def channel_attn(q, k, v, temperature):
            b, c, h, w = q.shape
            d, t = (c // NH, h * w)
            qT = q.reshape(b, NH, d, t)
            kk = k.reshape(b, NH, d, t).transpose(0, 1, 3, 2)
            vT = v.reshape(b, NH, d, t)
            a = jnp.einsum('bhdt,bhte->bhde', l2n(qT, -1), l2n(kk, -1)) * temperature[None]
            a = jax.nn.softmax(a, axis=-1)
            o = jnp.einsum('bhde,bhet->bhdt', a, vT)
            return o.transpose(0, 3, 1, 2).reshape(b, t, c).transpose(0, 2, 1).reshape(b, c, h, w)

        def upsample2x_align(x):
            b, c, h, w = x.shape
            H2, W2 = (2 * h, 2 * w)
            ys = jnp.arange(H2, dtype=x.dtype) * ((h - 1) / (H2 - 1))
            xs = jnp.arange(W2, dtype=x.dtype) * ((w - 1) / (W2 - 1))
            y0 = jnp.floor(ys).astype(jnp.int32)
            y1 = jnp.minimum(y0 + 1, h - 1)
            x0 = jnp.floor(xs).astype(jnp.int32)
            x1 = jnp.minimum(x0 + 1, w - 1)
            wy = (ys - y0.astype(x.dtype))[None, None, :, None]
            wx = (xs - x0.astype(x.dtype))[None, None, None, :]
            r = x[:, :, y0, :] * (1 - wy) + x[:, :, y1, :] * wy
            return r[:, :, :, x0] * (1 - wx) + r[:, :, :, x1] * wx
        key = jax.random.key(seed)
        ks = jax.random.split(key, 16)
        B, E, H, W = (8, 256, 128, 128)
        C = E // 2

        def w(k, shape, fan_in):
            return jax.random.normal(k, shape, jnp.float32) * np.float32(1.0 / np.sqrt(fan_in))
        return {'x': jax.random.normal(ks[0], (B, E, H, W), jnp.float32), 'wq': w(ks[1], (C, C, 3, 3), C * 9), 'bq': jnp.zeros((C,), jnp.float32), 'wk': w(ks[2], (C, C, 3, 3), C * 9), 'bk': jnp.zeros((C,), jnp.float32), 'wv': w(ks[3], (C, C, 3, 3), C * 9), 'bv': jnp.zeros((C,), jnp.float32), 'wk2': w(ks[4], (C, C, 3, 3), C * 9), 'bk2': jnp.zeros((C,), jnp.float32), 'wv2': w(ks[5], (C, C, 3, 3), C * 9), 'bv2': jnp.zeros((C,), jnp.float32), 'w_st1': w(ks[6], (C // 2, C, 1, 1), C), 'w_stfu': w(ks[7], (C, C, 1, 1), C), 'w_st2': w(ks[8], (C, C // 2, 1, 1), C // 2), 'temperature': jnp.ones((NH, 1, 1), jnp.float32), 'w_out': w(ks[9], (E, E, 1, 1), E), 'b_out': jnp.zeros((E,), jnp.float32)}
    _L1_conv_all = _L1_conv_setup()
    _L1_conv_in = {k: v for k, v in _L1_conv_all.items() if k in ('wq', 'bq', 'wk', 'bk', 'wv', 'bv', 'wk2', 'bk2', 'wv2', 'bv2', 'w_st1', 'w_stfu', 'w_st2', 'temperature', 'w_out', 'b_out', )}
    del _L1_conv_all

    return {
        "x": x,
        "L0_conv_wq": _L0_conv_in["wq"],
        "L0_conv_bq": _L0_conv_in["bq"],
        "L0_conv_wk": _L0_conv_in["wk"],
        "L0_conv_bk": _L0_conv_in["bk"],
        "L0_conv_wv": _L0_conv_in["wv"],
        "L0_conv_bv": _L0_conv_in["bv"],
        "L1_conv_wq": _L1_conv_in["wq"],
        "L1_conv_bq": _L1_conv_in["bq"],
        "L1_conv_wk": _L1_conv_in["wk"],
        "L1_conv_bk": _L1_conv_in["bk"],
        "L1_conv_wv": _L1_conv_in["wv"],
        "L1_conv_bv": _L1_conv_in["bv"],
        "L1_conv_wk2": _L1_conv_in["wk2"],
        "L1_conv_bk2": _L1_conv_in["bk2"],
        "L1_conv_wv2": _L1_conv_in["wv2"],
        "L1_conv_bv2": _L1_conv_in["bv2"],
        "L1_conv_w_st1": _L1_conv_in["w_st1"],
        "L1_conv_w_stfu": _L1_conv_in["w_stfu"],
        "L1_conv_w_st2": _L1_conv_in["w_st2"],
        "L1_conv_temperature": _L1_conv_in["temperature"],
        "L1_conv_w_out": _L1_conv_in["w_out"],
        "L1_conv_b_out": _L1_conv_in["b_out"],
    }

def reference(x, L0_conv_wq, L0_conv_bq, L0_conv_wk, L0_conv_bk, L0_conv_wv, L0_conv_bv, L1_conv_wq, L1_conv_bq, L1_conv_wk, L1_conv_bk, L1_conv_wv, L1_conv_bv, L1_conv_wk2, L1_conv_bk2, L1_conv_wv2, L1_conv_bv2, L1_conv_w_st1, L1_conv_w_stfu, L1_conv_w_st2, L1_conv_temperature, L1_conv_w_out, L1_conv_b_out):
    import jax
    import jax.numpy as jnp
    def _L0_conv_ref(x, wq, bq, wk, bk, wv, bv):
        import jax, jax.numpy as jnp
        import numpy as np
        CHANNELS = 256
        C8 = CHANNELS // 8
        b, c, h, w = x.shape
        n = h * w
        xf = x.reshape(b, c, n)
        q = jnp.einsum('oc,bcn->bon', wq, xf) + bq[None, :, None]
        k = jnp.einsum('oc,bcn->bon', wk, xf) + bk[None, :, None]
        v = jnp.einsum('oc,bcn->bon', wv, xf) + bv[None, :, None]
        scores = jnp.einsum('bdi,bdj->bij', q, k)
        attn = jax.nn.softmax(scores, axis=-1)
        out = jnp.einsum('bcj,bij->bci', v, attn)
        return out.reshape(b, c, h, w) + x

    def _L1_conv_ref(x, wq, bq, wk, bk, wv, bv, wk2, bk2, wv2, bv2, w_st1, w_stfu, w_st2, temperature, w_out, b_out):
        import jax, jax.numpy as jnp
        import numpy as np
        NH = 8
        BNS = np.float32(1.0 / np.sqrt(1.0 + 1e-05))

        def conv2d(x, w, b=None, stride=1, pad=0):
            y = jax.lax.conv_general_dilated(x, w, (stride, stride), [(pad, pad), (pad, pad)], dimension_numbers=('NCHW', 'OIHW', 'NCHW'))
            return y if b is None else y + b[None, :, None, None]

        def l2n(x, axis=-1):
            return x / jnp.maximum(jnp.linalg.norm(x, axis=axis, keepdims=True), 1e-12)

        def spectral_transform(x, w1, wfu, w2):
            b, c, h, w = x.shape
            x = x.reshape(b, c, h // 2, 2, w // 2, 2).mean(axis=(3, 5))
            x = jax.nn.relu(conv2d(x, w1) * BNS)
            bb, cc, hh, ww = x.shape
            f = jnp.fft.rfft2(x, norm='ortho')
            f = jnp.stack((f.real, f.imag), axis=2).reshape(bb, 2 * cc, hh, ww // 2 + 1)
            f = jax.nn.relu(conv2d(f, wfu) * BNS)
            f = f.reshape(bb, cc, 2, hh, ww // 2 + 1)
            out = jnp.fft.irfft2(jax.lax.complex(f[:, :, 0], f[:, :, 1]), s=(hh, ww), norm='ortho')
            return conv2d(x + out, w2)

        def channel_attn(q, k, v, temperature):
            b, c, h, w = q.shape
            d, t = (c // NH, h * w)
            qT = q.reshape(b, NH, d, t)
            kk = k.reshape(b, NH, d, t).transpose(0, 1, 3, 2)
            vT = v.reshape(b, NH, d, t)
            a = jnp.einsum('bhdt,bhte->bhde', l2n(qT, -1), l2n(kk, -1)) * temperature[None]
            a = jax.nn.softmax(a, axis=-1)
            o = jnp.einsum('bhde,bhet->bhdt', a, vT)
            return o.transpose(0, 3, 1, 2).reshape(b, t, c).transpose(0, 2, 1).reshape(b, c, h, w)

        def upsample2x_align(x):
            b, c, h, w = x.shape
            H2, W2 = (2 * h, 2 * w)
            ys = jnp.arange(H2, dtype=x.dtype) * ((h - 1) / (H2 - 1))
            xs = jnp.arange(W2, dtype=x.dtype) * ((w - 1) / (W2 - 1))
            y0 = jnp.floor(ys).astype(jnp.int32)
            y1 = jnp.minimum(y0 + 1, h - 1)
            x0 = jnp.floor(xs).astype(jnp.int32)
            x1 = jnp.minimum(x0 + 1, w - 1)
            wy = (ys - y0.astype(x.dtype))[None, None, :, None]
            wx = (xs - x0.astype(x.dtype))[None, None, None, :]
            r = x[:, :, y0, :] * (1 - wy) + x[:, :, y1, :] * wy
            return r[:, :, :, x0] * (1 - wx) + r[:, :, :, x1] * wx
        B, E, H, W = x.shape
        x1, x2 = (x[:, :E // 2], x[:, E // 2:])
        q_l = conv2d(x1, wq, bq, pad=1) * BNS
        k_l = conv2d(x1, wk, bk, pad=1) * BNS
        v_l = conv2d(x1, wv, bv, pad=1) * BNS
        q_h = spectral_transform(x2, w_st1, w_stfu, w_st2) * BNS
        k_h = conv2d(x2, wk2, bk2, stride=2, pad=1) * BNS
        v_h = conv2d(x2, wv2, bv2, stride=2, pad=1) * BNS
        attn_h = channel_attn(q_h, k_h, v_h, temperature)
        attn_l = channel_attn(q_l, k_l, v_l, temperature)
        attn_h = upsample2x_align(attn_h)
        attn = jnp.concatenate([attn_h, attn_l], axis=1)
        return conv2d(attn, w_out, b_out)

    def _gn(v, G=32, eps=1e-5):
        B_, C_, H_, W_ = v.shape
        g = v.reshape(B_, G, C_ // G, H_, W_)
        m = jnp.mean(g, axis=(2, 3, 4), keepdims=True)
        s = jnp.var(g, axis=(2, 3, 4), keepdims=True)
        return ((g - m) / jnp.sqrt(s + eps)).reshape(v.shape)

    def _ln_c(v, eps=1e-6):
        m = jnp.mean(v, axis=1, keepdims=True)
        s = jnp.var(v, axis=1, keepdims=True)
        return (v - m) / jnp.sqrt(s + eps)

    def _ln_t(v, eps=1e-5):
        m = jnp.mean(v, axis=-1, keepdims=True)
        s = jnp.var(v, axis=-1, keepdims=True)
        return (v - m) / jnp.sqrt(s + eps)

    def _to_tokens(v):
        B_, C_, H_, W_ = v.shape
        return v.reshape(B_, C_, H_ * W_).transpose(0, 2, 1)
    def _from_tokens(t, like):
        B_, C_, H_, W_ = like.shape
        return t.transpose(0, 2, 1).reshape(B_, C_, H_, W_)

    x = _L0_conv_ref(x, L0_conv_wq, L0_conv_bq, L0_conv_wk, L0_conv_bk, L0_conv_wv, L0_conv_bv)
    x = _L1_conv_ref(x, L1_conv_wq, L1_conv_bq, L1_conv_wk, L1_conv_bk, L1_conv_wv, L1_conv_bv, L1_conv_wk2, L1_conv_bk2, L1_conv_wv2, L1_conv_bv2, L1_conv_w_st1, L1_conv_w_stfu, L1_conv_w_st2, L1_conv_temperature, L1_conv_w_out, L1_conv_b_out)
    return x


_drawn_inputs = setup_inputs


def setup_inputs(seed=0):
    import zlib

    import numpy as np

    out = dict(_drawn_inputs(seed))
    spreads = {'L1_conv_bq': (0.0, 0.1),
     'L1_conv_bk': (0.0, 0.1),
     'L1_conv_bv': (0.0, 0.1),
     'L1_conv_bk2': (0.0, 0.1),
     'L1_conv_bv2': (0.0, 0.1),
     'L1_conv_temperature': (1.0, 0.2),
     'L1_conv_b_out': (0.0, 0.1)}
    factors = {'L0_conv_bq': 3.87, 'L0_conv_bk': 8.0}
    for name, (base, spread) in spreads.items():
        noise = np.random.default_rng([zlib.crc32(name.encode()), seed]).standard_normal(out[name].shape)
        drawn = base * np.exp(spread * noise) if base else spread * noise
        out[name] = jnp.asarray(drawn.astype(out[name].dtype))
    for name, factor in factors.items():
        out[name] = (out[name] * factor).astype(out[name].dtype)
    return out
```

```python
from contextlib import ExitStack

import concourse.bass as bass
import numpy as np
from concourse import mybir

ALU = mybir.AluOpType
ACT = mybir.ActivationFunctionType
F32 = mybir.dt.float32
F32R = mybir.dt.float32r
AX = mybir.AxisListType

P = 128
B, C, H, W = 4, 256, 64, 64
N = H * W
CT = C // P
CHUNK = 512
NCH = N // CHUNK
NT = N // P
QT = CHUNK // P
VC = C + 2
HP, WP = H + 2, W + 2
HH, WH = H // 2, W // 2
NHALF = HH * WH
HCH = NHALF // CHUNK
KX = WH // 2 + 1
BNS = float(np.float32(1.0 / np.sqrt(1.0 + 1e-05)))
NORM_FLOOR = 1e-12

W_Q, W_K, W_V = 0, CT * P, 2 * CT * P
W_L = W_V + CT * C
W_ST1 = W_L + 3 * 9 * P
W_FU = W_ST1 + P
W_ST2 = W_FU + 2 * P
NW = W_ST2 + P
D_X = 2 * 9 * P
D_Y0, D_Y, D_Y16 = D_X + P, D_X + 2 * P, D_X + 3 * P
D_RE = D_Y16 + 64
D_IM = D_RE + 2 * P
D_OUT = D_IM + 2 * P
ND = D_OUT + P
K_WO, K_ID, K_NEG, K_UP = 0, 2 * C, 2 * C + P, 2 * C + 2 * P
K_BIAS = K_UP + 4 * WH
BQ, BK, BV, BL, BH, BO, TEMP = 0, 1, 2, 4, 7, 9, 11
NK = K_BIAS + 12

M_PER_GROUP = NT + 2 + 2
M_PER_IMAGE = (NT + 2) + (NCH - 1) * M_PER_GROUP + 2
MAX_TILES = 24
MAX_AT = [t * NT // MAX_TILES - (t - 1) * NT // MAX_TILES if 0 < t <= MAX_TILES else 0 for t in range(NT)]


def build(nc, x, weights, weights2, consts, out):
    ctx = ExitStack()
    with ctx:
        def sb(name, cols, dt=F32):
            return ctx.enter_context(nc.sbuf_tensor(name, [P, cols], dt))

        def sem(name):
            return ctx.enter_context(nc.semaphore(name))

        image = sb("image", CT * N)
        qk = sb("qk", 2 * N, F32R)
        vhi = sb("vhi", NT * VC, F32R)
        vlo = sb("vlo", NT * C, F32R)
        ring = sb("ring", 4 * 2 * CHUNK, F32R)
        whi = sb("whi", NW, F32R)
        wlo = sb("wlo", NW, F32R)
        cst = sb("cst", NK)
        scr = sb("scr", 4 * CHUNK)
        stage = sb("stage", 4 * CHUNK)
        qmax = sb("qmax", CHUNK, F32R)
        maxcol = sb("maxcol", P + 32 * (QT - 1))
        mx = sb("mx", QT * NCH)
        rden = sb("rden", QT)
        bscaled = sb("bscaled", 5)
        gram = sb("gram", P)
        norms = sb("norms", 2 * NCH)
        knorm = sb("knorm", 2 * QT * 8)
        attn = sb("attn", P)
        stat = sb("stat", 8)
        ps = ctx.enter_context(nc.psum_tensor("ps", [P, 8, CHUNK], F32))

        img = image[:, :].rearrange("p (c n) -> p c n", c=CT)
        q_st, k_st = qk[:, 0:N], qk[:, N:2 * N]
        vhi_t = vhi[:, :].rearrange("p (t c) -> p t c", c=VC)
        vlo_t = vlo[:, :].rearrange("p (t c) -> p t c", c=C)
        prob = ring[:, :].rearrange("p (s a n) -> p s a n", s=4, a=2)
        xs = ring[:, :].rearrange("p (s a c n) -> p s a c n", s=2, a=2, c=CT)
        onorm = scr[:, 0:QT * C].rearrange("p (t c) -> p t c", c=C)
        mx_t = mx[:, :].rearrange("p (t c) -> p t c", c=NCH)
        ident = cst[:, K_ID:K_ID + P]
        bias = lambda i: cst[:, K_BIAS + i:K_BIAS + i + 1]
        pad_hi = vhi[:, 0:HP * WP].rearrange("p (h w) -> p h w", w=WP)
        pad_lo = vlo[:, 0:HP * WP].rearrange("p (h w) -> p h w", w=WP)
        D0 = 4400
        D1 = D0 + ND
        dhi, dlo = vhi[:, D0:D0 + ND], vlo[:, D0:D0 + ND]
        fold = {0: (vhi[:, D1:D1 + C], vlo[:, D1:D1 + C]), 1: (vhi[:, D0:D0 + C], vlo[:, D0:D0 + C])}
        up_hi, up_lo = vhi[:, 0:N], vlo[:, 0:N]
        vl_hi, vl_lo = qk[:, 0:N], qk[:, N:2 * N]
        t_hi = {a: ring[:, 2048 + 1024 * a:2560 + 1024 * a] for a in (0, 1)}
        t_lo = {a: ring[:, 2560 + 1024 * a:3072 + 1024 * a] for a in (0, 1)}

        w_in, c_in, w_hi, w_lo, prep = (sem(n) for n in ("w_in", "c_in", "w_hi", "w_lo", "prep"))
        x_in = [sem(f"x_in{i}") for i in range(2)]
        xs_hi, xs_lo = sem("xs_hi"), sem("xs_lo")
        qk_ps, qk_hi, qk_lo, v_ps, v_hi, v_lo = (sem(n) for n in ("qk_ps", "qk_hi", "qk_lo", "v_ps", "v_hi", "v_lo"))
        ones_set, qmax_in, m_ready, m_free, negmax = (sem(n) for n in ("ones_set", "qmax_in", "m_ready", "m_free", "negmax"))
        s_ready, p_used, p_full, p_lo = (sem(n) for n in ("s_ready", "p_used", "p_full", "p_lo"))
        o_done, rden_in, o_norm = (sem(n) for n in ("o_done", "rden_in", "o_norm"))
        border, pad_h, pad_l, d_in, d_hi, d_lo = (sem(n) for n in ("border", "pad_h", "pad_l", "d_in", "d_hi", "d_lo"))
        pool_f, pool_hi, pool_lo = (sem(n) for n in ("pool_f", "pool_hi", "pool_lo"))
        cv_ps, cv_out, sq_done, vl_h, vl_l = (sem(n) for n in ("cv_ps", "cv_out", "sq_done", "vl_h", "vl_l"))
        t_ps, t_h, t_l, g_ps, g_sum = (sem(n) for n in ("t_ps", "t_h", "t_l", "g_ps", "g_sum"))
        sp_ps, sp_f, sp_hi, sp_lo, sp_z = (sem(n) for n in ("sp_ps", "sp_f", "sp_hi", "sp_lo", "sp_z"))
        up_d, up_h, up_l = sem("up_d"), sem("up_h"), sem("up_l")
        a_dve, a_act = sem("a_dve"), sem("a_act")
        k_sq, k_sum, k_root, k_inv, k_unit = (sem(n) for n in ("k_sq", "k_sum", "k_root", "k_inv", "k_unit"))
        f_ps, f_hi, f_lo = sem("f_ps"), sem("f_hi"), sem("f_lo")
        r_ps, r_out = sem("r_ps"), sem("r_out")
        out_dma = [sem(f"out_dma{i}") for i in range(4)]

        f = lambda ap: ap.bitcast(F32)

        passed = sem("passed")

        def apart(eng):
            eng.sem_inc(passed, 1)

        block = ctx.enter_context(nc.Block())

        def freq(dst):
            d, s = [], []
            for bank, k0, n in ((0, 0, 8), (1, 8, 8), (2, 16, 1)):
                v = ps[:, bank, 0:n * 64].rearrange("p (k r y) -> p k r y", r=2, y=HH)
                for r in range(2):
                    d.append(dst[64 * r:64 * (r + 1), k0 * 32:(k0 + n) * 32].rearrange("p (k y) -> p k y", y=HH))
                    s.append(v[64 * r:64 * (r + 1), :, r, :])
            return d, s

        def ky_tiles(dst):
            return ([dst[:, 0:512], dst[:, 512:1024], dst[0:32, 1024:1280]],
                    [ps[:, 2, :], ps[:, 3, :], ps[0:32, 4, 0:256]])

        @block.sync
        def _(sp):
            sp.dma_start(cst[:, :], consts).then_inc(c_in, 16)
            sp.dma_start(image[:, 0:NW], weights).then_inc(w_in, 16)
            for s in range(2):
                sp.sem_inc(x_in[s], 16)
            for s in range(4):
                sp.sem_inc(out_dma[s], 16)
            sp.wait_ge(w_lo, 1)
            apart(sp)
            def load(b, c2):
                for s in range(2):
                    sp.wait_ge(x_in[s], b * (16 * NCH // 2) + c2 * 16 + 16)
                    sp.dma_start(
                        img[:, :, bass.ds(c2 * (2 * CHUNK) + s * CHUNK, CHUNK)],
                        x[bass.ds(b * CT, CT), :, bass.ds(c2 * (2 * CHUNK) + s * CHUNK, CHUNK)]
                        .rearrange("c p n -> p c n")).then_inc(x_in[s], 16)

            def load_weights2(b):
                sp.wait_ge(pad_l, b * 16 + 8)
                sp.dma_start(image[:, 0:ND], weights2).then_inc(d_in, 16)

            def store(b, c2):
                for s in range(4):
                    sp.wait_ge(r_out, b * 16 + c2 * 4 + (4 + s + 1))
                    sp.dma_start(
                        out[bass.ds(b * CT + s % 2, 1), :, bass.ds(c2 * (2 * CHUNK) + (s // 2) * CHUNK, CHUNK)]
                        .rearrange("c p n -> p (c n)"),
                        stage[:, s * CHUNK:(s + 1) * CHUNK]).then_inc(out_dma[s], 16)

            with sp.Fori(0, NCH // 2) as c2:
                load(0, c2)
            with sp.Fori(0, B - 1) as b:
                load_weights2(b)
                sp.wait_ge(up_l, b + 2)
                apart(sp)
                with sp.Fori(0, NCH // 2) as c2:
                    load(b + 1, c2)
                    store(b, c2)
            load_weights2(B - 1)
            with sp.Fori(0, NCH // 2) as c2:
                store(B - 1, c2)
            for s in range(4):
                sp.wait_ge(out_dma[s], 16 + 16 * B * NCH // 2)

        @block.tensor
        def _(pe):
            def three(o, w_hi_ap, w_lo_ap, x_hi_ap, x_lo_ap, start, stop):
                pe.matmul(o, w_hi_ap, x_hi_ap, start=start, stop=False)
                pe.matmul(o, w_hi_ap, x_lo_ap, start=False, stop=False)
                return pe.matmul(o, w_lo_ap, x_hi_ap, start=False, stop=stop)

            def transposes(o, src, n):
                for i in range(n):
                    last = pe.transpose(o[:, i * P:(i + 1) * P], src[:, i * P:(i + 1) * P], ident)
                return last

            def scores(group, t, n0):
                pe.wait_ge(p_lo, n0 + t + 1)
                pe.matmul(ps[:, 4 + t % 2, :], k_st[:, t * P:(t + 1) * P],
                          q_st[:, bass.ds(group * CHUNK, CHUNK)], start=True, stop=True).then_inc(s_ready, 1)

            def maxima(i, m):
                qt, jc = i // NCH, i % NCH
                pe.wait_ge(m_free, m + 1)
                pe.matmul(ps[:, 6 + i % 2, :], qmax[0:96, qt * P:(qt + 1) * P],
                          k_st[0:96, jc * CHUNK:(jc + 1) * CHUNK], start=True, stop=True).then_inc(m_ready, 1)

            def first_maxima(b, c2, s, qt):
                pe.wait_ge(m_free, b * M_PER_IMAGE + c2 * (2 * QT) + (s * QT - QT + qt + 1))
                pe.matmul(ps[:, 6 + qt % 2, :], qmax[0:96, qt * P:(qt + 1) * P],
                          k_st[0:96, bass.ds(c2 * (2 * CHUNK) + (s - 1) * CHUNK, CHUNK)],
                          start=True, stop=True).then_inc(m_ready, 1)

            def project(b, c2, s, first):
                n = b * NCH + c2 * 2 + s
                pe.wait_ge(xs_lo, n + 1)
                for a, w0 in ((0, W_Q), (1, W_K)):
                    for c in range(CT):
                        w = slice(w0 + c * P, w0 + (c + 1) * P)
                        last = three(ps[:, 4 * s + a, :], whi[:, w], wlo[:, w], xs[:, s, 0, c, :], xs[:, s, 1, c, :],
                                     c == 0, c == CT - 1)
                    last.then_inc(qk_ps, 1)
                if not first:
                    pe.wait_ge(qk_lo, n * 2)
                    pe.wait_ge(qmax_in, b * NCH + 1)
                for j in range(QT):
                    if not first:
                        first_maxima(b, c2, s, j)
                    if j % 2 == 0:
                        pe.wait_ge(v_lo, n * 2 + (j // 2 + 1))
                    for c in range(CT):
                        w = slice(W_V + c * C, W_V + (c + 1) * C)
                        last = three(ps[:, 2 + j // 2, (j % 2) * C:(j % 2 + 1) * C],
                                     xs[:, s, 0, c, j * P:(j + 1) * P], xs[:, s, 1, c, j * P:(j + 1) * P],
                                     whi[:, w], wlo[:, w], c == 0, c == CT - 1)
                    if j % 2:
                        last.then_inc(v_ps, 1)

            def maxima_rows(n, m):
                pe.wait_ge(negmax, n + 1)
                for h in range(2):
                    pe.wait_ge(m_free, m + h + 1)
                    for i in range(2):
                        last = pe.transpose(ps[:, 6 + h, i * P:(i + 1) * P], maxcol[:, 32 * (2 * h + i):32 * (2 * h + i) + P], ident)
                    last.then_inc(m_ready, 1)

            def weigh(t, n):
                pe.wait_ge(p_lo, n * NT + t + 3)
                for qt in range(QT):
                    if t == 0:
                        pe.wait_ge(o_norm, n * QT + qt + 1)
                    hi = prob[:, t % 4, 0, qt * P:(qt + 1) * P]
                    lo = prob[:, t % 4, 1, qt * P:(qt + 1) * P]
                    pe.matmul(ps[:, qt, 0:VC], hi, vhi_t[:, t, :], start=(t == 0), stop=False)
                    pe.matmul(ps[:, qt, 0:C], hi, vlo_t[:, t, :], start=False, stop=False)
                    last = pe.matmul(ps[:, qt, 0:VC], lo, vhi_t[:, t, :], start=False, stop=(t == NT - 1))
                    if t == NT - 1:
                        last.then_inc(o_done, 1)
                    elif qt == QT - 1:
                        last.then_inc(p_used, 1)

            def attend(b, g, last_group):
                n = b * NCH + g
                n0 = n * NT
                m0 = b * M_PER_IMAGE + (NT + 2) + g * M_PER_GROUP
                i = 0
                for t in range(1, NT):
                    if not last_group:
                        for _ in range(MAX_AT[t]):
                            if i == 0:
                                pe.wait_ge(qmax_in, n + 2)
                            maxima(i, m0 + i)
                            i += 1
                        if t == MAX_TILES + 3:
                            maxima_rows(n + 1, m0 + NT)
                    if t + 2 < NT:
                        scores(g, t + 2, n0)
                    elif not last_group:
                        if t + 2 == NT:
                            pe.wait_ge(m_free, m0 + NT + 2 + 2)
                        scores(g + 1, t + 2 - NT, n0 + NT)
                    weigh(t, n)
                if not last_group:
                    scores(g + 1, 2, n0 + NT)
                    weigh(0, n + 1)
                m1 = m0 + (0 if last_group else NT + 2)
                for c in range(CT):
                    pe.wait_ge(m_free, m1 + c + 1)
                for qt in range(QT):
                    pe.wait_ge(o_norm, (n + 1) * QT + qt + 1)
                    for c in range(CT):
                        last = pe.transpose(ps[:, 6 + c, qt * P:(qt + 1) * P], onorm[:, qt, c * P:(c + 1) * P], ident)
                        if qt == QT - 1:
                            last.then_inc(m_ready, 1)

            def conv(o, hi, lo, w0, src, taps=range(9), half=False, rows=None, c=None):
                for tap in taps:
                    dy, dx = tap // 3, tap % 3
                    w_h, w_l = hi[:, w0 + tap * P:w0 + (tap + 1) * P], lo[:, w0 + tap * P:w0 + (tap + 1) * P]
                    if half:
                        r0 = 2 * (CHUNK // WH) * c + dy
                        x_h, x_l = (z[:, r0:r0 + 2 * (CHUNK // WH) - 1:2, dx:dx + 2 * WH - 1:2] for z in src)
                    else:
                        x_h, x_l = (z[:, bass.ds(c * (CHUNK // W) + dy, CHUNK // W), dx:dx + W] for z in src)
                    last = three(o, w_h, w_l, x_h, x_l, tap == 0, tap == 8)
                return last

            def gram_chunk(n):
                pe.wait_ge(t_l, n * 2 + 2)
                pe.wait_ge(g_sum, n + 1)
                for i in range(QT):
                    s = slice(i * P, (i + 1) * P)
                    last = three(ps[:, 5, 0:P], t_hi[0][:, s], t_lo[0][:, s], t_hi[1][:, s], t_lo[1][:, s],
                                 i == 0, i == QT - 1)
                last.then_inc(g_ps, 1)

            def fold_weights(b, s):
                pe.wait_ge(a_dve, (2 * b + s) * 8 + 8)
                pe.matmul(ps[:, 5, 2 * P:2 * P + C], attn[:, :], cst[:, K_WO + (1 - s) * C:K_WO + (2 - s) * C],
                          start=True, stop=True).then_inc(f_ps, 1)

            for _ in range(4):
                pe.sem_inc(v_ps, 1)
                pe.sem_inc(p_used, 1)
            pe.wait_ge(w_lo, 1)
            pe.wait_ge(c_in, 16)
            pe.wait_ge(prep, 2)
            apart(pe)
            with pe.Fori(0, B) as b:
                pe.wait_ge(r_out, b * 16 + 4)
                apart(pe)
                for s in range(2):
                    project(b, 0, s, s == 0)
                with pe.Fori(1, NCH // 2) as c2:
                    for s in range(2):
                        project(b, c2, s, False)
                pe.wait_ge(qk_lo, b * (2 * NCH) + 2 * NCH)
                for qt in range(QT):
                    first_maxima(b, NCH // 2, 0, qt)
                pe.wait_ge(v_lo, b * (2 * NCH) + 2 * NCH + 2)
                maxima_rows(b * NCH, b * M_PER_IMAGE + NT)
                pe.wait_ge(ones_set, b * 2 + 2)
                pe.wait_ge(m_free, b * M_PER_IMAGE + NT + 2 + 2)
                for t in range(3):
                    scores(0, t, b * (NCH * NT))
                weigh(0, b * NCH)
                with pe.Fori(0, NCH - 1) as g:
                    attend(b, g, False)
                attend(b, NCH - 1, True)
                pe.wait_ge(border, b * 6 + 6)
                apart(pe)
                with pe.Fori(0, NCH) as c:
                    n = b * 10 + c
                    pe.wait_ge(pad_l, b * 16 + c + 1)
                    conv(ps[:, 1, :], whi, wlo, W_L + 9 * P, (pad_hi, pad_lo), c=c).then_inc(cv_ps, 1)
                    pe.wait_ge(sq_done, n + 1)
                    conv(ps[:, 0, :], whi, wlo, W_L, (pad_hi, pad_lo), taps=range(3), c=c)
                    pe.wait_ge(cv_out, b * 30 + c * 3 + 1)
                    transposes(ps[:, 4, :], scr[:, CHUNK:2 * CHUNK], QT).then_inc(t_ps, 1)
                    conv(ps[:, 0, :], whi, wlo, W_L, (pad_hi, pad_lo), taps=range(3, 9), c=c).then_inc(cv_ps, 1)
                    conv(ps[:, 2, :], whi, wlo, W_L + 18 * P, (pad_hi, pad_lo), taps=range(3), c=c)
                    pe.wait_ge(cv_out, b * 30 + c * 3 + 2)
                    transposes(ps[:, 3, :], scr[:, 0:CHUNK], QT).then_inc(t_ps, 1)
                    conv(ps[:, 2, :], whi, wlo, W_L + 18 * P, (pad_hi, pad_lo), taps=range(3, 9), c=c).then_inc(cv_ps, 1)
                    gram_chunk(n)
                sp0, lo0 = b * 10, b * 6
                nine = lambda k: slice(k, k + P)
                pe.wait_ge(pool_lo, b + 1)
                pe.wait_ge(sq_done, b * 10 + 9)
                for h in range(2):
                    w = nine(W_ST1)
                    last = three(ps[:, h, :], whi[:, w], wlo[:, w], ring[:, h * CHUNK:(h + 1) * CHUNK],
                                 ring[:, 1024 + h * CHUNK:1024 + (h + 1) * CHUNK], True, True)
                last.then_inc(sp_ps, 1)
                pe.wait_ge(d_lo, b + 1)
                src = (pad_hi, pad_lo)
                pe.wait_ge(pad_l, b * 16 + 12)
                conv(ps[:, 6, :], dhi, dlo, 9 * P, src, half=True, c=0).then_inc(cv_ps, 1)
                pe.wait_ge(cv_out, b * 30 + 24)
                pe.wait_ge(sp_f, b * 4 + 1)
                transposes(ps[:, 2, :], scr[:, 1024:1536], 4)
                transposes(ps[:, 3, :], scr[:, 1536:2048], 4).then_inc(sp_ps, 1)
                pe.wait_ge(pad_l, b * 16 + 16)
                conv(ps[:, 7, :], dhi, dlo, 9 * P, src, half=True, c=1).then_inc(cv_ps, 1)
                pe.wait_ge(sp_lo, lo0 + 1)
                for y in range(8):
                    last = three(ps[:, y // 4, (y % 4) * P:(y % 4 + 1) * P], ring[:, y * P:(y + 1) * P],
                                 ring[:, 1280 + y * P:1280 + (y + 1) * P], dhi[:, nine(D_X)], dlo[:, nine(D_X)], True, True)
                last.then_inc(sp_ps, 1)
                pe.wait_ge(cv_out, b * 30 + 25)
                conv(ps[:, 6, :], dhi, dlo, 0, src, half=True, c=0).then_inc(cv_ps, 1)
                pe.wait_ge(sp_f, b * 4 + 2)
                transposes(ps[:, 2, :], stage[:, 0:512], 4)
                transposes(ps[:, 3, :], stage[:, 512:1024], 4).then_inc(sp_ps, 1)
                pe.wait_ge(cv_out, b * 30 + 26)
                conv(ps[:, 7, :], dhi, dlo, 0, src, half=True, c=1).then_inc(cv_ps, 1)
                pe.wait_ge(sp_lo, lo0 + 2)
                for k in range(8):
                    d = nine(D_Y0 if k == 0 else D_Y)
                    three(ps[:, k // 4, (k % 4) * P:(k % 4 + 1) * P], ring[:, k * P:(k + 1) * P],
                          ring[:, 1280 + k * P:1280 + (k + 1) * P], dhi[:, d], dlo[:, d], True, True)
                d = slice(D_Y16, D_Y16 + 64)
                three(ps[:, 2, 0:64], ring[:, 0:P], ring[:, 1280:1280 + P], dhi[:, d], dlo[:, d], True, True).then_inc(sp_ps, 1)
                fold_weights(b, 0)
                pe.wait_ge(sp_lo, lo0 + 3)
                for part in range(2):
                    for h in range(2):
                        w, r = nine(W_FU + part * P), slice(h * 272, (h + 1) * 272)
                        last = three(ps[:, 3 * part + h, 0:272], whi[:, w], wlo[:, w], ring[:, 2304:2848][:, r],
                                     ring[:, 2848:3392][:, r], True, True)
                last.then_inc(sp_ps, 1)
                pe.wait_ge(sp_f, b * 4 + 3)
                for part in range(2):
                    transposes(ps[:, 2 + part, :], stage[:, part * 640:part * 640 + 512], 4)
                for part in range(2):
                    last = pe.transpose(ps[0:32, 4, part * P:(part + 1) * P], stage[:, part * 640 + 512:part * 640 + 544], ident)
                last.then_inc(sp_ps, 1)
                pe.wait_ge(sp_lo, lo0 + 4)
                for q in range(4):
                    o = ps[:, q // 2, (q % 2) * 256:(q % 2 + 1) * 256]
                    re, im = q * P, (4 + q) * P
                    three(o, ring[:, re:re + P], ring[:, 1280 + re:1280 + re + P],
                          dhi[:, D_RE:D_RE + 256], dlo[:, D_RE:D_RE + 256], True, False)
                    three(o, ring[:, im:im + P], ring[:, 1280 + im:1280 + im + P],
                          dhi[:, D_IM:D_IM + 256], dlo[:, D_IM:D_IM + 256], False, True)
                o = ps[:, 3, 0:64]
                three(o, ring[0:32, 1024:1152], ring[0:32, 2304:2432], dhi[0:32, D_RE:D_RE + 64], dlo[0:32, D_RE:D_RE + 64], True, False)
                three(o, ring[0:32, 1152:1280], ring[0:32, 2432:2560], dhi[0:32, D_IM:D_IM + 64], dlo[0:32, D_IM:D_IM + 64],
                      False, True).then_inc(sp_ps, 1)
                pe.wait_ge(sp_f, b * 4 + 4)
                transposes(ps[:, 2, :], stage[:, 0:512], 4)
                transposes(ps[:, 4, :], stage[:, 512:1024], 4).then_inc(sp_ps, 1)
                pe.wait_ge(sp_lo, lo0 + 5)
                for y in range(8):
                    last = three(ps[:, y // 4, (y % 4) * P:(y % 4 + 1) * P], ring[:, y * P:(y + 1) * P],
                                 ring[:, 1280 + y * P:1280 + (y + 1) * P], dhi[:, nine(D_OUT)], dlo[:, nine(D_OUT)], True, True)
                last.then_inc(sp_ps, 1)
                pe.wait_ge(sp_lo, lo0 + 6)
                for h in range(HCH):
                    w = nine(W_ST2)
                    three(ps[:, h, :], whi[:, w], wlo[:, w], ring[:, h * CHUNK:(h + 1) * CHUNK],
                          ring[:, 1024 + h * CHUNK:1024 + (h + 1) * CHUNK], True, True).then_inc(cv_ps, 1)
                for h in range(HCH):
                    pe.wait_ge(cv_out, b * 30 + 28)
                    transposes(ps[:, 4, :], scr[:, h * CHUNK:(h + 1) * CHUNK], QT).then_inc(t_ps, 1)
                    pe.wait_ge(cv_out, b * 30 + 29 + h)
                    transposes(ps[:, 3, :], stage[:, h * CHUNK:(h + 1) * CHUNK], QT).then_inc(t_ps, 1)
                    gram_chunk(b * 10 + 8 + h)
                fold_weights(b, 1)
                pe.wait_ge(up_l, b + 2)
                pe.wait_ge(f_lo, b * 2 + 3)
                pe.wait_ge(vl_l, b * 8 + 9)
                apart(pe)
                with pe.Fori(0, NCH // 2) as c2:
                    for s in range(4):
                        co = slice((s % 2) * P, (s % 2 + 1) * P)
                        px = bass.ds(c2 * (2 * CHUNK) + (s // 2) * CHUNK, CHUNK)
                        pe.wait_ge(r_out, b * 16 + c2 * 4 + (s + 1))
                        three(ps[:, s, :], fold[0][0][:, co], fold[0][1][:, co], vl_hi[:, px], vl_lo[:, px], True, False)
                        three(ps[:, s, :], fold[1][0][:, co], fold[1][1][:, co], up_hi[:, px], up_lo[:, px],
                              False, True).then_inc(r_ps, 1)

        @block.scalar
        def _(act):
            def pad(src, r, n):
                r0 = 0 if r == 0 else 8 * r + 1
                r1 = min(8 * r + 9, H)
                act.activation(pad_hi[:, 1 + r0:1 + r1, 1:1 + W],
                               img[:, src, r0 * W:r1 * W].rearrange("p (h w) -> p h w", w=W), ACT.Copy).then_inc(pad_h, 1)

            def evac(dst, bank, b_ap, ready, norm=None, scale=BNS):
                act.wait_ge(cv_ps, ready)
                act.activation(dst, ps[:, bank, :], ACT.Identity, bias=b_ap, scale=scale).then_inc(cv_out, 1)
                if norm is not None:
                    act.activation(ps[:, bank, :], ps[:, bank, :], ACT.Square, bias=b_ap, scale=scale,
                                   accum_out=norm).then_inc(sq_done, 1)

            def t_split(a, bank, ready):
                act.wait_ge(t_ps, ready)
                act.activation(t_hi[a], ps[:, bank, :], ACT.Copy).then_inc(t_h, 1)

            def k_unit_split(buf, n):
                act.wait_ge(t_ps, n * 2 + 1)
                act.activation(buf, ps[:, 4, :], ACT.Square).then_inc(k_sq, 1)
                act.wait_ge(k_sum, n + 1)
                act.activation(knorm[:, 32:64], knorm[:, 0:32], ACT.Sqrt).then_inc(k_root, 1)
                act.wait_ge(k_unit, n + 1)
                act.activation(t_hi[1], buf, ACT.Copy).then_inc(t_h, 1)

            def exps(t, n):
                act.wait_ge(s_ready, n * NT + t + 1)
                act.wait_ge(p_used, n * (NT - 1) + (t + 2 if t < 3 else t + 1))
                act.activation(prob[:, t % 4, 0, :], ps[:, 4 + t % 2, :], ACT.Exp)
                act.activation(ps[:, 4 + t % 2, :], ps[:, 4 + t % 2, :], ACT.Exp).then_inc(p_full, 1)

            def attend(b, g, last_group):
                n = b * NCH + g
                for t in range(3, NT):
                    exps(t, n)
                if not last_group:
                    exps(0, n + 1)
                    exps(1, n + 1)
                for qt in range(QT):
                    act.wait_ge(rden_in, n * QT + qt + 1)
                    act.activation(onorm[:, qt, :], ps[:, qt, 0:C], ACT.Copy, scale=rden[:, qt:qt + 1]).then_inc(o_norm, 1)
                if not last_group:
                    exps(2, n + 1)

            def chain(b, s, step):
                d = (2 * b + s) * 8
                if step == 0:
                    act.wait_ge(a_dve, d + 1)
                    act.activation(stat[:, 2:3], stat[:, 0:1], ACT.Sqrt).then_inc(a_act, 1)
                elif step == 1:
                    act.wait_ge(a_dve, d + 6)
                    act.activation(attn[:, :], attn[:, :], ACT.Exp, bias=stat[:, 4:5], accum_out=stat[:, 5:6]).then_inc(a_act, 1)
                else:
                    act.wait_ge(f_ps, 2 * b + s + 1)
                    act.activation(fold[s][0], ps[:, 5, 2 * P:2 * P + C], ACT.Copy).then_inc(f_hi, 1)

            def sp_split(step, dst, src, b):
                act.wait_ge(sp_ps, b * 10 + step)
                last = None
                for d, s_ in zip(dst, src):
                    last = act.activation(d, s_, ACT.Copy)
                last.then_inc(sp_hi, 1)

            for _ in range(4):
                act.sem_inc(o_norm, 1)
                act.sem_inc(r_out, 1)
            act.sem_inc(sq_done, 1)
            act.wait_ge(w_in, 16)
            act.activation(whi[:, :], image[:, 0:NW], ACT.Copy).then_inc(w_hi, 1)
            act.wait_ge(c_in, 16)
            act.wait_ge(prep, 1)
            with act.Fori(0, B) as b:
                with act.Fori(0, NCH // 2) as c2:
                    for s in range(2):
                        n = b * NCH + c2 * 2 + s
                        px = bass.ds(c2 * (2 * CHUNK) + s * CHUNK, CHUNK)
                        for a, dst, bb in ((0, q_st, BQ), (1, k_st, BK)):
                            act.wait_ge(qk_ps, n * 2 + a + 1)
                            act.activation(dst[0:96, px], ps[0:96, 4 * s + a, :], ACT.Identity,
                                           bias=cst[0:96, K_BIAS + bb:K_BIAS + bb + 1]).then_inc(qk_hi, 1)
                        for v in range(2):
                            act.wait_ge(v_ps, n * 2 + (v + 5))
                            act.activation(vhi_t[:, bass.ds(c2 * 8 + s * 4 + v * 2, 2), 0:C],
                                           ps[:, 2 + v, :].rearrange("p (t c) -> p t c", c=C), ACT.Copy).then_inc(v_hi, 1)
                for t in range(3):
                    exps(t, b * NCH)
                with act.Fori(0, NCH - 1) as g:
                    attend(b, g, False)
                attend(b, NCH - 1, True)
                act.wait_ge(m_free, b * M_PER_IMAGE + M_PER_IMAGE + 2)
                for r in range(8):
                    pad(0, r, b)
                act.wait_ge(d_in, b * 16 + 16)
                act.activation(dhi, image[:, 0:ND], ACT.Copy).then_inc(d_hi, 1)
                with act.Fori(0, NCH) as c:
                    cv = b * 30 + c * 3
                    evac(scr[:, CHUNK:2 * CHUNK], 1, bscaled[:, 1:2], cv + 1)
                    k_unit_split(scr[:, CHUNK:2 * CHUNK], b * 10 + c)
                    evac(scr[:, 0:CHUNK], 0, bscaled[:, 0:1], cv + 2, norms[:, bass.ds(c, 1)])
                    t_split(0, 3, b * 20 + c * 2 + 2)
                    act.wait_ge(vl_l, b * 8 + c + 1)
                    evac(scr[:, 2 * CHUNK:3 * CHUNK], 2, bscaled[:, 2:3], cv + 3)
                hi8 = ring[:, 0:1024]
                chain(b, 0, 0)
                act.wait_ge(vl_l, b * 8 + 9)
                act.wait_ge(sp_ps, b * 10 + 1)
                act.activation(scr[:, 1024:2048], ps[:, 0:2, :].rearrange("p a n -> p (a n)"), ACT.Relu, scale=0.25 * BNS).then_inc(sp_f, 1)
                for r in range(4):
                    pad(1, r, b)
                sp_split(2, [hi8], [ps[:, 2:4, :].rearrange("p a n -> p (a n)")], b)
                for r in range(4, 8):
                    pad(1, r, b)
                y1 = stage[:, 0:1024].rearrange("p (f y) -> p y f", y=HH)
                evac(image[:, N:N + CHUNK], 6, bscaled[:, 4:5], b * 30 + 25)
                act.wait_ge(sp_ps, b * 10 + 3)
                for h in range(2):
                    last = act.activation(y1[:, 16 * h:16 * (h + 1), :], ps[:, h, :].rearrange("p (y f) -> p y f", f=WH), ACT.Copy)
                last.then_inc(sp_f, 1)
                evac(image[:, N + CHUNK:N + 2 * CHUNK], 7, bscaled[:, 4:5], b * 30 + 26)
                sp_split(4, [hi8], [ps[:, 2:4, :].rearrange("p a n -> p (a n)")], b)
                evac(scr[:, 0:CHUNK], 6, bscaled[:, 3:4], b * 30 + 27)
                evac(scr[:, CHUNK:2 * CHUNK], 7, bscaled[:, 3:4], b * 30 + 28)
                chain(b, 0, 1)
                sp_split(5, *freq(ring[:, 2304:2848]), b)
                chain(b, 0, 2)
                act.wait_ge(sp_ps, b * 10 + 6)
                for part in range(2):
                    for h in range(2):
                        last = act.activation(stage[:, part * 640 + h * 272:part * 640 + (h + 1) * 272], ps[:, 3 * part + h, 0:272],
                                              ACT.Relu, scale=BNS)
                last.then_inc(sp_f, 1)
                sp_split(7, *ky_tiles(ring[:, 0:1280]), b)
                act.wait_ge(sp_ps, b * 10 + 8)
                z1 = stage[:, 0:1024].rearrange("p (y f) -> p f y", f=WH)
                act.activation(z1[:, 0:1, :], ps[:, 0, 0:32].rearrange("p (f y) -> p f y", y=HH), ACT.Copy)
                act.activation(z1[:, 2:16, :], ps[:, 0, 64:512].rearrange("p (f y) -> p f y", y=HH), ACT.Copy)
                act.activation(z1[:, 16:32, :], ps[:, 1, :].rearrange("p (f y) -> p f y", y=HH), ACT.Copy)
                act.activation(z1[:, 1:2, :], ps[:, 3, 0:32].rearrange("p (f y) -> p f y", y=HH), ACT.Copy).then_inc(sp_f, 1)
                sp_split(9, [ring[:, 0:512], ring[:, 512:1024]], [ps[:, 2, :], ps[:, 4, :]], b)
                act.wait_ge(sp_z, b + 1)
                act.activation(hi8, stage[:, 1024:2048], ACT.Copy).then_inc(sp_hi, 1)
                evac(stage[:, 0:CHUNK], 0, 0.0, b * 30 + 29, norms[:, NCH:NCH + 1])
                evac(stage[:, CHUNK:2 * CHUNK], 1, 0.0, b * 30 + 30, norms[:, NCH + 1:NCH + 2])
                for h in range(HCH):
                    k_unit_split(scr[:, h * CHUNK:(h + 1) * CHUNK], b * 10 + (8 + h))
                    t_split(0, 3, b * 20 + 16 + 2 * h + 2)
                chain(b, 1, 0)
                chain(b, 1, 1)
                act.wait_ge(up_d, b * 16 + 16)
                act.activation(up_hi, image[:, 0:N], ACT.Copy).then_inc(up_h, 1)
                chain(b, 1, 2)
                with act.Fori(0, NCH // 2) as c2:
                    for s in range(4):
                        act.wait_ge(r_ps, b * 16 + c2 * 4 + (s + 1))
                        act.wait_ge(out_dma[s], b * 64 + c2 * 16 + 16)
                        act.activation(stage[:, s * CHUNK:(s + 1) * CHUNK], ps[:, s, :], ACT.Identity,
                                       bias=bias(BO + s % 2)).then_inc(r_out, 1)

        @block.vector
        def _(dve):
            def sub(o, a, b_):
                return dve.tensor_tensor(o, a, f(b_), ALU.subtract)

            def pad(src, r, b):
                dve.wait_ge(pad_h, b * 16 + src * 8 + r + 1)
                r0 = 0 if r == 0 else 8 * r + 1
                r1 = min(8 * r + 9, H)
                sub(pad_lo[:, 1 + r0:1 + r1, 1:1 + W], img[:, src, r0 * W:r1 * W].rearrange("p (h w) -> p h w", w=W),
                    pad_hi[:, 1 + r0:1 + r1, 1:1 + W]).then_inc(pad_l, 1)

            def low(t, n0):
                dve.wait_ge(p_full, n0 + t + 1)
                sub(prob[:, t % 4, 1, :], ps[:, 4 + t % 2, :], prob[:, t % 4, 0, :]).then_inc(p_lo, 1)

            def maxima(i, m):
                dve.wait_ge(m_ready, m + 1)
                dve.tensor_reduce(mx_t[:, i // NCH, i % NCH:i % NCH + 1], ps[:, 6 + i % 2, :], AX.X, ALU.max).then_inc(m_free, 1)

            def first_maxima(b, c2, s, qt):
                dve.wait_ge(m_ready, b * M_PER_IMAGE + c2 * (2 * QT) + (s * QT - QT + qt + 1))
                apart(dve)
                dve.tensor_reduce(mx_t[:, qt, bass.ds(c2 * 2 + (s - 1), 1)], ps[:, 6 + qt % 2, :], AX.X, ALU.max).then_inc(m_free, 1)

            def x_split(b, c2, s):
                dve.wait_ge(xs_hi, b * NCH + c2 * 2 + (s + 1))
                sub(xs[:, s % 2, 1], img[:, :, bass.ds(c2 * (2 * CHUNK) + s * CHUNK, CHUNK)], xs[:, s % 2, 0]).then_inc(xs_lo, 1)

            def projected(b, c2, s, first, last):
                n = b * NCH + c2 * 2 + s
                px = bass.ds(c2 * (2 * CHUNK) + s * CHUNK, CHUNK)
                for a, dst, bb, r in ((0, q_st, BQ, 64), (1, k_st, BK, 32)):
                    dve.wait_ge(qk_hi, n * 2 + (a + 1))
                    dve.scalar_tensor_tensor(dst[r:r + 32, px], ps[r:r + 32, 4 * s + a, :],
                                             cst[r:r + 32, K_BIAS + bb:K_BIAS + bb + 1],
                                             f(dst[r:r + 32, px]), ALU.add, ALU.subtract).then_inc(qk_lo, 1)
                for qt in range(QT):
                    if not first:
                        first_maxima(b, c2, s, qt)
                    if qt == 1 and not last:
                        x_split(b, c2, s + 1)
                for v in range(2):
                    dve.wait_ge(v_hi, n * 2 + (v + 1))
                    t_ = bass.ds(c2 * 8 + (s * 4 + v * 2), 2)
                    sub(vlo_t[:, t_, :], ps[:, 2 + v, :].rearrange("p (t c) -> p t c", c=C),
                        vhi_t[:, t_, 0:C]).then_inc(v_lo, 1)

            def minus_maxima(m):
                dve.wait_ge(m_free, m + 2)
                dve.tensor_reduce(maxcol[:, 96:96 + 32 * (QT - 1) + 1:32], mx_t, AX.X, ALU.max, negate=True).then_inc(negmax, 1)

            def maxima_rows(group, m):
                for h in range(2):
                    dve.wait_ge(m_ready, m + h + 1)
                    dve.tensor_copy(q_st[96:128, bass.ds(group * CHUNK + h * 256, 256)], ps[96:128, 6 + h, 0:256]).then_inc(m_free, 1)

            def attend(b, g, last_group):
                n = b * NCH + g
                m0 = b * M_PER_IMAGE + (NT + 2) + g * M_PER_GROUP
                i = 0
                for t in range(1, NT):
                    if not last_group:
                        for _ in range(MAX_AT[t]):
                            maxima(i, m0 + i)
                            i += 1
                        if t == MAX_TILES + 1:
                            minus_maxima(m0 + NT)
                        if t == MAX_TILES + 3:
                            maxima_rows(g + 1, m0 + NT)
                    if t + 2 < NT:
                        low(t + 2, n * NT)
                    elif not last_group:
                        low(t + 2 - NT, (n + 1) * NT)
                for qt in range(QT):
                    dve.wait_ge(o_done, n * QT + qt + 1)
                    dve.reciprocal(rden[:, qt:qt + 1], ps[:, qt, C:C + 1]).then_inc(rden_in, 1)
                if not last_group:
                    low(2, (n + 1) * NT)
                m1 = m0 + (0 if last_group else NT + 2)
                px = bass.ds(g * CHUNK, CHUNK)
                for c in range(CT):
                    dve.wait_ge(m_ready, m1 + c + 1)
                    dve.scalar_tensor_tensor(img[:, c, px], ps[:, 6 + c, :], bias(BV + c), img[:, c, px],
                                             ALU.add, ALU.add).then_inc(m_free, 1)

            def t_split(a, bank, ready):
                dve.wait_ge(t_h, ready)
                sub(t_lo[a], ps[:, bank, :], t_hi[a]).then_inc(t_l, 1)

            def k_unit_split(buf, n):
                heads = lambda z: z.rearrange("p (a c) -> p a c", c=P // 8)
                dve.wait_ge(k_sq, n + 1)
                dve.tensor_reduce(knorm[:, 0:32], heads(buf), AX.X, ALU.add).then_inc(k_sum, 1)
                dve.wait_ge(k_root, n + 1)
                dve.tensor_scalar(knorm[:, 32:64], knorm[:, 32:64], NORM_FLOOR, None, ALU.max).then_inc(k_inv, 1)
                dve.wait_ge(k_inv, n * 2 + 1)
                dve.reciprocal(knorm[:, 32:64], knorm[:, 32:64]).then_inc(k_inv, 1)
                dve.wait_ge(k_inv, n * 2 + 2)
                dve.tensor_tensor(heads(buf), heads(ps[:, 4, :]),
                                  knorm[:, 32:64].unsqueeze(2).to_broadcast([P, 32, P // 8]), ALU.mult).then_inc(k_unit, 1)
                dve.wait_ge(t_h, n * 2 + 1)
                sub(t_lo[1], buf, t_hi[1]).then_inc(t_l, 1)

            def gram_add(n, first=False):
                dve.wait_ge(g_ps, n + 1)
                dve.wait_ge(g_sum, n + 1)
                if first:
                    dve.tensor_copy(gram[:, :], ps[:, 5, 0:P]).then_inc(g_sum, 1)
                else:
                    dve.tensor_tensor(gram[:, :], gram[:, :], ps[:, 5, 0:P], ALU.add).then_inc(g_sum, 1)

            def sp_split(step, dst, hi, src, b):
                dve.wait_ge(sp_hi, b * 6 + step)
                last = None
                for d, h_, s_ in zip(dst, hi, src):
                    last = sub(d, s_, h_)
                last.then_inc(sp_lo, 1)

            def chain(b, s, step):
                d = (2 * b + s) * 8
                a = (2 * b + s) * 2
                nch = NCH if s == 0 else HCH
                if step == 0:
                    dve.wait_ge(sq_done, b * 10 + (9 if s == 0 else 11))
                    dve.tensor_reduce(stat[:, 0:1], norms[:, s * NCH:s * NCH + nch], AX.X, ALU.add).then_inc(a_dve, 1)
                elif step == 1:
                    dve.wait_ge(a_act, a + 1)
                    dve.tensor_scalar(stat[:, 2:3], stat[:, 2:3], NORM_FLOOR, None, ALU.max).then_inc(a_dve, 1)
                    dve.wait_ge(a_dve, d + 2)
                    dve.reciprocal(stat[:, 2:3], stat[:, 2:3]).then_inc(a_dve, 1)
                    dve.wait_ge(a_dve, d + 3)
                    dve.tensor_tensor(stat[:, 2:3], stat[:, 2:3], bias(TEMP), ALU.mult).then_inc(a_dve, 1)
                elif step == 2:
                    dve.wait_ge(a_dve, d + 4)
                    dve.wait_ge(g_sum, b * 10 + (9 if s == 0 else 11))
                    dve.scalar_tensor_tensor(attn[:, :], gram[:, :], stat[:, 2:3], cst[:, K_NEG:K_NEG + P],
                                             ALU.mult, ALU.add).then_inc(a_dve, 1)
                    dve.wait_ge(a_dve, d + 5)
                    dve.tensor_reduce(stat[:, 4:5], attn[:, :], AX.X, ALU.max, negate=True).then_inc(a_dve, 1)
                elif step == 3:
                    dve.wait_ge(a_act, a + 2)
                    dve.reciprocal(stat[:, 6:7], stat[:, 5:6]).then_inc(a_dve, 1)
                    dve.wait_ge(a_dve, d + 7)
                    dve.tensor_scalar(attn[:, :], attn[:, :], stat[:, 6:7], None, ALU.mult).then_inc(a_dve, 1)
                else:
                    dve.wait_ge(f_hi, 2 * b + s + 1)
                    sub(fold[s][1], ps[:, 5, 2 * P:2 * P + C], fold[s][0]).then_inc(f_lo, 1)

            tab = [cst[:, K_UP + i * WH:K_UP + (i + 1) * WH] for i in range(4)]
            v_h = image[:, N:N + NHALF].rearrange("p (y x) -> p y x", x=WH)
            wide = image[:, N + NHALF:N + 3 * NHALF].rearrange("p (y x) -> p y x", x=W)
            up = image[:, 0:N].rearrange("p (y x) -> p y x", x=W)
            tmp = image[:, N + 3 * NHALF:N + 4 * NHALF]

            def up_step(b, i):
                dve.wait_ge(up_d, b * 16 + i + 1)
                if i == 0:
                    dve.wait_ge(cv_out, b * 30 + 26)
                if i < 6:
                    o = wide[:, :, (i // 3):W:2]
                    t_ = tmp[:, 0:HH * (WH - 1)].rearrange("p (y x) -> p y x", x=WH - 1)
                    row = lambda w_: w_.unsqueeze(1).to_broadcast([P, HH, w_.shape[-1]])
                    if i == 0 or i == 3:
                        ins = dve.tensor_tensor(o, v_h, row(tab[1 if i == 0 else 2]), ALU.mult)
                    elif i == 1:
                        ins = dve.tensor_tensor(t_, v_h[:, :, 0:WH - 1], row(tab[0][:, 1:WH]), ALU.mult)
                    elif i == 4:
                        ins = dve.tensor_tensor(t_, v_h[:, :, 1:WH], row(tab[3][:, 0:WH - 1]), ALU.mult)
                    elif i == 2:
                        ins = dve.tensor_tensor(o[:, :, 1:WH], o[:, :, 1:WH], t_, ALU.add)
                    else:
                        ins = dve.tensor_tensor(o[:, :, 0:WH - 1], o[:, :, 0:WH - 1], t_, ALU.add)
                else:
                    j = (i - 6) % 5
                    odd = (i - 6) // 5
                    o = up[:, odd:H:2, :]
                    col = lambda w_: w_.unsqueeze(2).to_broadcast([P, w_.shape[-1], W])
                    if j == 0:
                        ins = dve.tensor_tensor(o, wide, col(tab[2 if odd else 1]), ALU.mult)
                    else:
                        k0 = (1, 16)[(j - 1) // 2] if not odd else (0, 16)[(j - 1) // 2]
                        k1 = (16, 32)[(j - 1) // 2] if not odd else (16, 31)[(j - 1) // 2]
                        t_ = tmp[:, 0:(k1 - k0) * W].rearrange("p (y x) -> p y x", x=W)
                        if (j - 1) % 2 == 0:
                            s_ = wide[:, k0 + 1:k1 + 1, :] if odd else wide[:, k0 - 1:k1 - 1, :]
                            ins = dve.tensor_tensor(t_, s_, col(tab[3 if odd else 0][:, k0:k1]), ALU.mult)
                        else:
                            ins = dve.tensor_tensor(o[:, k0:k1, :], o[:, k0:k1, :], t_, ALU.add)
                ins.then_inc(up_d, 1)

            for _ in range(2):
                dve.sem_inc(p_lo, 1)
                dve.sem_inc(m_free, 1)
                dve.sem_inc(v_lo, 1)
            for s_ in (vl_l, g_sum, f_lo, up_d, up_l):
                dve.sem_inc(s_, 1)
            dve.wait_ge(c_in, 16)
            dve.tensor_scalar(bscaled[:, :], cst[:, K_BIAS + BL:K_BIAS + BL + 5], BNS, None, ALU.mult).then_inc(prep, 1)
            dve.memset(maxcol[:, :], 0.0).then_inc(prep, 1)
            dve.wait_ge(w_hi, 1)
            sub(wlo[:, :], image[:, 0:NW], whi[:, :]).then_inc(w_lo, 1)
            with dve.Fori(0, B) as b:
                x_split(b, 0, 0)
                for s in range(2):
                    projected(b, 0, s, s == 0, False)
                with dve.Fori(1, NCH // 2 - 1) as c2:
                    for s in range(2):
                        projected(b, c2, s, False, False)
                for s in range(2):
                    projected(b, NCH // 2 - 1, s, False, s == 1)
                m = b * M_PER_IMAGE
                for qt in range(QT):
                    first_maxima(b, NCH // 2, 0, qt)
                minus_maxima(m + NT)
                maxima_rows(0, m + NT)
                for t in range(3):
                    low(t, b * (NCH * NT))
                with dve.Fori(0, NCH - 1) as g:
                    attend(b, g, False)
                attend(b, NCH - 1, True)
                dve.wait_ge(g_sum, b * 10 + 1)
                dve.memset(gram[:, :], 0.0)
                for r in range(8):
                    pad(0, r, b)
                for s in range(4):
                    dve.wait_ge(out_dma[s], b * 64 + 16)
                dve.wait_ge(m_free, b * M_PER_IMAGE + M_PER_IMAGE + 2)
                dve.tensor_reduce(stage[:, 1024:2048].rearrange("p (y x) -> p y x", x=WH),
                                  img[:, 1, :].rearrange("p (y a x b) -> p y x a b", y=HH, a=2, b=2), AX.XY, ALU.add).then_inc(pool_f, 1)
                dve.wait_ge(pool_hi, b + 1)
                sub(ring[:, 1024:2048], stage[:, 1024:2048], ring[:, 0:1024]).then_inc(pool_lo, 1)
                dve.wait_ge(d_hi, b + 1)
                sub(dlo, image[:, 0:ND], dhi).then_inc(d_lo, 1)
                with dve.Fori(0, NCH) as c:
                    k_unit_split(scr[:, CHUNK:2 * CHUNK], b * 10 + c)
                    t_split(0, 3, b * 20 + c * 2 + 2)
                    px = bass.ds(c * CHUNK, CHUNK)
                    dve.wait_ge(vl_h, b * 8 + c + 1)
                    sub(vl_lo[:, px], scr[:, 2 * CHUNK:3 * CHUNK], vl_hi[:, px]).then_inc(vl_l, 1)
                    gram_add(b * 10 + c)
                chain(b, 0, 0)
                chain(b, 0, 1)
                for r in range(4):
                    pad(1, r, b)
                lo8, hi8 = ring[:, 1280:2304], ring[:, 0:1024]
                sp_split(1, [lo8], [hi8], [ps[:, 2:4, :].rearrange("p a n -> p (a n)")], b)
                for r in range(4, 8):
                    pad(1, r, b)
                chain(b, 0, 2)
                sp_split(2, [lo8], [hi8], [ps[:, 2:4, :].rearrange("p a n -> p (a n)")], b)
                chain(b, 0, 3)
                for i in range(0, 3):
                    up_step(b, i)
                d_, s_ = freq(ring[:, 2848:3392])
                h_, _ = freq(ring[:, 2304:2848])
                sp_split(3, d_, h_, s_, b)
                chain(b, 0, 4)
                for i in range(3, 7):
                    up_step(b, i)
                d_, s_ = ky_tiles(ring[:, 1280:2560])
                h_, _ = ky_tiles(ring[:, 0:1280])
                sp_split(4, d_, h_, s_, b)
                for i in range(7, 11):
                    up_step(b, i)
                sp_split(5, [lo8[:, 0:512], lo8[:, 512:1024]], [hi8[:, 0:512], hi8[:, 512:1024]], [ps[:, 2, :], ps[:, 4, :]], b)
                dve.wait_ge(sp_ps, b * 10 + 10)
                dve.tensor_tensor(stage[:, 1024:2048], ps[:, 0:2, :].rearrange("p a n -> p (a n)"), scr[:, 1024:2048], ALU.add).then_inc(sp_z, 1)
                dve.wait_ge(sp_hi, b * 6 + 6)
                sub(ring[:, 1024:2048], stage[:, 1024:2048], hi8).then_inc(sp_lo, 1)
                for i in range(11, 16):
                    up_step(b, i)
                for h in range(HCH):
                    k_unit_split(scr[:, h * CHUNK:(h + 1) * CHUNK], b * 10 + (8 + h))
                    t_split(0, 3, b * 20 + 16 + 2 * h + 2)
                    gram_add(b * 10 + 8 + h, h == 0)
                for step in range(4):
                    chain(b, 1, step)
                dve.wait_ge(up_h, b + 1)
                sub(up_lo, image[:, 0:N], up_hi).then_inc(up_l, 1)
                chain(b, 1, 4)

        @block.gpsimd
        def _(pool):
            def x_hi(b, c2, s):
                pool.wait_ge(x_in[s], b * (16 * NCH // 2) + c2 * 16 + 32)
                pool.wait_ge(v_ps, (b * NCH + c2 * 2 + s) * 2 + 2)
                apart(pool)
                pool.tensor_copy(xs[:, s, 0], img[:, :, bass.ds(c2 * (2 * CHUNK) + s * CHUNK, CHUNK)]).then_inc(xs_hi, 1)

            with pool.Fori(0, B) as b:
                pool.wait_ge(f_lo, b * 2 + 1)
                apart(pool)
                for s in range(2):
                    x_hi(b, 0, s)
                pool.wait_ge(qk_lo, b * (2 * NCH) + 2)
                apart(pool)
                pool.tensor_copy(qmax[0:96, :], f(q_st)[0:96, 0:CHUNK]).then_inc(qmax_in, 1)
                pool.wait_ge(qmax_in, b * NCH + 1)
                apart(pool)
                pool.memset(f(k_st[96:128, :]), 1.0).then_inc(ones_set, 1)
                pool.wait_ge(ones_set, b * 2 + 1)
                apart(pool)
                pool.memset(f(vhi_t[:, :, C:VC]), 1.0).then_inc(ones_set, 1)
                with pool.Fori(1, NCH // 2) as c2:
                    for s in range(2):
                        x_hi(b, c2, s)
                with pool.Fori(1, NCH) as g:
                    pool.wait_ge(m_ready, b * M_PER_IMAGE + g * M_PER_GROUP + (NT - M_PER_GROUP))
                    apart(pool)
                    pool.tensor_copy(qmax[0:96, :], f(q_st)[0:96, bass.ds(g * CHUNK, CHUNK)]).then_inc(qmax_in, 1)
                pool.wait_ge(m_free, b * M_PER_IMAGE + M_PER_IMAGE + 2)
                apart(pool)
                for z in (vhi, vlo):
                    pool.memset(f(z[:, 0:WP - 1]), 0.0).then_inc(border, 1)
                    pool.memset(f(z[:, WP - 1:WP - 1 + (HP - 1) * WP].rearrange("p (h w) -> p h w", w=WP)[:, :, 0:2]), 0.0).then_inc(border, 1)
                    pool.memset(f(z[:, (HP - 1) * WP + 1:HP * WP]), 0.0).then_inc(border, 1)
                pool.wait_ge(pool_f, b + 1)
                apart(pool)
                pool.tensor_copy(ring[:, 0:1024], stage[:, 1024:2048]).then_inc(pool_hi, 1)
                with pool.Fori(0, NCH) as c:
                    pool.wait_ge(cv_out, b * 30 + c * 3 + 3)
                    apart(pool)
                    pool.tensor_copy(vl_hi[:, bass.ds(c * CHUNK, CHUNK)], scr[:, 2 * CHUNK:3 * CHUNK]).then_inc(vl_h, 1)


def transforms():
    n = WH
    i = np.arange(n)
    s = 1 / np.sqrt(n)
    th = 2 * np.pi * np.outer(i, i) / n
    fx, ox = np.zeros((n, n)), np.zeros((n, n))
    fx[:, 0], fx[:, 1] = s, s * np.cos(np.pi * i)
    ox[0], ox[1] = s, s * np.cos(np.pi * i)
    for k in range(1, n // 2):
        fx[:, 2 * k], fx[:, 2 * k + 1] = s * np.cos(th[:, k]), -s * np.sin(th[:, k])
        ox[2 * k], ox[2 * k + 1] = 2 * s * np.cos(th[k]), -2 * s * np.sin(th[k])
    d_x, d_out = np.kron(np.eye(4), fx), np.kron(np.eye(4), ox)
    co, si = s * np.cos(th), s * np.sin(th)
    d_y = np.kron(np.eye(2), np.block([[co, -si], [si, co]]))
    real = np.concatenate([co, -si], 1)
    d_y0 = np.zeros((P, P))
    d_y0[0:32, 0:64] = real
    d_y0[64:128, 64:128] = d_y[0:64, 0:64]
    d_y16 = np.zeros((P, 64))
    d_y16[32:64] = real
    d_re = np.kron(np.eye(4), np.concatenate([co, si], 1))
    d_im = np.kron(np.eye(4), np.concatenate([-si, co], 1))
    return np.concatenate([d_x, d_y0, d_y, d_y16, d_re, d_im, d_out], 1).astype(np.float32)


def upsample_tables():
    k = np.arange(WH)
    e0, o1 = 2 * k / (W - 1) * 1.0, 0.5 - (2 * k + 1) / (2 * (W - 1))
    frac_e = 2 * k * (WH - 1) / (W - 1) - (k - 1)
    e0 = np.where(k > 0, 1 - frac_e, 0.0)
    e1 = np.where(k > 0, frac_e, 1.0)
    o1 = (2 * k + 1) * (WH - 1) / (W - 1) - k
    return np.concatenate([e0, e1, 1 - o1, o1]).astype(np.float32)


def kernel(**inputs):
    import concourse.bacc as bacc
    from concourse.bass_utils import run_bass_kernel_spmd

    a = {k: np.asarray(v) for k, v in inputs.items()}
    l1 = lambda n: a["L1_conv_" + n]

    def tiles(w):
        return w.reshape(-1, P, w.shape[1]).transpose(1, 0, 2).reshape(P, -1)

    def taps(w):
        return w.transpose(1, 2, 3, 0).reshape(P, -1)

    fu = l1("w_stfu")[:, :, 0, 0].reshape(64, 2, 64, 2).transpose(1, 0, 3, 2)
    fu = [fu[r].reshape(64, P).T for r in range(2)]
    st2 = np.zeros((P, P), np.float32)
    st2[0:64] = l1("w_st2")[:, :, 0, 0].T
    weights = np.concatenate(
        [tiles(np.tile(a["L0_conv_wq"].T, (1, 4))), tiles(np.tile(a["L0_conv_wk"].T, (1, 4))), tiles(a["L0_conv_wv"].T)]
        + [taps(l1(n)) for n in ("wq", "wk", "wv")]
        + [np.tile(l1("w_st1")[:, :, 0, 0].T, (1, 2))] + [np.tile(z, (1, 2)) for z in fu] + [st2], 1)
    weights2 = np.concatenate([taps(l1("wk2")), taps(l1("wv2")), transforms()], 1)
    head = np.arange(P) // (P // 8)
    other = np.where(head[:, None] == head[None, :], 0, -1e30).astype(np.float32)
    wo = l1("w_out")[:, :, 0, 0].T
    cols = [np.tile(a["L0_conv_bq"], 4), np.tile(a["L0_conv_bk"], 4), a["L0_conv_bv"][0:P], a["L0_conv_bv"][P:],
            l1("bq"), l1("bk"), l1("bv"), l1("bk2"), l1("bv2"), l1("b_out")[0:P], l1("b_out")[P:],
            np.repeat(l1("temperature").reshape(-1), P // 8)]
    consts = np.concatenate([tiles(wo), np.eye(P, dtype=np.float32), other,
                             np.tile(upsample_tables()[None], (P, 1)), np.stack(cols, 1)], 1)
    arrays = {"x": a["x"].reshape(B * CT, P, N), "weights": weights, "weights2": weights2, "consts": consts}
    arrays = {k: np.ascontiguousarray(v) for k, v in arrays.items()}
    assert weights.shape == (P, NW) and weights2.shape == (P, ND) and consts.shape == (P, NK)
    nc = bacc.Bacc("TRN2", target_bir_lowering=False, num_devices=1)
    args = [nc.dram_tensor(k, v.shape, mybir.dt.from_np(v.dtype), kind="ExternalInput").ap() for k, v in arrays.items()]
    args.append(nc.dram_tensor("out", (B * CT, P, N), F32, kind="ExternalOutput").ap())
    build(nc, *args)
    r = run_bass_kernel_spmd(nc, [arrays], core_ids=[0])
    return r.results[0]["out"].reshape(B, C, H, W)
```

```python
from contextlib import ExitStack

import concourse.bass as bass
import numpy as np
from concourse import mybir

ALU = mybir.AluOpType
ACT = mybir.ActivationFunctionType
F32 = mybir.dt.float32
F32R = mybir.dt.float32r
AX = mybir.AxisListType

P = 128
B, C, H, W = 4, 256, 64, 64
N = H * W
CT = C // P
CHUNK = 512
NCH = N // CHUNK
NT = N // P
QT = CHUNK // P
VC = C + 2
HP, WP = H + 2, W + 2
HH, WH = H // 2, W // 2
NHALF = HH * WH
HCH = NHALF // CHUNK
KX = WH // 2 + 1
BNS = float(np.float32(1.0 / np.sqrt(1.0 + 1e-05)))
NORM_FLOOR = 1e-12

W_Q, W_K, W_V = 0, CT * P, 2 * CT * P
W_L = W_V + CT * C
W_ST1 = W_L + 3 * 9 * P
W_FU = W_ST1 + P
W_ST2 = W_FU + 2 * P
NW = W_ST2 + P
D_X = 2 * 9 * P
D_Y0, D_Y, D_Y16 = D_X + P, D_X + 2 * P, D_X + 3 * P
D_RE = D_Y16 + 64
D_IM = D_RE + 2 * P
D_OUT = D_IM + 2 * P
ND = D_OUT + P
K_WO, K_ID, K_NEG, K_UP = 0, 2 * C, 2 * C + P, 2 * C + 2 * P
K_BIAS = K_UP + 2 * (WH - 1)
BQ, BK, BV, BL, BH, BO, TEMP = 0, 1, 2, 4, 7, 9, 11
NK = K_BIAS + 12

M_PER_GROUP = NT + 2 + 2
M_PER_IMAGE = (NT + 2) + (NCH - 1) * M_PER_GROUP + 2
MAX_TILES = 24
MAX_AT = [(t - 1) * NT // MAX_TILES - (t - 2) * NT // MAX_TILES if 1 < t <= MAX_TILES + 1 else 0 for t in range(NT)]


def build(nc, x, weights, weights2, consts, out):
    ctx = ExitStack()
    with ctx:
        def sb(name, cols, dt=F32):
            return ctx.enter_context(nc.sbuf_tensor(name, [P, cols], dt))

        def sem(name):
            return ctx.enter_context(nc.semaphore(name))

        image = sb("image", CT * N)
        qk = sb("qk", 2 * N, F32R)
        vhi = sb("vhi", NT * VC, F32R)
        vlo = sb("vlo", NT * C, F32R)
        ring = sb("ring", 4 * 2 * CHUNK, F32R)
        whi = sb("whi", NW, F32R)
        wlo = sb("wlo", NW, F32R)
        cst = sb("cst", NK)
        scr = sb("scr", 4 * CHUNK)
        stage = sb("stage", 4 * CHUNK)
        qmax = sb("qmax", CHUNK, F32R)
        maxcol = sb("maxcol", P + 32 * (QT - 1))
        mx = sb("mx", QT * NCH)
        rden = sb("rden", QT)
        bscaled = sb("bscaled", 5)
        gram = sb("gram", P)
        norms = sb("norms", 2 * NCH)
        knorm = sb("knorm", 2 * QT * 8)
        attn = sb("attn", P)
        stat = sb("stat", 8)
        ps = ctx.enter_context(nc.psum_tensor("ps", [P, 8, CHUNK], F32))

        img = image[:, :].rearrange("p (c n) -> p c n", c=CT)
        q_st, k_st = qk[:, 0:N], qk[:, N:2 * N]
        vhi_t = vhi[:, :].rearrange("p (t c) -> p t c", c=VC)
        vlo_t = vlo[:, :].rearrange("p (t c) -> p t c", c=C)
        prob = ring[:, :].rearrange("p (s a n) -> p s a n", s=4, a=2)
        xs = ring[:, :].rearrange("p (s a c n) -> p s a c n", s=2, a=2, c=CT)
        onorm = scr[:, 0:QT * C].rearrange("p (t c) -> p t c", c=C)
        mx_t = mx[:, :].rearrange("p (t c) -> p t c", c=NCH)
        ident = cst[:, K_ID:K_ID + P]
        bias = lambda i: cst[:, K_BIAS + i:K_BIAS + i + 1]
        pad_hi = vhi[:, 0:HP * WP].rearrange("p (h w) -> p h w", w=WP)
        pad_lo = vlo[:, 0:HP * WP].rearrange("p (h w) -> p h w", w=WP)
        D0 = 4400
        D1 = D0 + ND
        dhi, dlo = vhi[:, D0:D0 + ND], vlo[:, D0:D0 + ND]
        fold = {0: (vhi[:, D1:D1 + C], vlo[:, D1:D1 + C]), 1: (vhi[:, D0:D0 + C], vlo[:, D0:D0 + C])}
        up_hi, up_lo = vhi[:, 0:N], vlo[:, 0:N]
        vl_hi, vl_lo = qk[:, 0:N], qk[:, N:2 * N]
        t_hi = {a: ring[:, 2048 + 1024 * a:2560 + 1024 * a] for a in (0, 1)}
        t_lo = {a: ring[:, 2560 + 1024 * a:3072 + 1024 * a] for a in (0, 1)}
        kt_h = [(ring[:, 2560:3072], ring[:, 3072:3584]), (ring[:, 3584:4096], qmax[:, :])]
        qt_h = [tuple(z[:, D0 + C + h * CHUNK:D0 + C + (h + 1) * CHUNK] for z in (vhi, vlo)) for h in range(HCH)]
        OUT_BANKS = (0, 1, 6, 7)

        w_in, c_in, w_hi, w_lo, prep = (sem(n) for n in ("w_in", "c_in", "w_hi", "w_lo", "prep"))
        x_in = [sem(f"x_in{i}") for i in range(2)]
        xs_hi, xs_lo = sem("xs_hi"), sem("xs_lo")
        qk_ps, qk_hi, qk_lo, v_ps, v_hi, v_lo = (sem(n) for n in ("qk_ps", "qk_hi", "qk_lo", "v_ps", "v_hi", "v_lo"))
        ones_set, qmax_in, m_ready, m_free, negmax = (sem(n) for n in ("ones_set", "qmax_in", "m_ready", "m_free", "negmax"))
        s_ready, p_used, p_full, p_lo = (sem(n) for n in ("s_ready", "p_used", "p_full", "p_lo"))
        o_done, rden_in, o_norm = (sem(n) for n in ("o_done", "rden_in", "o_norm"))
        border, pad_h, pad_l, d_in, d_hi, d_lo = (sem(n) for n in ("border", "pad_h", "pad_l", "d_in", "d_hi", "d_lo"))
        pool_f, pool_hi, pool_lo = (sem(n) for n in ("pool_f", "pool_hi", "pool_lo"))
        cv_ps, cv_out, sq_done, vl_h, vl_l = (sem(n) for n in ("cv_ps", "cv_out", "sq_done", "vl_h", "vl_l"))
        t_ps, t_h, t_l, g_ps, g_sum = (sem(n) for n in ("t_ps", "t_h", "t_l", "g_ps", "g_sum"))
        sp_ps, sp_f, sp_hi, sp_lo, sp_z = (sem(n) for n in ("sp_ps", "sp_f", "sp_hi", "sp_lo", "sp_z"))
        up_d, up_h, up_l = sem("up_d"), sem("up_h"), sem("up_l")
        a_dve, a_act = sem("a_dve"), sem("a_act")
        k_sq, k_sum, k_root, k_inv, k_unit = (sem(n) for n in ("k_sq", "k_sum", "k_root", "k_inv", "k_unit"))
        f_ps, f_hi, f_lo = sem("f_ps"), sem("f_hi"), sem("f_lo")
        r_ps, r_out = sem("r_ps"), sem("r_out")
        out_dma = [sem(f"out_dma{i}") for i in range(4)]

        UP_STEPS = 12
        wide = image[:, N:N + 2 * NHALF].rearrange("p (y x) -> p y x", x=W)
        v_h = image[:, N + 3 * NHALF:N + 4 * NHALF]
        v_hw = v_h.rearrange("p (y x) -> p y x", x=WH)
        up_room = image[:, N + 2 * NHALF:N + 4 * NHALF]
        up = image[:, 0:N].rearrange("p (y x) -> p y x", x=W)

        f = lambda ap: ap.bitcast(F32)

        passed = sem("passed")

        def apart(eng):
            eng.sem_inc(passed, 1)

        block = ctx.enter_context(nc.Block())

        def freq(dst):
            d, s = [], []
            for bank, k0, n in ((0, 0, 8), (1, 8, 8), (2, 16, 1)):
                v = ps[:, bank, 0:n * 64].rearrange("p (k r y) -> p k r y", r=2, y=HH)
                for r in range(2):
                    d.append(dst[64 * r:64 * (r + 1), k0 * 32:(k0 + n) * 32].rearrange("p (k y) -> p k y", y=HH))
                    s.append(v[64 * r:64 * (r + 1), :, r, :])
            return d, s

        def ky_tiles(dst):
            return ([dst[:, 0:512], dst[:, 512:1024], dst[0:32, 1024:1280]],
                    [ps[:, 2, :], ps[:, 3, :], ps[0:32, 4, 0:256]])

        @block.sync
        def _(sp):
            sp.dma_start(cst[:, :], consts).then_inc(c_in, 16)
            sp.dma_start(image[:, 0:NW], weights).then_inc(w_in, 16)
            for s in range(2):
                sp.sem_inc(x_in[s], 16)
            for s in range(4):
                sp.sem_inc(out_dma[s], 16)
            sp.wait_ge(w_lo, 1)
            apart(sp)
            def load(b, c2):
                for s in range(2):
                    sp.wait_ge(x_in[s], b * (16 * NCH // 2) + c2 * 16 + 16)
                    sp.dma_start(
                        img[:, :, bass.ds(c2 * (2 * CHUNK) + s * CHUNK, CHUNK)],
                        x[bass.ds(b * CT, CT), :, bass.ds(c2 * (2 * CHUNK) + s * CHUNK, CHUNK)]
                        .rearrange("c p n -> p c n")).then_inc(x_in[s], 16)

            def load_weights2(b):
                sp.wait_ge(pad_l, b * 16 + 8)
                sp.dma_start(image[:, 0:ND], weights2).then_inc(d_in, 16)

            def store(b, c2):
                for s in range(4):
                    sp.wait_ge(r_out, b * 16 + c2 * 4 + (4 + s + 1))
                    sp.dma_start(
                        out[bass.ds(b * CT + s % 2, 1), :, bass.ds(c2 * (2 * CHUNK) + (s // 2) * CHUNK, CHUNK)]
                        .rearrange("c p n -> p (c n)"),
                        stage[:, s * CHUNK:(s + 1) * CHUNK]).then_inc(out_dma[s], 16)

            with sp.Fori(0, NCH // 2) as c2:
                load(0, c2)
            with sp.Fori(0, B - 1) as b:
                load_weights2(b)
                with sp.Fori(0, NCH // 2) as c2:
                    store(b, c2)
                    load(b + 1, c2)
            load_weights2(B - 1)
            with sp.Fori(0, NCH // 2) as c2:
                store(B - 1, c2)
            for s in range(4):
                sp.wait_ge(out_dma[s], 16 + 16 * B * NCH // 2)

        @block.tensor
        def _(pe):
            def three(o, w_hi_ap, w_lo_ap, x_hi_ap, x_lo_ap, start, stop):
                pe.matmul(o, w_hi_ap, x_hi_ap, start=start, stop=False)
                pe.matmul(o, w_hi_ap, x_lo_ap, start=False, stop=False)
                return pe.matmul(o, w_lo_ap, x_hi_ap, start=False, stop=stop)

            def transposes(o, src, n):
                for i in range(n):
                    last = pe.transpose(o[:, i * P:(i + 1) * P], src[:, i * P:(i + 1) * P], ident)
                return last

            def scores(group, t, n0):
                pe.wait_ge(p_lo, n0 + t + 1)
                pe.matmul(ps[:, 4 + t % 2, :], k_st[:, t * P:(t + 1) * P],
                          q_st[:, bass.ds(group * CHUNK, CHUNK)], start=True, stop=True).then_inc(s_ready, 1)

            def maxima(i, m):
                qt, jc = i // NCH, i % NCH
                pe.wait_ge(m_free, m + 1)
                pe.matmul(ps[:, 6 + i % 2, :], qmax[0:96, qt * P:(qt + 1) * P],
                          k_st[0:96, jc * CHUNK:(jc + 1) * CHUNK], start=True, stop=True).then_inc(m_ready, 1)

            def first_maxima(b, c2, s, qt):
                pe.wait_ge(m_free, b * M_PER_IMAGE + c2 * (2 * QT) + (s * QT - QT + qt + 1))
                pe.matmul(ps[:, 6 + qt % 2, :], qmax[0:96, qt * P:(qt + 1) * P],
                          k_st[0:96, bass.ds(c2 * (2 * CHUNK) + (s - 1) * CHUNK, CHUNK)],
                          start=True, stop=True).then_inc(m_ready, 1)

            def project(b, c2, s, first):
                n = b * NCH + c2 * 2 + s
                pe.wait_ge(xs_lo, n + 1)
                for a, w0 in ((0, W_Q), (1, W_K)):
                    for c in range(CT):
                        w = slice(w0 + c * P, w0 + (c + 1) * P)
                        last = three(ps[:, 4 * s + a, :], whi[:, w], wlo[:, w], xs[:, s, 0, c, :], xs[:, s, 1, c, :],
                                     c == 0, c == CT - 1)
                    last.then_inc(qk_ps, 1)
                if not first:
                    pe.wait_ge(qk_lo, n * 2)
                    pe.wait_ge(qmax_in, b * NCH + 1)
                    pe.wait_ge(r_out, b * 16 + 4)
                for j in range(QT):
                    if not first:
                        first_maxima(b, c2, s, j)
                    if j % 2 == 0:
                        pe.wait_ge(v_lo, n * 2 + (j // 2 + 1))
                    for c in range(CT):
                        w = slice(W_V + c * C, W_V + (c + 1) * C)
                        last = three(ps[:, 2 + j // 2, (j % 2) * C:(j % 2 + 1) * C],
                                     xs[:, s, 0, c, j * P:(j + 1) * P], xs[:, s, 1, c, j * P:(j + 1) * P],
                                     whi[:, w], wlo[:, w], c == 0, c == CT - 1)
                    if j % 2:
                        last.then_inc(v_ps, 1)

            def maxima_rows(n, m):
                pe.wait_ge(negmax, n + 1)
                for h in range(2):
                    pe.wait_ge(m_free, m + h + 1)
                    for i in range(2):
                        last = pe.transpose(ps[:, 6 + h, i * P:(i + 1) * P], maxcol[:, 32 * (2 * h + i):32 * (2 * h + i) + P], ident)
                    last.then_inc(m_ready, 1)

            def weigh(t, n):
                pe.wait_ge(p_lo, n * NT + t + 3)
                for qt in range(QT):
                    if t == 0:
                        pe.wait_ge(o_norm, n * QT + qt + 1)
                    hi = prob[:, t % 4, 0, qt * P:(qt + 1) * P]
                    lo = prob[:, t % 4, 1, qt * P:(qt + 1) * P]
                    pe.matmul(ps[:, qt, 0:VC], hi, vhi_t[:, t, :], start=(t == 0), stop=False)
                    pe.matmul(ps[:, qt, 0:C], hi, vlo_t[:, t, :], start=False, stop=False)
                    last = pe.matmul(ps[:, qt, 0:VC], lo, vhi_t[:, t, :], start=False, stop=(t == NT - 1))
                    if t == NT - 1:
                        last.then_inc(o_done, 1)
                    elif qt == QT - 1:
                        last.then_inc(p_used, 1)

            def attend(b, g, last_group):
                n = b * NCH + g
                n0 = n * NT
                m0 = b * M_PER_IMAGE + (NT + 2) + g * M_PER_GROUP
                i = 0
                for t in range(1, NT):
                    if not last_group:
                        for _ in range(MAX_AT[t]):
                            if i == 0:
                                pe.wait_ge(qmax_in, n + 2)
                            maxima(i, m0 + i)
                            i += 1
                        if t == MAX_TILES + 4:
                            maxima_rows(n + 1, m0 + NT)
                    if t + 2 < NT:
                        scores(g, t + 2, n0)
                    elif not last_group:
                        if t + 2 == NT:
                            pe.wait_ge(m_free, m0 + NT + 2 + 2)
                        scores(g + 1, t + 2 - NT, n0 + NT)
                    weigh(t, n)
                if not last_group:
                    scores(g + 1, 2, n0 + NT)
                    weigh(0, n + 1)
                m1 = m0 + (0 if last_group else NT + 2)
                for c in range(CT):
                    pe.wait_ge(m_free, m1 + c + 1)
                for qt in range(QT):
                    pe.wait_ge(o_norm, (n + 1) * QT + qt + 1)
                    for c in range(CT):
                        last = pe.transpose(ps[:, 6 + c, qt * P:(qt + 1) * P], onorm[:, qt, c * P:(c + 1) * P], ident)
                        if qt == QT - 1:
                            last.then_inc(m_ready, 1)

            def conv(o, hi, lo, w0, src, taps=range(9), half=False, rows=None, c=None):
                for tap in taps:
                    dy, dx = tap // 3, tap % 3
                    w_h, w_l = hi[:, w0 + tap * P:w0 + (tap + 1) * P], lo[:, w0 + tap * P:w0 + (tap + 1) * P]
                    if half:
                        r0 = 2 * (CHUNK // WH) * c + dy
                        x_h, x_l = (z[:, r0:r0 + 2 * (CHUNK // WH) - 1:2, dx:dx + 2 * WH - 1:2] for z in src)
                    else:
                        x_h, x_l = (z[:, bass.ds(c * (CHUNK // W) + dy, CHUNK // W), dx:dx + W] for z in src)
                    last = three(o, w_h, w_l, x_h, x_l, tap == 0, tap == 8)
                return last

            def gram(hi_lo_q, hi_lo_k, first, last):
                for i in range(QT):
                    s = slice(i * P, (i + 1) * P)
                    m = three(ps[:, 5, 0:P], hi_lo_q[0][:, s], hi_lo_q[1][:, s], hi_lo_k[0][:, s], hi_lo_k[1][:, s],
                              first and i == 0, last and i == QT - 1)
                return m

            def fold_weights(b, s):
                pe.wait_ge(a_dve, (2 * b + s) * 8 + 8)
                pe.matmul(ps[:, 5, 2 * P:2 * P + C], attn[:, :], cst[:, K_WO + (1 - s) * C:K_WO + (2 - s) * C],
                          start=True, stop=True).then_inc(f_ps, 1)

            for _ in range(4):
                pe.sem_inc(v_ps, 1)
                pe.sem_inc(p_used, 1)
            pe.wait_ge(w_lo, 1)
            pe.wait_ge(c_in, 16)
            pe.wait_ge(prep, 2)
            apart(pe)
            with pe.Fori(0, B) as b:
                pe.wait_ge(r_out, b * 16 + 2)
                for s in range(2):
                    project(b, 0, s, s == 0)
                with pe.Fori(1, NCH // 2) as c2:
                    for s in range(2):
                        project(b, c2, s, False)
                pe.wait_ge(qk_lo, b * (2 * NCH) + 2 * NCH)
                for qt in range(QT):
                    first_maxima(b, NCH // 2, 0, qt)
                pe.wait_ge(v_lo, b * (2 * NCH) + 2 * NCH + 2)
                maxima_rows(b * NCH, b * M_PER_IMAGE + NT)
                pe.wait_ge(ones_set, b * 2 + 2)
                pe.wait_ge(m_free, b * M_PER_IMAGE + NT + 2 + 2)
                for t in range(3):
                    scores(0, t, b * (NCH * NT))
                weigh(0, b * NCH)
                with pe.Fori(0, NCH - 1) as g:
                    attend(b, g, False)
                attend(b, NCH - 1, True)
                pe.wait_ge(border, b * 6 + 6)
                apart(pe)
                with pe.Fori(0, NCH) as c:
                    n = b * 10 + c
                    pe.wait_ge(pad_l, b * 16 + c + 1)
                    conv(ps[:, 1, :], whi, wlo, W_L + 9 * P, (pad_hi, pad_lo), c=c).then_inc(cv_ps, 1)
                    pe.wait_ge(sq_done, n + 1)
                    conv(ps[:, 0, :], whi, wlo, W_L, (pad_hi, pad_lo), taps=range(3), c=c)
                    pe.wait_ge(cv_out, b * 28 + c * 3 + 1)
                    transposes(ps[:, 4, :], scr[:, CHUNK:2 * CHUNK], QT).then_inc(t_ps, 1)
                    conv(ps[:, 0, :], whi, wlo, W_L, (pad_hi, pad_lo), taps=range(3, 9), c=c).then_inc(cv_ps, 1)
                    conv(ps[:, 2, :], whi, wlo, W_L + 18 * P, (pad_hi, pad_lo), taps=range(3), c=c)
                    pe.wait_ge(cv_out, b * 28 + c * 3 + 2)
                    transposes(ps[:, 3, :], scr[:, 0:CHUNK], QT).then_inc(t_ps, 1)
                    conv(ps[:, 2, :], whi, wlo, W_L + 18 * P, (pad_hi, pad_lo), taps=range(3, 9), c=c).then_inc(cv_ps, 1)
                    pe.wait_ge(t_l, b * 20 + c * 2 + 2)
                    pe.wait_ge(g_sum, b * 8 + c + 1)
                    gram((t_hi[0], t_lo[0]), (t_hi[1], t_lo[1]), True, True).then_inc(g_ps, 1)
                sp0, lo0 = b * 10, b * 6
                nine = lambda k: slice(k, k + P)
                pe.wait_ge(pool_lo, b + 1)
                pe.wait_ge(sq_done, b * 10 + 9)
                for h in range(2):
                    w = nine(W_ST1)
                    last = three(ps[:, h, :], whi[:, w], wlo[:, w], ring[:, h * CHUNK:(h + 1) * CHUNK],
                                 ring[:, 1024 + h * CHUNK:1024 + (h + 1) * CHUNK], True, True)
                last.then_inc(sp_ps, 1)
                pe.wait_ge(d_lo, b + 1)
                src = (pad_hi, pad_lo)
                v_conv = lambda c, taps: conv(ps[:, 6 + c, :], dhi, dlo, 9 * P, src, taps=taps, half=True, c=c)
                k_conv = lambda c, taps: conv(ps[:, 6 + c, :], dhi, dlo, 0, src, taps=taps, half=True, c=c)
                pe.wait_ge(pad_l, b * 16 + 12)
                v_conv(0, range(0, 3))
                pe.wait_ge(cv_out, b * 28 + 24)
                pe.wait_ge(sp_f, b * 4 + 1)
                transposes(ps[:, 2, :], scr[:, 1024:1536], 4)
                transposes(ps[:, 3, :], scr[:, 1536:2048], 4).then_inc(sp_ps, 1)
                pe.wait_ge(pad_l, b * 16 + 16)
                v_conv(0, range(3, 9)).then_inc(cv_ps, 1)
                pe.wait_ge(sp_lo, lo0 + 1)
                for y in range(8):
                    last = three(ps[:, y // 4, (y % 4) * P:(y % 4 + 1) * P], ring[:, y * P:(y + 1) * P],
                                 ring[:, 1280 + y * P:1280 + (y + 1) * P], dhi[:, nine(D_X)], dlo[:, nine(D_X)], True, True)
                last.then_inc(sp_ps, 1)
                v_conv(1, range(0, 3))
                pe.wait_ge(sp_f, b * 4 + 2)
                transposes(ps[:, 2, :], stage[:, 0:512], 4)
                transposes(ps[:, 3, :], stage[:, 512:1024], 4).then_inc(sp_ps, 1)
                v_conv(1, range(3, 9)).then_inc(cv_ps, 1)
                pe.wait_ge(sp_lo, lo0 + 2)
                for k in range(8):
                    d = nine(D_Y0 if k == 0 else D_Y)
                    three(ps[:, k // 4, (k % 4) * P:(k % 4 + 1) * P], ring[:, k * P:(k + 1) * P],
                          ring[:, 1280 + k * P:1280 + (k + 1) * P], dhi[:, d], dlo[:, d], True, True)
                d = slice(D_Y16, D_Y16 + 64)
                three(ps[:, 2, 0:64], ring[:, 0:P], ring[:, 1280:1280 + P], dhi[:, d], dlo[:, d], True, True).then_inc(sp_ps, 1)
                pe.wait_ge(cv_out, b * 28 + 25)
                k_conv(0, range(0, 4))
                fold_weights(b, 0)
                pe.wait_ge(sp_lo, lo0 + 3)
                for part in range(2):
                    for h in range(2):
                        w, r = nine(W_FU + part * P), slice(h * 272, (h + 1) * 272)
                        last = three(ps[:, 3 * part + h, 0:272], whi[:, w], wlo[:, w], ring[:, 2304:2848][:, r],
                                     ring[:, 2848:3392][:, r], True, True)
                last.then_inc(sp_ps, 1)
                k_conv(0, range(4, 6))
                pe.wait_ge(sp_f, b * 4 + 3)
                for part in range(2):
                    transposes(ps[:, 2 + part, :], stage[:, part * 640:part * 640 + 512], 4)
                for part in range(2):
                    last = pe.transpose(ps[0:32, 4, part * P:(part + 1) * P], stage[:, part * 640 + 512:part * 640 + 544], ident)
                last.then_inc(sp_ps, 1)
                k_conv(0, range(6, 9)).then_inc(cv_ps, 1)
                pe.wait_ge(cv_out, b * 28 + 26)
                k_conv(1, range(0, 2))
                pe.wait_ge(sp_lo, lo0 + 4)
                for q in range(4):
                    o = ps[:, q // 2, (q % 2) * 256:(q % 2 + 1) * 256]
                    re, im = q * P, (4 + q) * P
                    three(o, ring[:, re:re + P], ring[:, 1280 + re:1280 + re + P],
                          dhi[:, D_RE:D_RE + 256], dlo[:, D_RE:D_RE + 256], True, False)
                    three(o, ring[:, im:im + P], ring[:, 1280 + im:1280 + im + P],
                          dhi[:, D_IM:D_IM + 256], dlo[:, D_IM:D_IM + 256], False, True)
                o = ps[:, 3, 0:64]
                three(o, ring[0:32, 1024:1152], ring[0:32, 2304:2432], dhi[0:32, D_RE:D_RE + 64], dlo[0:32, D_RE:D_RE + 64], True, False)
                three(o, ring[0:32, 1152:1280], ring[0:32, 2432:2560], dhi[0:32, D_IM:D_IM + 64], dlo[0:32, D_IM:D_IM + 64],
                      False, True).then_inc(sp_ps, 1)
                pe.wait_ge(cv_out, b * 28 + 27)
                transposes(ps[:, 6, :], scr[:, 0:CHUNK], QT).then_inc(t_ps, 1)
                k_conv(1, range(2, 4))
                pe.wait_ge(sp_f, b * 4 + 4)
                transposes(ps[:, 2, :], stage[:, 0:512], 4)
                transposes(ps[:, 4, :], stage[:, 512:1024], 4).then_inc(sp_ps, 1)
                k_conv(1, range(4, 9)).then_inc(cv_ps, 1)
                pe.wait_ge(sp_lo, lo0 + 5)
                for y in range(8):
                    last = three(ps[:, y // 4, (y % 4) * P:(y % 4 + 1) * P], ring[:, y * P:(y + 1) * P],
                                 ring[:, 1280 + y * P:1280 + (y + 1) * P], dhi[:, nine(D_OUT)], dlo[:, nine(D_OUT)], True, True)
                last.then_inc(sp_ps, 1)
                pe.wait_ge(cv_out, b * 28 + 28)
                transposes(ps[:, 7, :], scr[:, CHUNK:2 * CHUNK], QT).then_inc(t_ps, 1)
                pe.wait_ge(sp_lo, lo0 + 6)
                w = nine(W_ST2)
                for h in range(HCH):
                    for i in range(QT):
                        z = slice(h * CHUNK + i * P, h * CHUNK + (i + 1) * P)
                        last = three(ps[:, 2 + h, i * P:(i + 1) * P], ring[:, z], ring[:, 1024:2048][:, z], whi[:, w], wlo[:, w],
                                     True, True)
                    last.then_inc(t_ps, 1)
                for h in range(HCH):
                    three(ps[:, h, :], whi[:, w], wlo[:, w], ring[:, h * CHUNK:(h + 1) * CHUNK],
                          ring[:, 1024 + h * CHUNK:1024 + (h + 1) * CHUNK], True, True).then_inc(cv_ps, 1)
                for h in range(HCH):
                    pe.wait_ge(t_l, b * 20 + 19 + h)
                    last = gram(qt_h[h], kt_h[h], h == 0, h == HCH - 1)
                last.then_inc(g_ps, 1)

                def output(c2, s, low):
                    co = slice((s % 2) * P, (s % 2 + 1) * P)
                    px = bass.ds(c2 * (2 * CHUNK) + (s // 2) * CHUNK, CHUNK)
                    hi, lo = (vl_hi, vl_lo) if low else (up_hi, up_lo)
                    w_h, w_l = fold[0 if low else 1]
                    return three(ps[:, OUT_BANKS[s], :], w_h[:, co], w_l[:, co], hi[:, px], lo[:, px], low, not low)

                pe.wait_ge(f_lo, b * 2 + 2)
                pe.wait_ge(vl_l, b * 8 + 9)
                pe.wait_ge(sq_done, b * 10 + 11)
                for s in range(4):
                    output(0, s, True)
                fold_weights(b, 1)
                pe.wait_ge(f_lo, b * 2 + 3)
                pe.wait_ge(up_l, b * 4 + 1)
                for s in range(4):
                    output(0, s, False).then_inc(r_ps, 1)
                with pe.Fori(1, NCH // 2) as c2:
                    pe.wait_ge(up_l, b * 4 + c2 + 1)
                    for s in range(4):
                        pe.wait_ge(r_out, b * 16 + c2 * 4 + (s + 1))
                        output(c2, s, True)
                        output(c2, s, False).then_inc(r_ps, 1)

        @block.scalar
        def _(act):
            def pad(src, r, n):
                r0 = 0 if r == 0 else 8 * r + 1
                r1 = min(8 * r + 9, H)
                act.activation(pad_hi[:, 1 + r0:1 + r1, 1:1 + W],
                               img[:, src, r0 * W:r1 * W].rearrange("p (h w) -> p h w", w=W), ACT.Copy).then_inc(pad_h, 1)

            def evac(dst, bank, b_ap, ready, norm=None, scale=BNS):
                act.wait_ge(cv_ps, ready)
                act.activation(dst, ps[:, bank, :], ACT.Identity, bias=b_ap, scale=scale).then_inc(cv_out, 1)
                if norm is not None:
                    act.activation(ps[:, bank, :], ps[:, bank, :], ACT.Square, bias=b_ap, scale=scale,
                                   accum_out=norm).then_inc(sq_done, 1)

            def t_split(hi, bank, ready, scale=1.0):
                act.wait_ge(t_ps, ready)
                act.activation(hi, ps[:, bank, :], ACT.Copy, scale=scale).then_inc(t_h, 1)

            def k_square(buf, bank, ready):
                act.wait_ge(t_ps, ready)
                act.activation(buf, ps[:, bank, :], ACT.Square).then_inc(k_sq, 1)

            def k_unit_hi(buf, n, hi):
                act.wait_ge(k_sum, n + 1)
                act.activation(knorm[:, 32:64], knorm[:, 0:32], ACT.Sqrt).then_inc(k_root, 1)
                act.wait_ge(k_unit, n + 1)
                act.activation(hi, buf, ACT.Copy).then_inc(t_h, 1)

            def exps(t, n):
                act.wait_ge(s_ready, n * NT + t + 1)
                if t == 3:
                    act.wait_ge(o_norm, n * QT + QT)
                act.wait_ge(p_used, n * (NT - 1) + (t + 2 if t < 3 else t + 1))
                act.activation(prob[:, t % 4, 0, :], ps[:, 4 + t % 2, :], ACT.Exp)
                act.activation(ps[:, 4 + t % 2, :], ps[:, 4 + t % 2, :], ACT.Exp).then_inc(p_full, 1)

            def attend(b, g, last_group):
                n = b * NCH + g
                for t in range(3, NT):
                    exps(t, n)
                if not last_group:
                    exps(0, n + 1)
                    exps(1, n + 1)
                if not last_group:
                    exps(2, n + 1)

            def chain(b, s, step):
                d = (2 * b + s) * 8
                if step == 0:
                    act.wait_ge(a_dve, d + 1)
                    act.activation(stat[:, 2:3], stat[:, 0:1], ACT.Sqrt).then_inc(a_act, 1)
                elif step == 1:
                    act.wait_ge(a_dve, d + 6)
                    act.activation(attn[:, :], attn[:, :], ACT.Exp, bias=stat[:, 4:5], accum_out=stat[:, 5:6]).then_inc(a_act, 1)
                else:
                    act.wait_ge(f_ps, 2 * b + s + 1)
                    act.activation(fold[s][0], ps[:, 5, 2 * P:2 * P + C], ACT.Copy).then_inc(f_hi, 1)

            def sp_split(step, dst, src, b):
                act.wait_ge(sp_ps, b * 10 + step)
                last = None
                for d, s_ in zip(dst, src):
                    last = act.activation(d, s_, ACT.Copy)
                last.then_inc(sp_hi, 1)

            for _ in range(4):
                act.sem_inc(r_out, 1)
            act.sem_inc(sq_done, 1)
            act.wait_ge(w_in, 16)
            act.activation(whi[:, :], image[:, 0:NW], ACT.Copy).then_inc(w_hi, 1)
            act.wait_ge(c_in, 16)
            act.wait_ge(prep, 1)
            with act.Fori(0, B) as b:
                with act.Fori(0, NCH // 2) as c2:
                    for s in range(2):
                        n = b * NCH + c2 * 2 + s
                        px = bass.ds(c2 * (2 * CHUNK) + s * CHUNK, CHUNK)
                        for a, dst, bb in ((0, q_st, BQ), (1, k_st, BK)):
                            act.wait_ge(qk_ps, n * 2 + a + 1)
                            act.activation(dst[0:96, px], ps[0:96, 4 * s + a, :], ACT.Identity,
                                           bias=cst[0:96, K_BIAS + bb:K_BIAS + bb + 1]).then_inc(qk_hi, 1)
                        for v in range(2):
                            act.wait_ge(v_ps, n * 2 + (v + 5))
                            act.activation(vhi_t[:, bass.ds(c2 * 8 + s * 4 + v * 2, 2), 0:C],
                                           ps[:, 2 + v, :].rearrange("p (t c) -> p t c", c=C), ACT.Copy).then_inc(v_hi, 1)
                for t in range(3):
                    exps(t, b * NCH)
                with act.Fori(0, NCH - 1) as g:
                    attend(b, g, False)
                attend(b, NCH - 1, True)
                act.wait_ge(o_done, b * (NCH * QT) + NCH * QT)
                for r in range(6):
                    pad(0, r, b)
                act.wait_ge(m_free, b * M_PER_IMAGE + M_PER_IMAGE + 2)
                for r in range(6, 8):
                    pad(0, r, b)

                def low_chunk(c, last):
                    n = b * NCH + c
                    evac(scr[:, CHUNK:2 * CHUNK], 1, bscaled[:, 1:2], b * 30 + c * 3 + 1)
                    k_square(scr[:, CHUNK:2 * CHUNK], 4, b * 20 + c * 2 + 1)
                    k_unit_hi(scr[:, CHUNK:2 * CHUNK], b * 10 + c, t_hi[1])
                    if last:
                        for r in range(6):
                            pad(1, r, b)
                    evac(scr[:, 0:CHUNK], 0, bscaled[:, 0:1], b * 30 + c * 3 + 2, norms[:, bass.ds(c, 1)])
                    t_split(t_hi[0], 3, b * 20 + c * 2 + 2)
                    act.wait_ge(vl_l, b * 8 + c + 1)
                    evac(scr[:, 2 * CHUNK:3 * CHUNK], 2, bscaled[:, 2:3], b * 30 + c * 3 + 3)

                with act.Fori(0, NCH - 1) as c:
                    low_chunk(c, False)
                low_chunk(NCH - 1, True)
                for r in range(6, 8):
                    pad(1, r, b)
                hi8 = ring[:, 0:1024]
                act.wait_ge(vl_l, b * 8 + 9)
                act.wait_ge(sp_ps, b * 10 + 1)
                act.activation(scr[:, 1024:2048], ps[:, 0:2, :].rearrange("p a n -> p (a n)"), ACT.Relu, scale=0.25 * BNS).then_inc(sp_f, 1)
                sp_split(2, [hi8], [ps[:, 2:4, :].rearrange("p a n -> p (a n)")], b)
                chain(b, 0, 0)
                y1 = stage[:, 0:1024].rearrange("p (f y) -> p y f", y=HH)
                act.wait_ge(sp_ps, b * 10 + 3)
                for h in range(2):
                    last = act.activation(y1[:, 16 * h:16 * (h + 1), :], ps[:, h, :].rearrange("p (y f) -> p y f", f=WH), ACT.Copy)
                last.then_inc(sp_f, 1)
                evac(v_h[:, 0:CHUNK], 6, bscaled[:, 4:5], b * 30 + 25)
                chain(b, 0, 1)
                sp_split(4, [hi8], [ps[:, 2:4, :].rearrange("p a n -> p (a n)")], b)
                evac(v_h[:, CHUNK:2 * CHUNK], 7, bscaled[:, 4:5], b * 30 + 26)
                sp_split(5, *freq(ring[:, 2304:2848]), b)
                chain(b, 0, 2)
                act.wait_ge(sp_ps, b * 10 + 6)
                for part in range(2):
                    for h in range(2):
                        last = act.activation(stage[:, part * 640 + h * 272:part * 640 + (h + 1) * 272], ps[:, 3 * part + h, 0:272],
                                              ACT.Relu, scale=BNS)
                last.then_inc(sp_f, 1)
                sp_split(7, *ky_tiles(ring[:, 0:1280]), b)
                evac(scr[:, 0:CHUNK], 6, bscaled[:, 3:4], b * 30 + 27)
                act.wait_ge(sp_ps, b * 10 + 8)
                z1 = stage[:, 0:1024].rearrange("p (y f) -> p f y", f=WH)
                act.activation(z1[:, 0:1, :], ps[:, 0, 0:32].rearrange("p (f y) -> p f y", y=HH), ACT.Copy)
                act.activation(z1[:, 2:16, :], ps[:, 0, 64:512].rearrange("p (f y) -> p f y", y=HH), ACT.Copy)
                act.activation(z1[:, 16:32, :], ps[:, 1, :].rearrange("p (f y) -> p f y", y=HH), ACT.Copy)
                act.activation(z1[:, 1:2, :], ps[:, 3, 0:32].rearrange("p (f y) -> p f y", y=HH), ACT.Copy).then_inc(sp_f, 1)
                k_square(scr[:, 0:CHUNK], 6, b * 20 + 17)
                sp_split(9, [ring[:, 0:512], ring[:, 512:1024]], [ps[:, 2, :], ps[:, 4, :]], b)
                k_unit_hi(scr[:, 0:CHUNK], b * 10 + 8, kt_h[0][0])
                evac(scr[:, CHUNK:2 * CHUNK], 7, bscaled[:, 3:4], b * 30 + 28)
                act.wait_ge(sp_z, b + 1)
                act.activation(hi8, stage[:, 1024:2048], ACT.Copy).then_inc(sp_hi, 1)
                k_square(scr[:, CHUNK:2 * CHUNK], 7, b * 20 + 18)
                k_unit_hi(scr[:, CHUNK:2 * CHUNK], b * 10 + 9, kt_h[1][0])
                for h in range(HCH):
                    t_split(qt_h[h][0], 2 + h, b * 20 + 19 + h, BNS)
                for h in range(HCH):
                    act.wait_ge(cv_ps, b * 30 + 29 + h)
                    act.activation(ps[:, h, :], ps[:, h, :], ACT.Square, scale=BNS, accum_out=norms[:, NCH + h:NCH + h + 1]).then_inc(sq_done, 1)
                chain(b, 1, 0)
                for i in range(4):
                    act.wait_ge(up_d, b * UP_STEPS + UP_STEPS + 1)
                    act.activation(up_hi[:, i * 1024:(i + 1) * 1024], image[:, i * 1024:(i + 1) * 1024], ACT.Copy).then_inc(up_h, 1)
                    if i == 0:
                        chain(b, 1, 1)
                chain(b, 1, 2)
                with act.Fori(0, NCH // 2) as c2:
                    for s in range(4):
                        act.wait_ge(r_ps, b * 16 + c2 * 4 + (s + 1))
                        act.wait_ge(out_dma[s], b * 64 + c2 * 16 + 16)
                        act.activation(stage[:, s * CHUNK:(s + 1) * CHUNK], ps[:, OUT_BANKS[s], :], ACT.Identity,
                                       bias=bias(BO + s % 2)).then_inc(r_out, 1)

        @block.vector
        def _(dve):
            def sub(o, a, b_):
                return dve.tensor_tensor(o, a, f(b_), ALU.subtract)

            def pad(src, r, b):
                dve.wait_ge(pad_h, b * 16 + src * 8 + r + 1)
                r0 = 0 if r == 0 else 8 * r + 1
                r1 = min(8 * r + 9, H)
                sub(pad_lo[:, 1 + r0:1 + r1, 1:1 + W], img[:, src, r0 * W:r1 * W].rearrange("p (h w) -> p h w", w=W),
                    pad_hi[:, 1 + r0:1 + r1, 1:1 + W]).then_inc(pad_l, 1)

            def low(t, n0):
                dve.wait_ge(p_full, n0 + t + 1)
                sub(prob[:, t % 4, 1, :], ps[:, 4 + t % 2, :], prob[:, t % 4, 0, :]).then_inc(p_lo, 1)

            def maxima(i, m):
                dve.wait_ge(m_ready, m + 1)
                dve.tensor_reduce(mx_t[:, i // NCH, i % NCH:i % NCH + 1], ps[:, 6 + i % 2, :], AX.X, ALU.max).then_inc(m_free, 1)

            def first_maxima(b, c2, s, qt):
                dve.wait_ge(m_ready, b * M_PER_IMAGE + c2 * (2 * QT) + (s * QT - QT + qt + 1))
                apart(dve)
                dve.tensor_reduce(mx_t[:, qt, bass.ds(c2 * 2 + (s - 1), 1)], ps[:, 6 + qt % 2, :], AX.X, ALU.max).then_inc(m_free, 1)

            def x_split(b, c2, s):
                dve.wait_ge(xs_hi, b * NCH + c2 * 2 + (s + 1))
                sub(xs[:, s % 2, 1], img[:, :, bass.ds(c2 * (2 * CHUNK) + s * CHUNK, CHUNK)], xs[:, s % 2, 0]).then_inc(xs_lo, 1)

            def projected(b, c2, s, first, last):
                n = b * NCH + c2 * 2 + s
                px = bass.ds(c2 * (2 * CHUNK) + s * CHUNK, CHUNK)
                for a, dst, bb, r in ((0, q_st, BQ, 64), (1, k_st, BK, 32)):
                    if a == 1 and not first:
                        first_maxima(b, c2, s, 0)
                    dve.wait_ge(qk_hi, n * 2 + (a + 1))
                    dve.scalar_tensor_tensor(dst[r:r + 32, px], ps[r:r + 32, 4 * s + a, :],
                                             cst[r:r + 32, K_BIAS + bb:K_BIAS + bb + 1],
                                             f(dst[r:r + 32, px]), ALU.add, ALU.subtract).then_inc(qk_lo, 1)
                for qt in range(1, QT):
                    if not first:
                        first_maxima(b, c2, s, qt)
                    if qt == 1 and not last:
                        x_split(b, c2, s + 1)
                for v in range(2):
                    dve.wait_ge(v_hi, n * 2 + (v + 1))
                    t_ = bass.ds(c2 * 8 + (s * 4 + v * 2), 2)
                    sub(vlo_t[:, t_, :], ps[:, 2 + v, :].rearrange("p (t c) -> p t c", c=C),
                        vhi_t[:, t_, 0:C]).then_inc(v_lo, 1)

            def minus_maxima(m):
                dve.wait_ge(m_free, m + 2)
                dve.tensor_reduce(maxcol[:, 96:96 + 32 * (QT - 1) + 1:32], mx_t, AX.X, ALU.max, negate=True).then_inc(negmax, 1)

            def maxima_rows(group, m):
                for h in range(2):
                    dve.wait_ge(m_ready, m + h + 1)
                    dve.tensor_copy(q_st[96:128, bass.ds(group * CHUNK + h * 256, 256)], ps[96:128, 6 + h, 0:256]).then_inc(m_free, 1)

            def attend(b, g, last_group):
                n = b * NCH + g
                m0 = b * M_PER_IMAGE + (NT + 2) + g * M_PER_GROUP
                i = 0
                for t in range(1, NT):
                    if not last_group:
                        for _ in range(MAX_AT[t]):
                            maxima(i, m0 + i)
                            i += 1
                        if t == MAX_TILES + 2:
                            minus_maxima(m0 + NT)
                        if t == MAX_TILES + 4:
                            maxima_rows(g + 1, m0 + NT)
                    if t + 2 < NT:
                        low(t + 2, n * NT)
                    elif t + 2 == NT and not last_group:
                        low(0, (n + 1) * NT)
                for qt in range(QT):
                    if qt == 2 and not last_group:
                        low(1, (n + 1) * NT)
                    dve.wait_ge(o_done, n * QT + qt + 1)
                    dve.reciprocal(rden[:, qt:qt + 1], ps[:, qt, C:C + 1]).then_inc(rden_in, 1)
                    dve.wait_ge(rden_in, n * QT + qt + 1)
                    dve.tensor_scalar(onorm[:, qt, :], ps[:, qt, 0:C], rden[:, qt:qt + 1], None, ALU.mult).then_inc(o_norm, 1)
                if not last_group:
                    low(2, (n + 1) * NT)
                m1 = m0 + (0 if last_group else NT + 2)
                px = bass.ds(g * CHUNK, CHUNK)
                for c in range(CT):
                    dve.wait_ge(m_ready, m1 + c + 1)
                    dve.scalar_tensor_tensor(img[:, c, px], ps[:, 6 + c, :], bias(BV + c), img[:, c, px],
                                             ALU.add, ALU.add).then_inc(m_free, 1)

            def t_split(hi, lo, bank, ready):
                dve.wait_ge(t_h, ready)
                sub(lo, ps[:, bank, :], hi).then_inc(t_l, 1)

            heads = lambda z: z.rearrange("p (a c) -> p a c", c=P // 8)

            def k_squares(buf, n):
                dve.wait_ge(k_sq, n + 1)
                dve.tensor_reduce(knorm[:, 0:32], heads(buf), AX.X, ALU.add).then_inc(k_sum, 1)

            def k_unit_split(buf, n, bank, hi, lo, ready):
                dve.wait_ge(k_root, n + 1)
                dve.tensor_scalar(knorm[:, 32:64], knorm[:, 32:64], NORM_FLOOR, None, ALU.max).then_inc(k_inv, 1)
                dve.wait_ge(k_inv, n * 2 + 1)
                dve.reciprocal(knorm[:, 32:64], knorm[:, 32:64]).then_inc(k_inv, 1)
                dve.wait_ge(k_inv, n * 2 + 2)
                dve.tensor_tensor(heads(buf), heads(ps[:, bank, :]),
                                  knorm[:, 32:64].unsqueeze(2).to_broadcast([P, 32, P // 8]), ALU.mult).then_inc(k_unit, 1)
                dve.wait_ge(t_h, ready)
                sub(lo, buf, hi).then_inc(t_l, 1)

            def gram_add(b, c):
                dve.wait_ge(g_ps, b * 9 + c + 1)
                dve.wait_ge(g_sum, b * 8 + c + 1)
                dve.tensor_tensor(gram[:, :], gram[:, :], ps[:, 5, 0:P], ALU.add).then_inc(g_sum, 1)

            def sp_split(step, dst, hi, src, b):
                dve.wait_ge(sp_hi, b * 6 + step)
                last = None
                for d, h_, s_ in zip(dst, hi, src):
                    last = sub(d, s_, h_)
                last.then_inc(sp_lo, 1)

            def chain(b, s, step):
                d = (2 * b + s) * 8
                a = (2 * b + s) * 2
                nch = NCH if s == 0 else HCH
                if step == 0:
                    dve.wait_ge(sq_done, b * 10 + (9 if s == 0 else 11))
                    dve.tensor_reduce(stat[:, 0:1], norms[:, s * NCH:s * NCH + nch], AX.X, ALU.add).then_inc(a_dve, 1)
                elif step == 1:
                    dve.wait_ge(a_act, a + 1)
                    dve.tensor_scalar(stat[:, 2:3], stat[:, 2:3], NORM_FLOOR, None, ALU.max).then_inc(a_dve, 1)
                    dve.wait_ge(a_dve, d + 2)
                    dve.reciprocal(stat[:, 2:3], stat[:, 2:3]).then_inc(a_dve, 1)
                    dve.wait_ge(a_dve, d + 3)
                    dve.tensor_tensor(stat[:, 2:3], stat[:, 2:3], bias(TEMP), ALU.mult).then_inc(a_dve, 1)
                elif step == 2:
                    dve.wait_ge(a_dve, d + 4)
                    if s == 0:
                        dve.wait_ge(g_sum, b * 8 + 9)
                    else:
                        dve.wait_ge(g_ps, b * 9 + 9)
                    dve.scalar_tensor_tensor(attn[:, :], gram[:, :] if s == 0 else ps[:, 5, 0:P], stat[:, 2:3], cst[:, K_NEG:K_NEG + P],
                                             ALU.mult, ALU.add).then_inc(a_dve, 1)
                    dve.wait_ge(a_dve, d + 5)
                    dve.tensor_reduce(stat[:, 4:5], attn[:, :], AX.X, ALU.max, negate=True).then_inc(a_dve, 1)
                elif step == 3:
                    dve.wait_ge(a_act, a + 2)
                    dve.reciprocal(stat[:, 6:7], stat[:, 5:6]).then_inc(a_dve, 1)
                    dve.wait_ge(a_dve, d + 7)
                    dve.tensor_scalar(attn[:, :], attn[:, :], stat[:, 6:7], None, ALU.mult).then_inc(a_dve, 1)
                else:
                    dve.wait_ge(f_hi, 2 * b + s + 1)
                    sub(fold[s][1], ps[:, 5, 2 * P:2 * P + C], fold[s][0]).then_inc(f_lo, 1)

            wide_e, wide_o = wide[:, :, 0:W:2], wide[:, :, 1:W:2]
            up_e, up_o = up[:, 0:H:2, :], up[:, 1:H:2, :]
            K = WH - 1
            even, odd = (cst[:, K_UP + i * K:K_UP + (i + 1) * K] for i in range(2))
            d_x = up_room[:, 0:HH * K].rearrange("p (y x) -> p y x", x=K)
            d_y = up_room[:, 0:K * W].rearrange("p (y x) -> p y x", x=W)
            row = lambda w_: w_.unsqueeze(1).to_broadcast([P, HH, K])
            col = lambda w_: w_.unsqueeze(2).to_broadcast([P, K, W])

            def up_step(b, i):
                dve.wait_ge(up_d, b * UP_STEPS + i + 1)
                if i == 0:
                    dve.wait_ge(cv_out, b * 28 + 26)
                if i == 0:
                    ins = dve.tensor_tensor(d_x, v_hw[:, :, 0:K], v_hw[:, :, 1:WH], ALU.subtract)
                elif i == 1:
                    ins = dve.tensor_tensor(wide_e[:, :, 1:WH], d_x, row(even), ALU.mult)
                elif i == 2:
                    ins = dve.tensor_tensor(wide_e[:, :, 1:WH], wide_e[:, :, 1:WH], v_hw[:, :, 1:WH], ALU.add)
                elif i == 3:
                    ins = dve.tensor_tensor(wide_o[:, :, 0:K], d_x, row(odd), ALU.mult)
                elif i == 4:
                    ins = dve.tensor_tensor(wide_o[:, :, 0:K], wide_o[:, :, 0:K], v_hw[:, :, 0:K], ALU.add)
                elif i == 5:
                    ins = dve.tensor_copy(wide[:, :, 0:W:W - 1], v_hw[:, :, 0:WH:WH - 1])
                elif i == 6:
                    ins = dve.tensor_tensor(d_y, wide[:, 0:K, :], wide[:, 1:HH, :], ALU.subtract)
                elif i == 7:
                    ins = dve.tensor_tensor(up_e[:, 1:HH, :], d_y, col(even), ALU.mult)
                elif i == 8:
                    ins = dve.tensor_tensor(up_e[:, 1:HH, :], up_e[:, 1:HH, :], wide[:, 1:HH, :], ALU.add)
                elif i == 9:
                    ins = dve.tensor_tensor(up_o[:, 0:K, :], d_y, col(odd), ALU.mult)
                elif i == 10:
                    ins = dve.tensor_tensor(up_o[:, 0:K, :], up_o[:, 0:K, :], wide[:, 0:K, :], ALU.add)
                else:
                    ins = dve.tensor_copy(up[:, 0:H:H - 1, :], wide[:, 0:HH:HH - 1, :])
                ins.then_inc(up_d, 1)

            for _ in range(2):
                dve.sem_inc(p_lo, 1)
                dve.sem_inc(m_free, 1)
                dve.sem_inc(v_lo, 1)
            for _ in range(QT):
                dve.sem_inc(o_norm, 1)
            for s_ in (vl_l, g_sum, f_lo, up_d):
                dve.sem_inc(s_, 1)
            dve.wait_ge(c_in, 16)
            dve.tensor_scalar(bscaled[:, :], cst[:, K_BIAS + BL:K_BIAS + BL + 5], BNS, None, ALU.mult).then_inc(prep, 1)
            dve.memset(maxcol[:, :], 0.0).then_inc(prep, 1)
            dve.wait_ge(w_hi, 1)
            sub(wlo[:, :], image[:, 0:NW], whi[:, :]).then_inc(w_lo, 1)
            with dve.Fori(0, B) as b:
                x_split(b, 0, 0)
                for s in range(2):
                    projected(b, 0, s, s == 0, False)
                with dve.Fori(1, NCH // 2 - 1) as c2:
                    for s in range(2):
                        projected(b, c2, s, False, False)
                for s in range(2):
                    projected(b, NCH // 2 - 1, s, False, s == 1)
                m = b * M_PER_IMAGE
                for qt in range(QT):
                    first_maxima(b, NCH // 2, 0, qt)
                minus_maxima(m + NT)
                maxima_rows(0, m + NT)
                for t in range(3):
                    low(t, b * (NCH * NT))
                with dve.Fori(0, NCH - 1) as g:
                    attend(b, g, False)
                attend(b, NCH - 1, True)
                dve.wait_ge(g_sum, b * 8 + 1)
                dve.memset(gram[:, :], 0.0)
                for r in range(8):
                    pad(0, r, b)
                for s in range(4):
                    dve.wait_ge(out_dma[s], b * 64 + 16)
                dve.wait_ge(m_free, b * M_PER_IMAGE + M_PER_IMAGE + 2)
                dve.tensor_reduce(stage[:, 1024:2048].rearrange("p (y x) -> p y x", x=WH),
                                  img[:, 1, :].rearrange("p (y a x b) -> p y x a b", y=HH, a=2, b=2), AX.XY, ALU.add).then_inc(pool_f, 1)

                def low_chunk(c, last):
                    k_squares(scr[:, CHUNK:2 * CHUNK], b * 10 + c)
                    k_unit_split(scr[:, CHUNK:2 * CHUNK], b * 10 + c, 4, t_hi[1], t_lo[1], b * 20 + c * 2 + 1)
                    if last:
                        for r in range(6):
                            pad(1, r, b)
                    t_split(t_hi[0], t_lo[0], 3, b * 20 + c * 2 + 2)
                    px = bass.ds(c * CHUNK, CHUNK)
                    dve.wait_ge(vl_h, b * 8 + c + 1)
                    sub(vl_lo[:, px], scr[:, 2 * CHUNK:3 * CHUNK], vl_hi[:, px]).then_inc(vl_l, 1)
                    gram_add(b, c)

                low_chunk(0, False)
                dve.wait_ge(pool_hi, b + 1)
                sub(ring[:, 1024:2048], stage[:, 1024:2048], ring[:, 0:1024]).then_inc(pool_lo, 1)
                dve.wait_ge(d_hi, b + 1)
                sub(dlo, image[:, 0:ND], dhi).then_inc(d_lo, 1)
                with dve.Fori(1, NCH - 1) as c:
                    low_chunk(c, False)
                low_chunk(NCH - 1, True)
                for r in range(6, 8):
                    pad(1, r, b)
                lo8, hi8 = ring[:, 1280:2304], ring[:, 0:1024]
                chain(b, 0, 0)
                sp_split(1, [lo8], [hi8], [ps[:, 2:4, :].rearrange("p a n -> p (a n)")], b)
                chain(b, 0, 1)
                chain(b, 0, 2)
                sp_split(2, [lo8], [hi8], [ps[:, 2:4, :].rearrange("p a n -> p (a n)")], b)
                chain(b, 0, 3)
                d_, s_ = freq(ring[:, 2848:3392])
                h_, _ = freq(ring[:, 2304:2848])
                sp_split(3, d_, h_, s_, b)
                chain(b, 0, 4)
                for i in range(0, 4):
                    up_step(b, i)
                d_, s_ = ky_tiles(ring[:, 1280:2560])
                h_, _ = ky_tiles(ring[:, 0:1280])
                sp_split(4, d_, h_, s_, b)
                for i in range(4, 8):
                    up_step(b, i)
                k_squares(scr[:, 0:CHUNK], b * 10 + 8)
                sp_split(5, [lo8[:, 0:512], lo8[:, 512:1024]], [hi8[:, 0:512], hi8[:, 512:1024]], [ps[:, 2, :], ps[:, 4, :]], b)
                k_unit_split(scr[:, 0:CHUNK], b * 10 + 8, 6, *kt_h[0], b * 20 + 17)
                dve.wait_ge(sp_ps, b * 10 + 10)
                dve.tensor_tensor(stage[:, 1024:2048], ps[:, 0:2, :].rearrange("p a n -> p (a n)"), scr[:, 1024:2048], ALU.add).then_inc(sp_z, 1)
                dve.wait_ge(sp_hi, b * 6 + 6)
                sub(ring[:, 1024:2048], stage[:, 1024:2048], hi8).then_inc(sp_lo, 1)
                k_squares(scr[:, CHUNK:2 * CHUNK], b * 10 + 9)
                k_unit_split(scr[:, CHUNK:2 * CHUNK], b * 10 + 9, 7, *kt_h[1], b * 20 + 18)
                for h in range(HCH):
                    dve.wait_ge(t_h, b * 20 + 19 + h)
                    dve.scalar_tensor_tensor(qt_h[h][1], ps[:, 2 + h, :], BNS, f(qt_h[h][0]),
                                             ALU.mult, ALU.subtract).then_inc(t_l, 1)
                for i in range(8, 12):
                    up_step(b, i)
                for step in range(4):
                    chain(b, 1, step)
                for i in range(4):
                    if i == 1:
                        chain(b, 1, 4)
                    dve.wait_ge(up_h, b * 4 + i + 1)
                    sub(up_lo[:, i * 1024:(i + 1) * 1024], image[:, i * 1024:(i + 1) * 1024],
                        up_hi[:, i * 1024:(i + 1) * 1024]).then_inc(up_l, 1)

        @block.gpsimd
        def _(pool):
            def x_hi(b, c2, s):
                pool.wait_ge(x_in[s], b * (16 * NCH // 2) + c2 * 16 + 32)
                pool.wait_ge(v_ps, (b * NCH + c2 * 2 + s) * 2 + 2)
                apart(pool)
                pool.tensor_copy(xs[:, s, 0], img[:, :, bass.ds(c2 * (2 * CHUNK) + s * CHUNK, CHUNK)]).then_inc(xs_hi, 1)

            with pool.Fori(0, B) as b:
                pool.wait_ge(f_lo, b * 2 + 1)
                apart(pool)
                for s in range(2):
                    x_hi(b, 0, s)
                pool.wait_ge(qk_lo, b * (2 * NCH) + 2)
                apart(pool)
                pool.tensor_copy(qmax[0:96, :], f(q_st)[0:96, 0:CHUNK]).then_inc(qmax_in, 1)
                with pool.Fori(1, NCH // 2) as c2:
                    for s in range(2):
                        x_hi(b, c2, s)
                pool.wait_ge(xs_hi, b * NCH + NCH)
                apart(pool)
                pool.memset(f(k_st[96:128, :]), 1.0).then_inc(ones_set, 1)
                pool.wait_ge(ones_set, b * 2 + 1)
                apart(pool)
                pool.memset(f(vhi_t[:, :, C:VC]), 1.0).then_inc(ones_set, 1)
                with pool.Fori(1, NCH) as g:
                    pool.wait_ge(m_ready, b * M_PER_IMAGE + g * M_PER_GROUP + (NT - M_PER_GROUP))
                    apart(pool)
                    pool.tensor_copy(qmax[0:96, :], f(q_st)[0:96, bass.ds(g * CHUNK, CHUNK)]).then_inc(qmax_in, 1)
                pool.wait_ge(o_done, b * (NCH * QT) + NCH * QT)
                apart(pool)
                for z in (vhi, vlo):
                    pool.memset(f(z[:, 0:WP - 1]), 0.0).then_inc(border, 1)
                    pool.memset(f(z[:, WP - 1:WP - 1 + (HP - 1) * WP].rearrange("p (h w) -> p h w", w=WP)[:, :, 0:2]), 0.0).then_inc(border, 1)
                    pool.memset(f(z[:, (HP - 1) * WP + 1:HP * WP]), 0.0).then_inc(border, 1)
                pool.wait_ge(pool_f, b + 1)
                apart(pool)
                pool.tensor_copy(ring[:, 0:1024], stage[:, 1024:2048]).then_inc(pool_hi, 1)
                pool.wait_ge(d_in, b * 16 + 16)
                apart(pool)
                pool.tensor_copy(dhi, image[:, 0:ND]).then_inc(d_hi, 1)
                with pool.Fori(0, NCH) as c:
                    pool.wait_ge(cv_out, b * 28 + c * 3 + 3)
                    apart(pool)
                    pool.tensor_copy(vl_hi[:, bass.ds(c * CHUNK, CHUNK)], scr[:, 2 * CHUNK:3 * CHUNK]).then_inc(vl_h, 1)


def transforms():
    n = WH
    i = np.arange(n)
    s = 1 / np.sqrt(n)
    th = 2 * np.pi * np.outer(i, i) / n
    fx, ox = np.zeros((n, n)), np.zeros((n, n))
    fx[:, 0], fx[:, 1] = s, s * np.cos(np.pi * i)
    ox[0], ox[1] = s, s * np.cos(np.pi * i)
    for k in range(1, n // 2):
        fx[:, 2 * k], fx[:, 2 * k + 1] = s * np.cos(th[:, k]), -s * np.sin(th[:, k])
        ox[2 * k], ox[2 * k + 1] = 2 * s * np.cos(th[k]), -2 * s * np.sin(th[k])
    d_x, d_out = np.kron(np.eye(4), fx), np.kron(np.eye(4), ox)
    co, si = s * np.cos(th), s * np.sin(th)
    d_y = np.kron(np.eye(2), np.block([[co, -si], [si, co]]))
    real = np.concatenate([co, -si], 1)
    d_y0 = np.zeros((P, P))
    d_y0[0:32, 0:64] = real
    d_y0[64:128, 64:128] = d_y[0:64, 0:64]
    d_y16 = np.zeros((P, 64))
    d_y16[32:64] = real
    d_re = np.kron(np.eye(4), np.concatenate([co, si], 1))
    d_im = np.kron(np.eye(4), np.concatenate([-si, co], 1))
    return np.concatenate([d_x, d_y0, d_y, d_y16, d_re, d_im, d_out], 1).astype(np.float32)


def upsample_tables():
    k = np.arange(1, WH)
    e = 1 - (2 * k * (WH - 1) / (W - 1) - (k - 1))
    k = np.arange(WH - 1)
    o = (2 * k + 1) * (WH - 1) / (W - 1) - k
    return np.concatenate([e, -o]).astype(np.float32)


def kernel(**inputs):
    import concourse.bacc as bacc
    from concourse.bass_utils import run_bass_kernel_spmd

    a = {k: np.asarray(v) for k, v in inputs.items()}
    l1 = lambda n: a["L1_conv_" + n]

    def tiles(w):
        return w.reshape(-1, P, w.shape[1]).transpose(1, 0, 2).reshape(P, -1)

    def taps(w):
        return w.transpose(1, 2, 3, 0).reshape(P, -1)

    fu = l1("w_stfu")[:, :, 0, 0].reshape(64, 2, 64, 2).transpose(1, 0, 3, 2)
    fu = [fu[r].reshape(64, P).T for r in range(2)]
    st2 = np.zeros((P, P), np.float32)
    st2[0:64] = l1("w_st2")[:, :, 0, 0].T
    weights = np.concatenate(
        [tiles(np.tile(a["L0_conv_wq"].T, (1, 4))), tiles(np.tile(a["L0_conv_wk"].T, (1, 4))), tiles(a["L0_conv_wv"].T)]
        + [taps(l1(n)) for n in ("wq", "wk", "wv")]
        + [np.tile(l1("w_st1")[:, :, 0, 0].T, (1, 2))] + [np.tile(z, (1, 2)) for z in fu] + [st2], 1)
    weights2 = np.concatenate([taps(l1("wk2")), taps(l1("wv2")), transforms()], 1)
    head = np.arange(P) // (P // 8)
    other = np.where(head[:, None] == head[None, :], 0, -1e30).astype(np.float32)
    wo = l1("w_out")[:, :, 0, 0].T
    cols = [np.tile(a["L0_conv_bq"], 4), np.tile(a["L0_conv_bk"], 4), a["L0_conv_bv"][0:P], a["L0_conv_bv"][P:],
            l1("bq"), l1("bk"), l1("bv"), l1("bk2"), l1("bv2"), l1("b_out")[0:P], l1("b_out")[P:],
            np.repeat(l1("temperature").reshape(-1), P // 8)]
    consts = np.concatenate([tiles(wo), np.eye(P, dtype=np.float32), other,
                             np.tile(upsample_tables()[None], (P, 1)), np.stack(cols, 1)], 1)
    arrays = {"x": a["x"].reshape(B * CT, P, N), "weights": weights, "weights2": weights2, "consts": consts}
    arrays = {k: np.ascontiguousarray(v) for k, v in arrays.items()}
    assert weights.shape == (P, NW) and weights2.shape == (P, ND) and consts.shape == (P, NK)
    nc = bacc.Bacc("TRN2", target_bir_lowering=False, num_devices=1)
    args = [nc.dram_tensor(k, v.shape, mybir.dt.from_np(v.dtype), kind="ExternalInput").ap() for k, v in arrays.items()]
    args.append(nc.dram_tensor("out", (B * CT, P, N), F32, kind="ExternalOutput").ap())
    build(nc, *args)
    r = run_bass_kernel_spmd(nc, [arrays], core_ids=[0])
    return r.results[0]["out"].reshape(B, C, H, W)
```

```python
from contextlib import ExitStack

import concourse.bass as bass
import numpy as np
from concourse import mybir

ALU = mybir.AluOpType
ACT = mybir.ActivationFunctionType
F32 = mybir.dt.float32
F32R = mybir.dt.float32r
AX = mybir.AxisListType

P = 128
B, C, H, W = 4, 256, 64, 64
N = H * W
CT = C // P
CHUNK = 512
NCH = N // CHUNK
NT = N // P
QT = CHUNK // P
VC = C + 2
HP, WP = H + 2, W + 2
HH, WH = H // 2, W // 2
NHALF = HH * WH
HCH = NHALF // CHUNK
BNS = float(np.float32(1.0 / np.sqrt(1.0 + 1e-05)))
NORM_FLOOR = 1e-12

W_QK, W_V = 0, CT * P
W_L = W_V + CT * C
W_ST1 = W_L + 3 * 9 * P
W_FU = W_ST1 + P
W_ST2 = W_FU + 2 * P
NW = W_ST2 + P
D_X = 2 * 9 * P
D_Y0, D_Y, D_Y16 = D_X + P, D_X + 2 * P, D_X + 3 * P
D_RE = D_Y16 + 64
D_IM = D_RE + 2 * P
D_OUT = D_IM + 2 * P
ND = D_OUT + P
NREST = (NW - W_L) // 2
K_WO, K_ID, K_NEG, K_UP = 0, 2 * C, 2 * C + P, 2 * C + 2 * P
K_BIAS = K_UP + 2 * (WH - 1)
BQK, BV, BL, BH, BO, TEMP = 0, 1, 3, 6, 8, 10
NK = K_BIAS + 11

M_PER_GROUP = NT + 2 + 2
M_PER_IMAGE = (NT + 2) + (NCH - 1) * M_PER_GROUP + 2
MAX_TILES = 24
MAX_AT = [(t - 1) * NT // MAX_TILES - (t - 2) * NT // MAX_TILES if 1 < t <= MAX_TILES + 1 else 0 for t in range(NT)]


def build(nc, x, weights, weights2, consts, out):
    ctx = ExitStack()
    with ctx:
        def sb(name, cols, dt=F32):
            return ctx.enter_context(nc.sbuf_tensor(name, [P, cols], dt))

        def sem(name):
            return ctx.enter_context(nc.semaphore(name))

        image = sb("image", CT * N)
        qk = sb("qk", 2 * N, F32R)
        vhi = sb("vhi", NT * VC, F32R)
        vlo = sb("vlo", NT * C, F32R)
        ring = sb("ring", 4 * 2 * CHUNK, F32R)
        whi = sb("whi", NW, F32R)
        wlo = sb("wlo", NW, F32R)
        cst = sb("cst", NK)
        scr = sb("scr", 4 * CHUNK)
        stage = sb("stage", 4 * CHUNK)
        qmax = sb("qmax", CHUNK, F32R)
        maxcol = sb("maxcol", P + 32 * (QT - 1))
        mx = sb("mx", QT * NCH)
        rden = sb("rden", QT)
        bscaled = sb("bscaled", 5)
        gram = sb("gram", P)
        norms = sb("norms", 2 * NCH)
        knorm = sb("knorm", 2 * QT * 8)
        attn = sb("attn", P)
        stat = sb("stat", 8)
        ps = ctx.enter_context(nc.psum_tensor("ps", [P, 8, CHUNK], F32))

        img = image[:, :].rearrange("p (c n) -> p c n", c=CT)
        q_st, k_st = qk[:, 0:N], qk[:, N:2 * N]
        vhi_t = vhi[:, :].rearrange("p (t c) -> p t c", c=VC)
        vlo_t = vlo[:, :].rearrange("p (t c) -> p t c", c=C)
        prob = ring[:, :].rearrange("p (s a n) -> p s a n", s=4, a=2)
        xs = ring[:, :].rearrange("p (s a c n) -> p s a c n", s=2, a=2, c=CT)
        onorm = scr[:, 0:QT * C].rearrange("p (t c) -> p t c", c=C)
        mx_t = mx[:, :].rearrange("p (t c) -> p t c", c=NCH)
        ident = cst[:, K_ID:K_ID + P]
        bias = lambda i: cst[:, K_BIAS + i:K_BIAS + i + 1]
        pad_hi = vhi[:, 0:HP * WP].rearrange("p (h w) -> p h w", w=WP)
        pad_lo = vlo[:, 0:HP * WP].rearrange("p (h w) -> p h w", w=WP)
        D0 = 4400
        D1 = D0 + ND
        dhi, dlo = vhi[:, D0:D0 + ND], vlo[:, D0:D0 + ND]
        fold = {0: (vhi[:, D1:D1 + C], vlo[:, D1:D1 + C]), 1: (vhi[:, D0:D0 + C], vlo[:, D0:D0 + C])}
        up_hi, up_lo = vhi[:, 0:N], vlo[:, 0:N]
        vl_hi, vl_lo = qk[:, 0:N], qk[:, N:2 * N]
        t_hi = {a: ring[:, 2048 + 1024 * a:2560 + 1024 * a] for a in (0, 1)}
        t_lo = {a: ring[:, 2560 + 1024 * a:3072 + 1024 * a] for a in (0, 1)}
        kt_h = [(ring[:, 2560:3072], ring[:, 3072:3584]), (ring[:, 3584:4096], qmax[:, :])]
        qt_h = [tuple(z[:, D0 + C + h * CHUNK:D0 + C + (h + 1) * CHUNK] for z in (vhi, vlo)) for h in range(HCH)]
        OUT_BANKS = (0, 1, 6, 7)

        w_in, c_in, w_hi, w_lo, prep = (sem(n) for n in ("w_in", "c_in", "w_hi", "w_lo", "prep"))
        w_rest_in, w_rest = sem("w_rest_in"), sem("w_rest")
        x_in = [sem(f"x_in{i}") for i in range(2)]
        xs_hi_e, xs_lo_e, xs_hi, xs_lo = (sem(n) for n in ("xs_hi_e", "xs_lo_e", "xs_hi", "xs_lo"))
        qk_ps, qk_hi, qk_lo, v_ps, v_hi, v_lo = (sem(n) for n in ("qk_ps", "qk_hi", "qk_lo", "v_ps", "v_hi", "v_lo"))
        ones_set, qmax_in, m_ready, m_free, negmax = (sem(n) for n in ("ones_set", "qmax_in", "m_ready", "m_free", "negmax"))
        s_ready, p_used, p_full, p_lo = (sem(n) for n in ("s_ready", "p_used", "p_full", "p_lo"))
        o_done, rden_in, o_norm, o_norm3 = (sem(n) for n in ("o_done", "rden_in", "o_norm", "o_norm3"))
        border, pad_h, pad_l, d_in, d_hi, d_lo = (sem(n) for n in ("border", "pad_h", "pad_l", "d_in", "d_hi", "d_lo"))
        pool_f, pool_hi, pool_lo = (sem(n) for n in ("pool_f", "pool_hi", "pool_lo"))
        cv_ps, cv_out, sq_done, vl_h, vl_l = (sem(n) for n in ("cv_ps", "cv_out", "sq_done", "vl_h", "vl_l"))
        t_ps, t_h, t_l, g_ps, g_sum = (sem(n) for n in ("t_ps", "t_h", "t_l", "g_ps", "g_sum"))
        sp_ps, sp_f, sp_hi, sp_lo, sp_z = (sem(n) for n in ("sp_ps", "sp_f", "sp_hi", "sp_lo", "sp_z"))
        up_d, up_rest, up_h, up_l = sem("up_d"), sem("up_rest"), sem("up_h"), sem("up_l")
        a_dve, a_act = sem("a_dve"), sem("a_act")
        k_sq, k_sum, k_root, k_inv, k_unit = (sem(n) for n in ("k_sq", "k_sum", "k_root", "k_inv", "k_unit"))
        f_ps, f_hi, f_lo = sem("f_ps"), sem("f_hi"), sem("f_lo")
        r_ps, r_out = sem("r_ps"), sem("r_out")
        out_dma = [sem(f"out_dma{i}") for i in range(4)]

        UP_STEPS = 9
        wide = image[:, N:N + 2 * NHALF].rearrange("p (y x) -> p y x", x=W)
        v_h = image[:, N + 3 * NHALF:N + 4 * NHALF]
        v_hw = v_h.rearrange("p (y x) -> p y x", x=WH)
        up_room = image[:, N + 2 * NHALF:N + 4 * NHALF]
        up = image[:, 0:N].rearrange("p (y x) -> p y x", x=W)

        wide_e, wide_o = wide[:, :, 0:W:2], wide[:, :, 1:W:2]
        up_e, up_o = up[:, 0:H:2, :], up[:, 1:H:2, :]
        K = WH - 1
        even, odd = (cst[:, K_UP + i * K:K_UP + (i + 1) * K] for i in range(2))
        d_x = up_room[:, 0:HH * K].rearrange("p (y x) -> p y x", x=K)
        d_y = up_room[:, 0:K * W].rearrange("p (y x) -> p y x", x=W)
        row = lambda w_: w_.unsqueeze(1).to_broadcast([P, HH, K])
        col = lambda w_: w_.unsqueeze(2).to_broadcast([P, K, W])

        f = lambda ap: ap.bitcast(F32)

        passed = sem("passed")

        def apart(eng):
            eng.sem_inc(passed, 1)

        block = ctx.enter_context(nc.Block())

        def freq(dst):
            d, s = [], []
            for bank, k0, n in ((0, 0, 8), (1, 8, 8), (2, 16, 1)):
                v = ps[:, bank, 0:n * 64].rearrange("p (k r y) -> p k r y", r=2, y=HH)
                for r in range(2):
                    d.append(dst[64 * r:64 * (r + 1), k0 * 32:(k0 + n) * 32].rearrange("p (k y) -> p k y", y=HH))
                    s.append(v[64 * r:64 * (r + 1), :, r, :])
            return d, s

        def ky_tiles(dst):
            return ([dst[:, 0:512], dst[:, 512:1024], dst[0:32, 1024:1280]],
                    [ps[:, 2, :], ps[:, 3, :], ps[0:32, 4, 0:256]])

        @block.sync
        def _(sp):
            sp.dma_start(stage[:, 0:W_L], weights[:, 0:W_L]).then_inc(w_in, 16)
            for s in range(2):
                sp.sem_inc(x_in[s], 16)
            for s in range(4):
                sp.sem_inc(out_dma[s], 16)
            def load(b, c2):
                for s in range(2):
                    sp.wait_ge(x_in[s], b * (16 * NCH // 2) + c2 * 16 + 16)
                    sp.dma_start(
                        img[:, :, bass.ds(c2 * (2 * CHUNK) + s * CHUNK, CHUNK)],
                        x[bass.ds(b * CT, CT), :, bass.ds(c2 * (2 * CHUNK) + s * CHUNK, CHUNK)]
                        .rearrange("c p n -> p c n")).then_inc(x_in[s], 16)

            def load_weights2(b):
                sp.wait_ge(pad_l, b * 16 + 8)
                sp.dma_start(image[:, 0:ND], weights2).then_inc(d_in, 16)

            def store(b, c2):
                for s in range(4):
                    sp.wait_ge(r_out, b * 16 + c2 * 4 + (4 + s + 1))
                    sp.dma_start(
                        out[bass.ds(b * CT + s % 2, 1), :, bass.ds(c2 * (2 * CHUNK) + (s // 2) * CHUNK, CHUNK)]
                        .rearrange("c p n -> p (c n)"),
                        stage[:, s * CHUNK:(s + 1) * CHUNK]).then_inc(out_dma[s], 16)

            load(0, 0)
            sp.dma_start(cst[:, :], consts).then_inc(c_in, 16)
            with sp.Fori(1, NCH // 2) as c2:
                load(0, c2)
            sp.wait_ge(w_lo, 1)
            sp.dma_start(stage[:, 0:NREST], weights[:, W_L:W_L + NREST]).then_inc(w_rest_in, 16)
            sp.wait_ge(w_rest, 2)
            sp.dma_start(stage[:, 0:NREST], weights[:, W_L + NREST:NW]).then_inc(w_rest_in, 16)
            with sp.Fori(0, B - 1) as b:
                load_weights2(b)
                with sp.Fori(0, NCH // 2) as c2:
                    store(b, c2)
                    load(b + 1, c2)
            load_weights2(B - 1)
            with sp.Fori(0, NCH // 2) as c2:
                store(B - 1, c2)
            for s in range(4):
                sp.wait_ge(out_dma[s], 16 + 16 * B * NCH // 2)

        @block.tensor
        def _(pe):
            def three(o, w_hi_ap, w_lo_ap, x_hi_ap, x_lo_ap, start, stop):
                pe.matmul(o, w_hi_ap, x_hi_ap, start=start, stop=False)
                pe.matmul(o, w_hi_ap, x_lo_ap, start=False, stop=False)
                return pe.matmul(o, w_lo_ap, x_hi_ap, start=False, stop=stop)

            def transposes(o, src, n):
                for i in range(n):
                    last = pe.transpose(o[:, i * P:(i + 1) * P], src[:, i * P:(i + 1) * P], ident)
                return last

            def scores(group, t, n0):
                pe.wait_ge(p_lo, n0 + t + 1)
                pe.matmul(ps[:, 4 + t % 2, :], k_st[:, t * P:(t + 1) * P],
                          q_st[:, bass.ds(group * CHUNK, CHUNK)], start=True, stop=True).then_inc(s_ready, 1)

            def maxima(i, m):
                qt, jc = i // NCH, i % NCH
                pe.wait_ge(m_free, m + 1)
                pe.matmul(ps[:, 6 + i % 2, :], qmax[0:96, qt * P:(qt + 1) * P],
                          k_st[0:96, jc * CHUNK:(jc + 1) * CHUNK], start=True, stop=True).then_inc(m_ready, 1)

            def first_maxima(b, c2, s, qt):
                pe.wait_ge(m_free, b * M_PER_IMAGE + c2 * (2 * QT) + (s * QT - QT + qt + 1))
                pe.matmul(ps[:, 6 + qt % 2, :], qmax[0:96, qt * P:(qt + 1) * P],
                          k_st[0:96, bass.ds(c2 * (2 * CHUNK) + (s - 1) * CHUNK, CHUNK)],
                          start=True, stop=True).then_inc(m_ready, 1)

            def project(b, c2, s, early):
                n = b * NCH + c2 * 2 + s
                first = early and s == 0
                w = [slice(W_QK + c * P, W_QK + (c + 1) * P) for c in range(CT)]
                if early:
                    pe.wait_ge(xs_lo_e, b * 2 + s + 1)
                else:
                    pe.wait_ge(xs_hi, b * (NCH - 2) + c2 * 2 + (s - 1))
                for c in range(CT):
                    pe.matmul(ps[:, 4 * s, :], whi[:, w[c]], xs[:, s, 0, c, :], start=(c == 0), stop=False)
                    pe.matmul(ps[:, 4 * s, :], wlo[:, w[c]], xs[:, s, 0, c, :], start=False, stop=False)
                if not early:
                    pe.wait_ge(xs_lo, b * (NCH - 2) + c2 * 2 + (s - 1))
                for c in range(CT):
                    last = pe.matmul(ps[:, 4 * s, :], whi[:, w[c]], xs[:, s, 1, c, :], start=False, stop=(c == CT - 1))
                last.then_inc(qk_ps, 1)
                for j in range(QT):
                    if j == (1 if early else 0) and not first:
                        pe.wait_ge(qk_lo, n * 2)
                    if not early:
                        first_maxima(b, c2, s, j)
                    if j % 2 == 0:
                        pe.wait_ge(v_lo, n * 2 + (j // 2 + 1))
                    for c in range(CT):
                        w = slice(W_V + c * C, W_V + (c + 1) * C)
                        last = three(ps[:, 2 + j // 2, (j % 2) * C:(j % 2 + 1) * C],
                                     xs[:, s, 0, c, j * P:(j + 1) * P], xs[:, s, 1, c, j * P:(j + 1) * P],
                                     whi[:, w], wlo[:, w], c == 0, c == CT - 1)
                    if j % 2:
                        last.then_inc(v_ps, 1)
                    if early and not first and j == 1:
                        pe.wait_ge(qmax_in, b * NCH + 1)
                        pe.wait_ge(r_out, b * 16 + 4)
                    if early and not first and j >= 1:
                        for qt in ((0,), (1,), (2, 3))[j - 1]:
                            first_maxima(b, c2, s, qt)

            def maxima_rows(n, m):
                pe.wait_ge(negmax, n + 1)
                for h in range(2):
                    pe.wait_ge(m_free, m + h + 1)
                    for i in range(2):
                        last = pe.transpose(ps[:, 6 + h, i * P:(i + 1) * P], maxcol[:, 32 * (2 * h + i):32 * (2 * h + i) + P], ident)
                    last.then_inc(m_ready, 1)

            def weigh(t, n):
                pe.wait_ge(p_lo, n * NT + t + 3)
                for qt in range(QT):
                    if t == 0:
                        if qt < 3:
                            pe.wait_ge(o_norm, n * 3 + qt + 1)
                        else:
                            pe.wait_ge(o_norm3, n + 1)
                    hi = prob[:, t % 4, 0, qt * P:(qt + 1) * P]
                    lo = prob[:, t % 4, 1, qt * P:(qt + 1) * P]
                    pe.matmul(ps[:, qt, 0:VC], hi, vhi_t[:, t, :], start=(t == 0), stop=False)
                    pe.matmul(ps[:, qt, 0:C], hi, vlo_t[:, t, :], start=False, stop=False)
                    last = pe.matmul(ps[:, qt, 0:VC], lo, vhi_t[:, t, :], start=False, stop=(t == NT - 1))
                    if t == NT - 1:
                        last.then_inc(o_done, 1)
                    elif qt == QT - 1:
                        last.then_inc(p_used, 1)

            def attend(b, g, last_group):
                n = b * NCH + g
                n0 = n * NT
                m0 = b * M_PER_IMAGE + (NT + 2) + g * M_PER_GROUP
                i = 0
                for t in range(1, NT):
                    if not last_group:
                        for _ in range(MAX_AT[t]):
                            if i == 0:
                                pe.wait_ge(qmax_in, n + 2)
                            maxima(i, m0 + i)
                            i += 1
                        if t == MAX_TILES + 4:
                            maxima_rows(n + 1, m0 + NT)
                    if t + 2 < NT:
                        scores(g, t + 2, n0)
                    elif not last_group:
                        if t + 2 == NT:
                            pe.wait_ge(m_free, m0 + NT + 2 + 2)
                        scores(g + 1, t + 2 - NT, n0 + NT)
                    weigh(t, n)
                if not last_group:
                    scores(g + 1, 2, n0 + NT)
                    weigh(0, n + 1)
                m1 = m0 + (0 if last_group else NT + 2)
                for c in range(CT):
                    pe.wait_ge(m_free, m1 + c + 1)
                for qt in range(QT):
                    if qt < 3:
                        pe.wait_ge(o_norm, (n + 1) * 3 + qt + 1)
                    else:
                        pe.wait_ge(o_norm3, n + 2)
                    for c in range(CT):
                        last = pe.transpose(ps[:, 6 + c, qt * P:(qt + 1) * P], onorm[:, qt, c * P:(c + 1) * P], ident)
                        if qt == QT - 1:
                            last.then_inc(m_ready, 1)

            def conv(o, hi, lo, w0, src, taps=range(9), half=False, rows=None, c=None):
                for tap in taps:
                    dy, dx = tap // 3, tap % 3
                    w_h, w_l = hi[:, w0 + tap * P:w0 + (tap + 1) * P], lo[:, w0 + tap * P:w0 + (tap + 1) * P]
                    if half:
                        r0 = 2 * (CHUNK // WH) * c + dy
                        x_h, x_l = (z[:, r0:r0 + 2 * (CHUNK // WH) - 1:2, dx:dx + 2 * WH - 1:2] for z in src)
                    else:
                        x_h, x_l = (z[:, bass.ds(c * (CHUNK // W) + dy, CHUNK // W), dx:dx + W] for z in src)
                    last = three(o, w_h, w_l, x_h, x_l, tap == 0, tap == 8)
                return last

            def gram(hi_lo_q, hi_lo_k, first, last):
                for i in range(QT):
                    s = slice(i * P, (i + 1) * P)
                    m = three(ps[:, 5, 0:P], hi_lo_q[0][:, s], hi_lo_q[1][:, s], hi_lo_k[0][:, s], hi_lo_k[1][:, s],
                              first and i == 0, last and i == QT - 1)
                return m

            def fold_weights(b, s):
                pe.wait_ge(a_dve, (2 * b + s) * 8 + 8)
                pe.matmul(ps[:, 5, 2 * P:2 * P + C], attn[:, :], cst[:, K_WO + (1 - s) * C:K_WO + (2 - s) * C],
                          start=True, stop=True).then_inc(f_ps, 1)

            for _ in range(4):
                pe.sem_inc(v_ps, 1)
                pe.sem_inc(p_used, 1)
            pe.wait_ge(w_lo, 1)
            pe.wait_ge(c_in, 16)
            pe.wait_ge(prep, 1)
            apart(pe)
            with pe.Fori(0, B) as b:
                pe.wait_ge(r_out, b * 16 + 2)
                for s in range(2):
                    project(b, 0, s, True)
                with pe.Fori(1, NCH // 2) as c2:
                    for s in range(2):
                        project(b, c2, s, False)
                pe.wait_ge(qk_lo, b * (2 * NCH) + 2 * NCH)
                for qt in range(QT):
                    first_maxima(b, NCH // 2, 0, qt)
                maxima_rows(b * NCH, b * M_PER_IMAGE + NT)
                pe.wait_ge(ones_set, b * 2 + 2)
                pe.wait_ge(m_free, b * M_PER_IMAGE + NT + 2 + 2)
                for t in range(3):
                    scores(0, t, b * (NCH * NT))
                pe.wait_ge(v_lo, b * (2 * NCH) + 2 * NCH + 2)
                weigh(0, b * NCH)
                with pe.Fori(0, NCH - 1) as g:
                    attend(b, g, False)
                attend(b, NCH - 1, True)
                pe.wait_ge(w_rest, 4)
                pe.wait_ge(border, b * 6 + 6)
                apart(pe)
                with pe.Fori(0, NCH) as c:
                    n = b * 10 + c
                    pe.wait_ge(pad_l, b * 16 + c + 1)
                    conv(ps[:, 1, :], whi, wlo, W_L + 9 * P, (pad_hi, pad_lo), c=c).then_inc(cv_ps, 1)
                    pe.wait_ge(sq_done, n + 1)
                    conv(ps[:, 0, :], whi, wlo, W_L, (pad_hi, pad_lo), taps=range(3), c=c)
                    pe.wait_ge(cv_out, b * 28 + c * 3 + 1)
                    transposes(ps[:, 4, :], scr[:, CHUNK:2 * CHUNK], QT).then_inc(t_ps, 1)
                    conv(ps[:, 0, :], whi, wlo, W_L, (pad_hi, pad_lo), taps=range(3, 9), c=c).then_inc(cv_ps, 1)
                    conv(ps[:, 2, :], whi, wlo, W_L + 18 * P, (pad_hi, pad_lo), taps=range(6), c=c)
                    pe.wait_ge(cv_out, b * 28 + c * 3 + 2)
                    transposes(ps[:, 3, :], scr[:, 0:CHUNK], QT).then_inc(t_ps, 1)
                    conv(ps[:, 2, :], whi, wlo, W_L + 18 * P, (pad_hi, pad_lo), taps=range(6, 9), c=c).then_inc(cv_ps, 1)
                    pe.wait_ge(t_l, b * 20 + c * 2 + 2)
                    pe.wait_ge(g_sum, b * 8 + c + 1)
                    gram((t_hi[0], t_lo[0]), (t_hi[1], t_lo[1]), True, True).then_inc(g_ps, 1)
                lo0 = b * 7
                nine = lambda k: slice(k, k + P)
                pe.wait_ge(pool_lo, b + 1)
                pe.wait_ge(sq_done, b * 10 + 9)
                for h in range(2):
                    w = nine(W_ST1)
                    last = three(ps[:, h, :], whi[:, w], wlo[:, w], ring[:, h * CHUNK:(h + 1) * CHUNK],
                                 ring[:, 1024 + h * CHUNK:1024 + (h + 1) * CHUNK], True, True)
                last.then_inc(sp_ps, 1)
                pe.wait_ge(d_lo, b * 2 + 2)
                src = (pad_hi, pad_lo)
                v_conv = lambda c, taps: conv(ps[:, 6 + c, :], dhi, dlo, 9 * P, src, taps=taps, half=True, c=c)
                k_conv = lambda c, taps: conv(ps[:, 6 + c, :], dhi, dlo, 0, src, taps=taps, half=True, c=c)
                pe.wait_ge(pad_l, b * 16 + 12)
                v_conv(0, range(0, 5))
                pe.wait_ge(cv_out, b * 28 + 24)
                pe.wait_ge(sp_f, b * 4 + 1)
                transposes(ps[:, 2, :], scr[:, 1024:1536], 4)
                transposes(ps[:, 3, :], scr[:, 1536:2048], 4).then_inc(sp_ps, 1)
                pe.wait_ge(pad_l, b * 16 + 16)
                v_conv(0, range(5, 9)).then_inc(cv_ps, 1)
                pe.wait_ge(sp_lo, lo0 + 1)
                for y in range(8):
                    last = three(ps[:, y // 4, (y % 4) * P:(y % 4 + 1) * P], ring[:, y * P:(y + 1) * P],
                                 ring[:, 1280 + y * P:1280 + (y + 1) * P], dhi[:, nine(D_X)], dlo[:, nine(D_X)], True, True)
                last.then_inc(sp_ps, 1)
                v_conv(1, range(0, 3))
                pe.wait_ge(sp_f, b * 4 + 2)
                transposes(ps[:, 2, :], stage[:, 0:512], 4)
                transposes(ps[:, 3, :], stage[:, 512:1024], 4).then_inc(sp_ps, 1)
                v_conv(1, range(3, 9)).then_inc(cv_ps, 1)
                pe.wait_ge(sp_lo, lo0 + 2)
                for k in range(8):
                    d = nine(D_Y0 if k == 0 else D_Y)
                    three(ps[:, k // 4, (k % 4) * P:(k % 4 + 1) * P], ring[:, k * P:(k + 1) * P],
                          ring[:, 1280 + k * P:1280 + (k + 1) * P], dhi[:, d], dlo[:, d], True, True)
                d = slice(D_Y16, D_Y16 + 64)
                three(ps[:, 2, 0:64], ring[:, 0:P], ring[:, 1280:1280 + P], dhi[:, d], dlo[:, d], True, True).then_inc(sp_ps, 1)
                pe.wait_ge(cv_out, b * 28 + 25)
                k_conv(0, range(0, 4))
                fold_weights(b, 0)
                pe.wait_ge(sp_lo, lo0 + 3)
                for part in range(2):
                    for h in range(2):
                        w, r = nine(W_FU + part * P), slice(h * 272, (h + 1) * 272)
                        last = three(ps[:, 3 * part + h, 0:272], whi[:, w], wlo[:, w], ring[:, 2304:2848][:, r],
                                     ring[:, 2848:3392][:, r], True, True)
                last.then_inc(sp_ps, 1)
                k_conv(0, range(4, 6))
                pe.wait_ge(sp_f, b * 4 + 3)
                for part in range(2):
                    transposes(ps[:, 2 + part, :], stage[:, part * 640:part * 640 + 512], 4)
                for part in range(2):
                    last = pe.transpose(ps[0:32, 4, part * P:(part + 1) * P], stage[:, part * 640 + 512:part * 640 + 544], ident)
                last.then_inc(sp_ps, 1)
                k_conv(0, range(6, 9)).then_inc(cv_ps, 1)
                pe.wait_ge(cv_out, b * 28 + 26)
                k_conv(1, range(0, 2))
                pe.wait_ge(sp_lo, lo0 + 4)
                for q in range(4):
                    o = ps[:, q // 2, (q % 2) * 256:(q % 2 + 1) * 256]
                    re, im = q * P, (4 + q) * P
                    three(o, ring[:, re:re + P], ring[:, 1280 + re:1280 + re + P],
                          dhi[:, D_RE:D_RE + 256], dlo[:, D_RE:D_RE + 256], True, False)
                    three(o, ring[:, im:im + P], ring[:, 1280 + im:1280 + im + P],
                          dhi[:, D_IM:D_IM + 256], dlo[:, D_IM:D_IM + 256], False, True)
                o = ps[:, 3, 0:64]
                three(o, ring[0:32, 1024:1152], ring[0:32, 2304:2432], dhi[0:32, D_RE:D_RE + 64], dlo[0:32, D_RE:D_RE + 64], True, False)
                three(o, ring[0:32, 1152:1280], ring[0:32, 2432:2560], dhi[0:32, D_IM:D_IM + 64], dlo[0:32, D_IM:D_IM + 64],
                      False, True).then_inc(sp_ps, 1)
                pe.wait_ge(cv_out, b * 28 + 27)
                transposes(ps[:, 6, :], scr[:, 0:CHUNK], QT).then_inc(t_ps, 1)
                k_conv(1, range(2, 4))
                pe.wait_ge(sp_f, b * 4 + 4)
                transposes(ps[:, 2, :], stage[:, 0:512], 4)
                transposes(ps[:, 4, :], stage[:, 512:1024], 4).then_inc(sp_ps, 1)
                k_conv(1, range(4, 9)).then_inc(cv_ps, 1)
                pe.wait_ge(sp_lo, lo0 + 5)
                for y in range(8):
                    last = three(ps[:, y // 4, (y % 4) * P:(y % 4 + 1) * P], ring[:, y * P:(y + 1) * P],
                                 ring[:, 1280 + y * P:1280 + (y + 1) * P], dhi[:, nine(D_OUT)], dlo[:, nine(D_OUT)], True, True)
                last.then_inc(sp_ps, 1)
                pe.wait_ge(cv_out, b * 28 + 28)
                transposes(ps[:, 7, :], scr[:, CHUNK:2 * CHUNK], QT).then_inc(t_ps, 1)
                def output(c2, s, low):
                    co = slice((s % 2) * P, (s % 2 + 1) * P)
                    px = bass.ds(c2 * (2 * CHUNK) + (s // 2) * CHUNK, CHUNK)
                    hi, lo = (vl_hi, vl_lo) if low else (up_hi, up_lo)
                    w_h, w_l = fold[0 if low else 1]
                    return three(ps[:, OUT_BANKS[s], :], w_h[:, co], w_l[:, co], hi[:, px], lo[:, px], low, not low)

                pe.wait_ge(f_lo, b * 2 + 2)
                pe.wait_ge(vl_l, b * 8 + 9)
                pe.wait_ge(t_l, b * 20 + 17)
                output(0, 2, True)
                w = nine(W_ST2)
                for h in range(HCH):
                    pe.wait_ge(sp_lo, lo0 + 6 + h)
                    for i in range(QT):
                        z = slice(h * CHUNK + i * P, h * CHUNK + (i + 1) * P)
                        last = three(ps[:, 2 + h, i * P:(i + 1) * P], ring[:, z], ring[:, 1024:2048][:, z], whi[:, w], wlo[:, w],
                                     True, True)
                    last.then_inc(t_ps, 1)
                for h in range(HCH):
                    three(ps[:, h, :], whi[:, w], wlo[:, w], ring[:, h * CHUNK:(h + 1) * CHUNK],
                          ring[:, 1024 + h * CHUNK:1024 + (h + 1) * CHUNK], True, True).then_inc(cv_ps, 1)
                for h in range(HCH):
                    pe.wait_ge(t_l, b * 20 + 19 + h)
                    last = gram(qt_h[h], kt_h[h], h == 0, h == HCH - 1)
                last.then_inc(g_ps, 1)

                pe.wait_ge(sq_done, b * 10 + 11)
                for s in (0, 1, 3):
                    output(0, s, True)
                fold_weights(b, 1)
                pe.wait_ge(f_lo, b * 2 + 3)
                pe.wait_ge(up_l, b * 4 + 1)
                for s in range(4):
                    output(0, s, False).then_inc(r_ps, 1)
                with pe.Fori(1, NCH // 2) as c2:
                    pe.wait_ge(up_l, b * 4 + c2 + 1)
                    for s in range(4):
                        pe.wait_ge(r_out, b * 16 + c2 * 4 + (s + 1))
                        output(c2, s, True)
                        output(c2, s, False).then_inc(r_ps, 1)

        @block.scalar
        def _(act):
            def pad(src, r, n):
                r0 = 0 if r == 0 else 8 * r + 1
                r1 = min(8 * r + 9, H)
                act.activation(pad_hi[:, 1 + r0:1 + r1, 1:1 + W],
                               img[:, src, r0 * W:r1 * W].rearrange("p (h w) -> p h w", w=W), ACT.Copy).then_inc(pad_h, 1)

            def evac(dst, bank, b_ap, ready, norm=None, scale=BNS):
                act.wait_ge(cv_ps, ready)
                act.activation(dst, ps[:, bank, :], ACT.Identity, bias=b_ap, scale=scale).then_inc(cv_out, 1)
                if norm is not None:
                    act.activation(ps[:, bank, :], ps[:, bank, :], ACT.Square, bias=b_ap, scale=scale,
                                   accum_out=norm).then_inc(sq_done, 1)

            def projected(b, c2, s, ahead):
                n = b * NCH + c2 * 2 + s
                px = bass.ds(c2 * (2 * CHUNK) + s * CHUNK, CHUNK)
                if ahead:
                    s1 = (s + 1) % 2
                    act.wait_ge(x_in[s1], b * (16 * NCH // 2) + c2 * 16 + (48 if s else 32))
                    act.wait_ge(v_ps, n * 2 + 4)
                    act.activation(xs[:, s1, 0], img[:, :, bass.ds(c2 * (2 * CHUNK) + (s + 1) * CHUNK, CHUNK)],
                                   ACT.Copy).then_inc(xs_hi, 1)
                act.wait_ge(qk_ps, n + 1)
                for dst, to, fr, rows in ((q_st, 0, 0, 64), (k_st, 64, 64, 32), (k_st, 0, 96, 32)):
                    last = act.activation(dst[to:to + rows, px], ps[fr:fr + rows, 4 * s, :], ACT.Identity,
                                          bias=cst[fr:fr + rows, K_BIAS + BQK:K_BIAS + BQK + 1])
                last.then_inc(qk_hi, 1)
                for v in range(2):
                    act.wait_ge(v_ps, n * 2 + (v + 5))
                    act.activation(vhi_t[:, bass.ds(c2 * 8 + (s * 4 + v * 2), 2), 0:C],
                                   ps[:, 2 + v, :].rearrange("p (t c) -> p t c", c=C), ACT.Copy).then_inc(v_hi, 1)

            def t_split(hi, bank, ready, scale=1.0):
                act.wait_ge(t_ps, ready)
                act.activation(hi, ps[:, bank, :], ACT.Copy, scale=scale).then_inc(t_h, 1)

            def k_square(buf, bank, ready):
                act.wait_ge(t_ps, ready)
                act.activation(buf, ps[:, bank, :], ACT.Square).then_inc(k_sq, 1)

            def k_unit_hi(buf, n, hi):
                act.wait_ge(k_sum, n + 1)
                act.activation(knorm[:, 32:64], knorm[:, 0:32], ACT.Sqrt).then_inc(k_root, 1)
                act.wait_ge(k_unit, n + 1)
                act.activation(hi, buf, ACT.Copy).then_inc(t_h, 1)

            def exps(t, n):
                act.wait_ge(s_ready, n * NT + t + 1)
                if t == 3:
                    act.wait_ge(o_norm, n * 3 + 3)
                act.wait_ge(p_used, n * (NT - 1) + (t + 2 if t < 3 else t + 1))
                act.activation(prob[:, t % 4, 0, :], ps[:, 4 + t % 2, :], ACT.Exp)
                act.activation(ps[:, 4 + t % 2, :], ps[:, 4 + t % 2, :], ACT.Exp).then_inc(p_full, 1)

            def attend(b, g, last_group):
                n = b * NCH + g
                for t in range(3, NT):
                    exps(t, n)
                if not last_group:
                    exps(0, n + 1)
                    exps(1, n + 1)
                act.wait_ge(rden_in, n * QT + 3)
                act.activation(onorm[:, 3, :], ps[:, 3, 0:C], ACT.Copy, scale=rden[:, 3:4]).then_inc(o_norm3, 1)
                if not last_group:
                    exps(2, n + 1)

            def chain(b, s, step):
                d = (2 * b + s) * 8
                if step == 0:
                    act.wait_ge(a_dve, d + 1)
                    act.activation(stat[:, 2:3], stat[:, 0:1], ACT.Sqrt).then_inc(a_act, 1)
                elif step == 1:
                    act.wait_ge(a_dve, d + 6)
                    act.activation(attn[:, :], attn[:, :], ACT.Exp, bias=stat[:, 4:5], accum_out=stat[:, 5:6]).then_inc(a_act, 1)
                else:
                    act.wait_ge(f_ps, 2 * b + s + 1)
                    act.activation(fold[s][0], ps[:, 5, 2 * P:2 * P + C], ACT.Copy).then_inc(f_hi, 1)

            def sp_split(step, dst, src, b):
                act.wait_ge(sp_ps, b * 10 + step)
                last = None
                for d, s_ in zip(dst, src):
                    last = act.activation(d, s_, ACT.Copy)
                last.then_inc(sp_hi, 1)

            for _ in range(4):
                act.sem_inc(r_out, 1)
            act.sem_inc(o_norm3, 1)
            act.sem_inc(sq_done, 1)
            act.wait_ge(w_in, 16)
            act.activation(whi[:, 0:W_L], stage[:, 0:W_L], ACT.Copy).then_inc(w_hi, 1)
            act.wait_ge(c_in, 16)
            act.wait_ge(prep, 2)
            with act.Fori(0, B) as b:
                for s in range(2):
                    projected(b, 0, s, s == 1)
                with act.Fori(1, NCH // 2 - 1) as c2:
                    for s in range(2):
                        projected(b, c2, s, True)
                for s in range(2):
                    projected(b, NCH // 2 - 1, s, s == 0)
                for t in range(3):
                    exps(t, b * NCH)
                with act.Fori(0, NCH - 1) as g:
                    attend(b, g, False)
                attend(b, NCH - 1, True)
                act.wait_ge(o_done, b * (NCH * QT) + NCH * QT)
                for r in range(6):
                    pad(0, r, b)
                act.wait_ge(m_free, b * M_PER_IMAGE + M_PER_IMAGE + 2)
                for r in range(6, 8):
                    pad(0, r, b)

                def low_chunk(c, last):
                    n = b * NCH + c
                    evac(scr[:, CHUNK:2 * CHUNK], 1, bscaled[:, 1:2], b * 30 + c * 3 + 1)
                    k_square(scr[:, CHUNK:2 * CHUNK], 4, b * 20 + c * 2 + 1)
                    k_unit_hi(scr[:, CHUNK:2 * CHUNK], b * 10 + c, t_hi[1])
                    if last:
                        for r in range(6):
                            pad(1, r, b)
                    evac(scr[:, 0:CHUNK], 0, bscaled[:, 0:1], b * 30 + c * 3 + 2, norms[:, bass.ds(c, 1)])
                    t_split(t_hi[0], 3, b * 20 + c * 2 + 2)
                    act.wait_ge(vl_l, b * 8 + c + 1)
                    evac(scr[:, 2 * CHUNK:3 * CHUNK], 2, bscaled[:, 2:3], b * 30 + c * 3 + 3)

                with act.Fori(0, NCH - 1) as c:
                    low_chunk(c, False)
                low_chunk(NCH - 1, True)
                for r in range(6, 8):
                    pad(1, r, b)
                hi8 = ring[:, 0:1024]
                act.wait_ge(vl_l, b * 8 + 9)
                act.wait_ge(sp_ps, b * 10 + 1)
                act.activation(scr[:, 1024:2048], ps[:, 0:2, :].rearrange("p a n -> p (a n)"), ACT.Relu, scale=0.25 * BNS).then_inc(sp_f, 1)
                sp_split(2, [hi8], [ps[:, 2:4, :].rearrange("p a n -> p (a n)")], b)
                chain(b, 0, 0)
                y1 = stage[:, 0:1024].rearrange("p (f y) -> p y f", y=HH)
                act.wait_ge(sp_ps, b * 10 + 3)
                for h in range(2):
                    last = act.activation(y1[:, 16 * h:16 * (h + 1), :], ps[:, h, :].rearrange("p (y f) -> p y f", f=WH), ACT.Copy)
                last.then_inc(sp_f, 1)
                evac(v_h[:, 0:CHUNK], 6, bscaled[:, 4:5], b * 30 + 25)
                chain(b, 0, 1)
                sp_split(4, [hi8], [ps[:, 2:4, :].rearrange("p a n -> p (a n)")], b)
                evac(v_h[:, CHUNK:2 * CHUNK], 7, bscaled[:, 4:5], b * 30 + 26)
                sp_split(5, *freq(ring[:, 2304:2848]), b)
                chain(b, 0, 2)
                act.wait_ge(sp_ps, b * 10 + 6)
                for part in range(2):
                    for h in range(2):
                        last = act.activation(stage[:, part * 640 + h * 272:part * 640 + (h + 1) * 272], ps[:, 3 * part + h, 0:272],
                                              ACT.Relu, scale=BNS)
                last.then_inc(sp_f, 1)
                sp_split(7, *ky_tiles(ring[:, 0:1280]), b)
                evac(scr[:, 0:CHUNK], 6, bscaled[:, 3:4], b * 30 + 27)
                act.wait_ge(sp_ps, b * 10 + 8)
                z1 = stage[:, 0:1024].rearrange("p (y f) -> p f y", f=WH)
                act.activation(z1[:, 0:1, :], ps[:, 0, 0:32].rearrange("p (f y) -> p f y", y=HH), ACT.Copy)
                act.activation(z1[:, 2:16, :], ps[:, 0, 64:512].rearrange("p (f y) -> p f y", y=HH), ACT.Copy)
                act.activation(z1[:, 16:32, :], ps[:, 1, :].rearrange("p (f y) -> p f y", y=HH), ACT.Copy)
                act.activation(z1[:, 1:2, :], ps[:, 3, 0:32].rearrange("p (f y) -> p f y", y=HH), ACT.Copy).then_inc(sp_f, 1)
                k_square(scr[:, 0:CHUNK], 6, b * 20 + 17)
                sp_split(9, [ring[:, 0:512], ring[:, 512:1024]], [ps[:, 2, :], ps[:, 4, :]], b)
                k_unit_hi(scr[:, 0:CHUNK], b * 10 + 8, kt_h[0][0])
                evac(scr[:, CHUNK:2 * CHUNK], 7, bscaled[:, 3:4], b * 30 + 28)
                for h in range(HCH):
                    act.wait_ge(sp_z, b * 2 + h + 1)
                    act.activation(hi8[:, h * CHUNK:(h + 1) * CHUNK], stage[:, (2 + h) * CHUNK:(3 + h) * CHUNK],
                                   ACT.Copy).then_inc(sp_hi, 1)
                k_square(scr[:, CHUNK:2 * CHUNK], 7, b * 20 + 18)
                k_unit_hi(scr[:, CHUNK:2 * CHUNK], b * 10 + 9, kt_h[1][0])
                for h in range(HCH):
                    t_split(qt_h[h][0], 2 + h, b * 20 + 19 + h, BNS)
                for h in range(HCH):
                    act.wait_ge(cv_ps, b * 30 + 29 + h)
                    act.activation(ps[:, h, :], ps[:, h, :], ACT.Square, scale=BNS, accum_out=norms[:, NCH + h:NCH + h + 1]).then_inc(sq_done, 1)
                chain(b, 1, 0)
                act.activation(stat[:, 7:8], ident[:, 0:1], ACT.Exp)
                for i in range(4):
                    act.wait_ge(up_d, b * UP_STEPS + UP_STEPS + 1)
                    act.wait_ge(up_rest, b * 3 + 3)
                    act.activation(up_hi[:, i * 1024:(i + 1) * 1024], image[:, i * 1024:(i + 1) * 1024], ACT.Copy).then_inc(up_h, 1)
                    if i == 0:
                        chain(b, 1, 1)
                    elif i == 1:
                        chain(b, 1, 2)
                with act.Fori(0, NCH // 2) as c2:
                    for s in range(4):
                        act.wait_ge(r_ps, b * 16 + c2 * 4 + (s + 1))
                        act.wait_ge(out_dma[s], b * 64 + c2 * 16 + 16)
                        act.activation(stage[:, s * CHUNK:(s + 1) * CHUNK], ps[:, OUT_BANKS[s], :], ACT.Identity,
                                       bias=bias(BO + s % 2)).then_inc(r_out, 1)

        @block.vector
        def _(dve):
            def sub(o, a, b_):
                return dve.tensor_tensor(o, a, f(b_), ALU.subtract)

            def pad(src, r, b):
                dve.wait_ge(pad_h, b * 16 + src * 8 + r + 1)
                r0 = 0 if r == 0 else 8 * r + 1
                r1 = min(8 * r + 9, H)
                sub(pad_lo[:, 1 + r0:1 + r1, 1:1 + W], img[:, src, r0 * W:r1 * W].rearrange("p (h w) -> p h w", w=W),
                    pad_hi[:, 1 + r0:1 + r1, 1:1 + W]).then_inc(pad_l, 1)

            def low(t, n0):
                dve.wait_ge(p_full, n0 + t + 1)
                sub(prob[:, t % 4, 1, :], ps[:, 4 + t % 2, :], prob[:, t % 4, 0, :]).then_inc(p_lo, 1)

            def maxima(i, m):
                dve.wait_ge(m_ready, m + 1)
                dve.tensor_reduce(mx_t[:, i // NCH, i % NCH:i % NCH + 1], ps[:, 6 + i % 2, :], AX.X, ALU.max).then_inc(m_free, 1)

            def first_maxima(b, c2, s, qt):
                dve.wait_ge(m_ready, b * M_PER_IMAGE + c2 * (2 * QT) + (s * QT - QT + qt + 1))
                apart(dve)
                dve.tensor_reduce(mx_t[:, qt, bass.ds(c2 * 2 + (s - 1), 1)], ps[:, 6 + qt % 2, :], AX.X, ALU.max).then_inc(m_free, 1)

            def x_split(b, s):
                dve.wait_ge(xs_hi_e, b * 2 + s + 1)
                sub(xs[:, s, 1], img[:, :, s * CHUNK:(s + 1) * CHUNK], xs[:, s, 0]).then_inc(xs_lo_e, 1)

            def values_lo(b, c2, s):
                n = b * NCH + c2 * 2 + s
                for v in range(2):
                    dve.wait_ge(v_hi, n * 2 + (v + 1))
                    t_ = bass.ds(c2 * 8 + (s * 4 + v * 2), 2)
                    sub(vlo_t[:, t_, :], ps[:, 2 + v, :].rearrange("p (t c) -> p t c", c=C),
                        vhi_t[:, t_, 0:C]).then_inc(v_lo, 1)

            def projected(b, c2, s, early=False, last=False):
                n = b * NCH + c2 * 2 + s
                px = bass.ds(c2 * (2 * CHUNK) + s * CHUNK, CHUNK)
                first, second = early and s == 0, early and s == 1
                if not early:
                    for qt in range(2):
                        first_maxima(b, c2, s, qt)
                dve.wait_ge(qk_hi, n + 1)
                for dst, to, fr, hi in ((q_st, 64, 0, 0), (k_st, 32, 64, 64)):
                    dve.scalar_tensor_tensor(dst[to:to + 32, px], ps[fr:fr + 32, 4 * s, :],
                                             cst[fr:fr + 32, K_BIAS + BQK:K_BIAS + BQK + 1],
                                             f(dst[hi:hi + 32, px]), ALU.add, ALU.subtract).then_inc(qk_lo, 1)
                if not first:
                    for qt in range(0 if second else 2, QT):
                        first_maxima(b, c2, s, qt)
                if not last:
                    values_lo(b, c2, s)

            def minus_maxima(m):
                dve.wait_ge(m_free, m + 2)
                dve.tensor_reduce(maxcol[:, 96:96 + 32 * (QT - 1) + 1:32], mx_t, AX.X, ALU.max, negate=True).then_inc(negmax, 1)

            def maxima_rows(group, m):
                for h in range(2):
                    dve.wait_ge(m_ready, m + h + 1)
                    dve.tensor_copy(q_st[96:128, bass.ds(group * CHUNK + h * 256, 256)], ps[96:128, 6 + h, 0:256]).then_inc(m_free, 1)

            def attend(b, g, last_group):
                n = b * NCH + g
                m0 = b * M_PER_IMAGE + (NT + 2) + g * M_PER_GROUP
                i = 0
                for t in range(1, NT):
                    if not last_group:
                        for _ in range(MAX_AT[t]):
                            maxima(i, m0 + i)
                            i += 1
                        if t == MAX_TILES + 2:
                            minus_maxima(m0 + NT)
                        if t == MAX_TILES + 4:
                            maxima_rows(g + 1, m0 + NT)
                    if t + 2 < NT:
                        low(t + 2, n * NT)
                    elif t + 2 == NT and not last_group:
                        low(0, (n + 1) * NT)
                for i, qt in enumerate((0, 1, 3, 2)):
                    dve.wait_ge(o_done, n * QT + qt + 1)
                    dve.reciprocal(rden[:, qt:qt + 1], ps[:, qt, C:C + 1]).then_inc(rden_in, 1)
                    if qt != 3:
                        dve.wait_ge(rden_in, n * QT + i + 1)
                        dve.tensor_scalar(onorm[:, qt, :], ps[:, qt, 0:C], rden[:, qt:qt + 1], None, ALU.mult).then_inc(o_norm, 1)
                if last_group:
                    pad(0, 0, b)
                else:
                    low(1, (n + 1) * NT)
                    low(2, (n + 1) * NT)
                m1 = m0 + (0 if last_group else NT + 2)
                px = bass.ds(g * CHUNK, CHUNK)
                for c in range(CT):
                    dve.wait_ge(m_ready, m1 + c + 1)
                    dve.scalar_tensor_tensor(img[:, c, px], ps[:, 6 + c, :], bias(BV + c), img[:, c, px],
                                             ALU.add, ALU.add).then_inc(m_free, 1)

            def t_split(hi, lo, bank, ready):
                dve.wait_ge(t_h, ready)
                sub(lo, ps[:, bank, :], hi).then_inc(t_l, 1)

            heads = lambda z: z.rearrange("p (a c) -> p a c", c=P // 8)

            def k_squares(buf, n):
                dve.wait_ge(k_sq, n + 1)
                dve.tensor_reduce(knorm[:, 0:32], heads(buf), AX.X, ALU.add).then_inc(k_sum, 1)

            def k_unit_split(buf, n, bank, hi, lo, ready):
                dve.wait_ge(k_root, n + 1)
                dve.tensor_scalar(knorm[:, 32:64], knorm[:, 32:64], NORM_FLOOR, None, ALU.max).then_inc(k_inv, 1)
                dve.wait_ge(k_inv, n * 2 + 1)
                dve.reciprocal(knorm[:, 32:64], knorm[:, 32:64]).then_inc(k_inv, 1)
                dve.wait_ge(k_inv, n * 2 + 2)
                dve.tensor_tensor(heads(buf), heads(ps[:, bank, :]),
                                  knorm[:, 32:64].unsqueeze(2).to_broadcast([P, 32, P // 8]), ALU.mult).then_inc(k_unit, 1)
                dve.wait_ge(t_h, ready)
                sub(lo, buf, hi).then_inc(t_l, 1)

            def gram_add(b, c):
                dve.wait_ge(g_ps, b * 9 + c + 1)
                dve.wait_ge(g_sum, b * 8 + c + 1)
                dve.tensor_tensor(gram[:, :], gram[:, :], ps[:, 5, 0:P], ALU.add).then_inc(g_sum, 1)

            def sp_split(step, dst, hi, src, b):
                dve.wait_ge(sp_hi, b * 7 + step)
                last = None
                for d, h_, s_ in zip(dst, hi, src):
                    last = sub(d, s_, h_)
                last.then_inc(sp_lo, 1)

            def chain(b, s, step):
                d = (2 * b + s) * 8
                a = (2 * b + s) * 2
                nch = NCH if s == 0 else HCH
                if step == 0:
                    dve.wait_ge(sq_done, b * 10 + (9 if s == 0 else 11))
                    dve.tensor_reduce(stat[:, 0:1], norms[:, s * NCH:s * NCH + nch], AX.X, ALU.add).then_inc(a_dve, 1)
                elif step == 1:
                    dve.wait_ge(a_act, a + 1)
                    dve.tensor_scalar(stat[:, 2:3], stat[:, 2:3], NORM_FLOOR, None, ALU.max).then_inc(a_dve, 1)
                    dve.wait_ge(a_dve, d + 2)
                    dve.reciprocal(stat[:, 2:3], stat[:, 2:3]).then_inc(a_dve, 1)
                    dve.wait_ge(a_dve, d + 3)
                    dve.tensor_tensor(stat[:, 2:3], stat[:, 2:3], bias(TEMP), ALU.mult).then_inc(a_dve, 1)
                elif step == 2:
                    dve.wait_ge(a_dve, d + 4)
                    if s == 0:
                        dve.wait_ge(g_sum, b * 8 + 9)
                    else:
                        dve.wait_ge(g_ps, b * 9 + 9)
                    dve.scalar_tensor_tensor(attn[:, :], gram[:, :] if s == 0 else ps[:, 5, 0:P], stat[:, 2:3], cst[:, K_NEG:K_NEG + P],
                                             ALU.mult, ALU.add).then_inc(a_dve, 1)
                    dve.wait_ge(a_dve, d + 5)
                    dve.tensor_reduce(stat[:, 4:5], attn[:, :], AX.X, ALU.max, negate=True).then_inc(a_dve, 1)
                elif step == 3:
                    dve.wait_ge(a_act, a + 2)
                    dve.reciprocal(stat[:, 6:7], stat[:, 5:6]).then_inc(a_dve, 1)
                    dve.wait_ge(a_dve, d + 7)
                    dve.tensor_scalar(attn[:, :], attn[:, :], stat[:, 6:7], None, ALU.mult).then_inc(a_dve, 1)
                else:
                    dve.wait_ge(f_hi, 2 * b + s + 1)
                    sub(fold[s][1], ps[:, 5, 2 * P:2 * P + C], fold[s][0]).then_inc(f_lo, 1)

            def up_step(b, i):
                dve.wait_ge(up_d, b * UP_STEPS + i + 1)
                if i == 0:
                    dve.wait_ge(cv_out, b * 28 + 26)
                if i == 0:
                    ins = dve.tensor_tensor(d_x, v_hw[:, :, 0:K], v_hw[:, :, 1:WH], ALU.subtract)
                elif i == 1:
                    ins = dve.tensor_tensor(wide_e[:, :, 1:WH], d_x, row(even), ALU.mult)
                elif i == 2:
                    ins = dve.tensor_tensor(wide_e[:, :, 1:WH], wide_e[:, :, 1:WH], v_hw[:, :, 1:WH], ALU.add)
                elif i == 3:
                    ins = dve.tensor_tensor(wide_o[:, :, 0:K], d_x, row(odd), ALU.mult)
                elif i == 4:
                    ins = dve.tensor_tensor(wide_o[:, :, 0:K], wide_o[:, :, 0:K], v_hw[:, :, 0:K], ALU.add)
                elif i == 5:
                    ins = dve.tensor_copy(wide[:, :, 0:W:W - 1], v_hw[:, :, 0:WH:WH - 1])
                elif i == 6:
                    ins = dve.tensor_tensor(d_y, wide[:, 0:K, :], wide[:, 1:HH, :], ALU.subtract)
                elif i == 7:
                    ins = dve.tensor_tensor(up_e[:, 1:HH, :], d_y, col(even), ALU.mult)
                else:
                    ins = dve.tensor_copy(up[:, 0:H:H - 1, :], wide[:, 0:HH:HH - 1, :])
                ins.then_inc(up_d, 1)

            for _ in range(2):
                dve.sem_inc(p_lo, 1)
                dve.sem_inc(m_free, 1)
                dve.sem_inc(v_lo, 1)
            for _ in range(3):
                dve.sem_inc(o_norm, 1)
            for s_ in (vl_l, g_sum, f_lo, up_d):
                dve.sem_inc(s_, 1)
            dve.memset(maxcol[:, :], 0.0).then_inc(prep, 1)
            dve.wait_ge(w_hi, 1)
            sub(wlo[:, 0:W_L], stage[:, 0:W_L], whi[:, 0:W_L]).then_inc(w_lo, 1)
            dve.wait_ge(c_in, 16)
            dve.tensor_scalar(bscaled[:, :], cst[:, K_BIAS + BL:K_BIAS + BL + 5], BNS, None, ALU.mult).then_inc(prep, 1)
            with dve.Fori(0, B) as b:
                for s in range(2):
                    x_split(b, s)
                for s in range(2):
                    projected(b, 0, s, early=True)
                with dve.Fori(1, NCH // 2 - 1) as c2:
                    for s in range(2):
                        projected(b, c2, s)
                for s in range(2):
                    projected(b, NCH // 2 - 1, s, last=s == 1)
                m = b * M_PER_IMAGE
                for qt in range(QT):
                    first_maxima(b, NCH // 2, 0, qt)
                minus_maxima(m + NT)
                maxima_rows(0, m + NT)
                values_lo(b, NCH // 2 - 1, 1)
                for t in range(3):
                    low(t, b * (NCH * NT))
                with dve.Fori(0, NCH - 1) as g:
                    attend(b, g, False)
                attend(b, NCH - 1, True)
                for r in range(1, 8):
                    pad(0, r, b)
                dve.wait_ge(g_sum, b * 8 + 1)
                dve.memset(gram[:, :], 0.0)
                for s in range(4):
                    dve.wait_ge(out_dma[s], b * 64 + 16)
                dve.wait_ge(m_free, b * M_PER_IMAGE + M_PER_IMAGE + 2)
                dve.tensor_reduce(stage[:, 1024:2048].rearrange("p (y x) -> p y x", x=WH),
                                  img[:, 1, :].rearrange("p (y a x b) -> p y x a b", y=HH, a=2, b=2), AX.XY, ALU.add).then_inc(pool_f, 1)

                def low_chunk(c, last):
                    k_squares(scr[:, CHUNK:2 * CHUNK], b * 10 + c)
                    k_unit_split(scr[:, CHUNK:2 * CHUNK], b * 10 + c, 4, t_hi[1], t_lo[1], b * 20 + c * 2 + 1)
                    if last:
                        for r in range(6):
                            pad(1, r, b)
                    t_split(t_hi[0], t_lo[0], 3, b * 20 + c * 2 + 2)
                    px = bass.ds(c * CHUNK, CHUNK)
                    dve.wait_ge(vl_h, b * 8 + c + 1)
                    sub(vl_lo[:, px], scr[:, 2 * CHUNK:3 * CHUNK], vl_hi[:, px]).then_inc(vl_l, 1)
                    gram_add(b, c)

                low_chunk(0, False)
                dve.wait_ge(pool_hi, b + 1)
                sub(ring[:, 1024:2048], stage[:, 1024:2048], ring[:, 0:1024]).then_inc(pool_lo, 1)
                dve.wait_ge(d_hi, b + 1)
                sub(dlo[:, 0:ND // 2], image[:, 0:ND // 2], dhi[:, 0:ND // 2]).then_inc(d_lo, 1)
                with dve.Fori(1, NCH - 1) as c:
                    low_chunk(c, False)
                sub(dlo[:, ND // 2:ND], image[:, ND // 2:ND], dhi[:, ND // 2:ND]).then_inc(d_lo, 1)
                low_chunk(NCH - 1, True)
                for r in range(6, 8):
                    pad(1, r, b)
                lo8, hi8 = ring[:, 1280:2304], ring[:, 0:1024]
                chain(b, 0, 0)
                sp_split(1, [lo8], [hi8], [ps[:, 2:4, :].rearrange("p a n -> p (a n)")], b)
                chain(b, 0, 1)
                chain(b, 0, 2)
                sp_split(2, [lo8], [hi8], [ps[:, 2:4, :].rearrange("p a n -> p (a n)")], b)
                chain(b, 0, 3)
                d_, s_ = freq(ring[:, 2848:3392])
                h_, _ = freq(ring[:, 2304:2848])
                sp_split(3, d_, h_, s_, b)
                chain(b, 0, 4)
                for i in range(0, 4):
                    up_step(b, i)
                d_, s_ = ky_tiles(ring[:, 1280:2560])
                h_, _ = ky_tiles(ring[:, 0:1280])
                sp_split(4, d_, h_, s_, b)
                for i in range(4, 8):
                    up_step(b, i)
                k_squares(scr[:, 0:CHUNK], b * 10 + 8)
                sp_split(5, [lo8[:, 0:512], lo8[:, 512:1024]], [hi8[:, 0:512], hi8[:, 512:1024]], [ps[:, 2, :], ps[:, 4, :]], b)
                k_unit_split(scr[:, 0:CHUNK], b * 10 + 8, 6, *kt_h[0], b * 20 + 17)
                dve.wait_ge(sp_ps, b * 10 + 10)
                half = lambda z, h: z[:, h * CHUNK:(h + 1) * CHUNK]
                for h in range(HCH):
                    dve.tensor_tensor(half(stage, 2 + h), ps[:, h, :], half(scr, 2 + h), ALU.add).then_inc(sp_z, 1)
                for h in range(HCH):
                    dve.wait_ge(sp_hi, b * 7 + 6 + h)
                    sub(half(ring, 2 + h), half(stage, 2 + h), half(hi8, h)).then_inc(sp_lo, 1)
                k_squares(scr[:, CHUNK:2 * CHUNK], b * 10 + 9)
                k_unit_split(scr[:, CHUNK:2 * CHUNK], b * 10 + 9, 7, *kt_h[1], b * 20 + 18)
                for h in range(HCH):
                    dve.wait_ge(t_h, b * 20 + 19 + h)
                    dve.scalar_tensor_tensor(qt_h[h][1], ps[:, 2 + h, :], BNS, f(qt_h[h][0]),
                                             ALU.mult, ALU.subtract).then_inc(t_l, 1)
                for i in range(8, UP_STEPS):
                    up_step(b, i)
                for step in range(4):
                    chain(b, 1, step)
                for i in range(4):
                    if i == 1:
                        chain(b, 1, 4)
                    dve.wait_ge(up_h, b * 4 + i + 1)
                    sub(up_lo[:, i * 1024:(i + 1) * 1024], image[:, i * 1024:(i + 1) * 1024],
                        up_hi[:, i * 1024:(i + 1) * 1024]).then_inc(up_l, 1)

        @block.gpsimd
        def _(pool):
            def x_hi(b, s):
                pool.wait_ge(x_in[s], b * (16 * NCH // 2) + 32)
                pool.wait_ge(v_ps, (b * NCH + s) * 2 + 2)
                apart(pool)
                pool.tensor_copy(xs[:, s, 0], img[:, :, s * CHUNK:(s + 1) * CHUNK]).then_inc(xs_hi_e, 1)

            def next_queries(b, g):
                pool.wait_ge(m_ready, b * M_PER_IMAGE + g * M_PER_GROUP + (NT - M_PER_GROUP))
                apart(pool)
                pool.tensor_copy(qmax[0:96, :], f(q_st)[0:96, bass.ds(g * CHUNK, CHUNK)]).then_inc(qmax_in, 1)

            def other_weights():
                for i in range(2):
                    w = slice(W_L + i * NREST, W_L + (i + 1) * NREST)
                    pool.wait_ge(w_rest_in, 16 * (i + 1))
                    pool.tensor_copy(whi[:, w], stage[:, 0:NREST]).then_inc(w_rest, 1)
                    pool.wait_ge(w_rest, 2 * i + 1)
                    pool.tensor_tensor(wlo[:, w], stage[:, 0:NREST], f(whi[:, w]), ALU.subtract).then_inc(w_rest, 1)

            def work(b, first):
                pool.wait_ge(f_lo, b * 2 + 1)
                apart(pool)
                for s in range(2):
                    x_hi(b, s)
                pool.wait_ge(qk_lo, b * (2 * NCH) + 2)
                apart(pool)
                pool.tensor_copy(qmax[0:96, :], f(q_st)[0:96, 0:CHUNK]).then_inc(qmax_in, 1)
                with pool.Fori(1, NCH // 2) as c2:
                    for s in range(2):
                        pool.wait_ge(xs_hi, b * (NCH - 2) + c2 * 2 + (s - 1))
                        apart(pool)
                        pool.tensor_tensor(xs[:, s, 1], img[:, :, bass.ds(c2 * (2 * CHUNK) + s * CHUNK, CHUNK)],
                                           f(xs[:, s, 0]), ALU.subtract).then_inc(xs_lo, 1)
                pool.wait_ge(xs_lo, b * (NCH - 2) + (NCH - 2))
                apart(pool)
                pool.memset(f(k_st[96:128, :]), 1.0).then_inc(ones_set, 1)
                pool.wait_ge(ones_set, b * 2 + 1)
                apart(pool)
                pool.memset(f(vhi_t[:, :, C:VC]), 1.0).then_inc(ones_set, 1)
                if first:
                    next_queries(b, 1)
                    other_weights()
                with pool.Fori(2 if first else 1, NCH) as g:
                    next_queries(b, g)
                pool.wait_ge(o_done, b * (NCH * QT) + NCH * QT)
                apart(pool)
                for z in (vhi, vlo):
                    pool.memset(f(z[:, 0:WP - 1]), 0.0).then_inc(border, 1)
                    pool.memset(f(z[:, WP - 1:WP - 1 + (HP - 1) * WP].rearrange("p (h w) -> p h w", w=WP)[:, :, 0:2]), 0.0).then_inc(border, 1)
                    pool.memset(f(z[:, (HP - 1) * WP + 1:HP * WP]), 0.0).then_inc(border, 1)
                pool.wait_ge(pool_f, b + 1)
                apart(pool)
                pool.tensor_copy(ring[:, 0:1024], stage[:, 1024:2048]).then_inc(pool_hi, 1)
                pool.wait_ge(d_in, b * 16 + 16)
                apart(pool)
                pool.tensor_copy(dhi, image[:, 0:ND]).then_inc(d_hi, 1)
                with pool.Fori(0, NCH) as c:
                    pool.wait_ge(cv_out, b * 28 + c * 3 + 3)
                    apart(pool)
                    pool.tensor_copy(vl_hi[:, bass.ds(c * CHUNK, CHUNK)], scr[:, 2 * CHUNK:3 * CHUNK]).then_inc(vl_h, 1)
                pool.wait_ge(up_d, b * UP_STEPS + 8)
                apart(pool)
                pool.tensor_tensor(up_o[:, 0:K, :], d_y, col(odd), ALU.mult).then_inc(up_rest, 1)
                pool.wait_ge(up_rest, b * 3 + 1)
                apart(pool)
                pool.tensor_tensor(up_o[:, 0:K, :], up_o[:, 0:K, :], wide[:, 0:K, :], ALU.add).then_inc(up_rest, 1)
                pool.wait_ge(up_d, b * UP_STEPS + 9)
                apart(pool)
                pool.tensor_tensor(up_e[:, 1:HH, :], up_e[:, 1:HH, :], wide[:, 1:HH, :], ALU.add).then_inc(up_rest, 1)

            work(0, True)
            with pool.Fori(1, B) as b:
                work(b, False)


def transforms():
    n = WH
    i = np.arange(n)
    s = 1 / np.sqrt(n)
    th = 2 * np.pi * np.outer(i, i) / n
    fx, ox = np.zeros((n, n)), np.zeros((n, n))
    fx[:, 0], fx[:, 1] = s, s * np.cos(np.pi * i)
    ox[0], ox[1] = s, s * np.cos(np.pi * i)
    for k in range(1, n // 2):
        fx[:, 2 * k], fx[:, 2 * k + 1] = s * np.cos(th[:, k]), -s * np.sin(th[:, k])
        ox[2 * k], ox[2 * k + 1] = 2 * s * np.cos(th[k]), -2 * s * np.sin(th[k])
    d_x, d_out = np.kron(np.eye(4), fx), np.kron(np.eye(4), ox)
    co, si = s * np.cos(th), s * np.sin(th)
    d_y = np.kron(np.eye(2), np.block([[co, -si], [si, co]]))
    real = np.concatenate([co, -si], 1)
    d_y0 = np.zeros((P, P))
    d_y0[0:32, 0:64] = real
    d_y0[64:128, 64:128] = d_y[0:64, 0:64]
    d_y16 = np.zeros((P, 64))
    d_y16[32:64] = real
    d_re = np.kron(np.eye(4), np.concatenate([co, si], 1))
    d_im = np.kron(np.eye(4), np.concatenate([-si, co], 1))
    return np.concatenate([d_x, d_y0, d_y, d_y16, d_re, d_im, d_out], 1).astype(np.float32)


def upsample_tables():
    k = np.arange(1, WH)
    e = 1 - (2 * k * (WH - 1) / (W - 1) - (k - 1))
    k = np.arange(WH - 1)
    o = (2 * k + 1) * (WH - 1) / (W - 1) - k
    return np.concatenate([e, -o]).astype(np.float32)


def kernel(**inputs):
    import concourse.bacc as bacc
    from concourse.bass_utils import run_bass_kernel_spmd

    a = {k: np.asarray(v) for k, v in inputs.items()}
    l1 = lambda n: a["L1_conv_" + n]

    def tiles(w):
        return w.reshape(-1, P, w.shape[1]).transpose(1, 0, 2).reshape(P, -1)

    def taps(w):
        return w.transpose(1, 2, 3, 0).reshape(P, -1)

    fu = l1("w_stfu")[:, :, 0, 0].reshape(64, 2, 64, 2).transpose(1, 0, 3, 2)
    fu = [fu[r].reshape(64, P).T for r in range(2)]
    st2 = np.zeros((P, P), np.float32)
    st2[0:64] = l1("w_st2")[:, :, 0, 0].T
    weights = np.concatenate(
        [tiles(np.repeat(np.stack([a["L0_conv_wq"].T, a["L0_conv_wk"].T], 1), 2, 1).reshape(C, P)), tiles(a["L0_conv_wv"].T)]
        + [taps(l1(n)) for n in ("wq", "wk", "wv")]
        + [np.tile(l1("w_st1")[:, :, 0, 0].T, (1, 2))] + [np.tile(z, (1, 2)) for z in fu] + [st2], 1)
    weights2 = np.concatenate([taps(l1("wk2")), taps(l1("wv2")), transforms()], 1)
    head = np.arange(P) // (P // 8)
    other = np.where(head[:, None] == head[None, :], 0, -1e30).astype(np.float32)
    wo = l1("w_out")[:, :, 0, 0].T
    cols = [np.concatenate([np.tile(a["L0_conv_b" + z], 2) for z in "qk"]), a["L0_conv_bv"][0:P], a["L0_conv_bv"][P:],
            l1("bq"), l1("bk"), l1("bv"), l1("bk2"), l1("bv2"), l1("b_out")[0:P], l1("b_out")[P:],
            np.repeat(l1("temperature").reshape(-1), P // 8)]
    consts = np.concatenate([tiles(wo), np.eye(P, dtype=np.float32), other,
                             np.tile(upsample_tables()[None], (P, 1)), np.stack(cols, 1)], 1)
    arrays = {"x": a["x"].reshape(B * CT, P, N), "weights": weights, "weights2": weights2, "consts": consts}
    arrays = {k: np.ascontiguousarray(v) for k, v in arrays.items()}
    assert weights.shape == (P, NW) and weights2.shape == (P, ND) and consts.shape == (P, NK)
    nc = bacc.Bacc("TRN2", target_bir_lowering=False, num_devices=1)
    args = [nc.dram_tensor(k, v.shape, mybir.dt.from_np(v.dtype), kind="ExternalInput").ap() for k, v in arrays.items()]
    args.append(nc.dram_tensor("out", (B * CT, P, N), F32, kind="ExternalOutput").ap())
    build(nc, *args)
    r = run_bass_kernel_spmd(nc, [arrays], core_ids=[0])
    return r.results[0]["out"].reshape(B, C, H, W)
```
